# Optimizing a Trainium2 kernel written in Bass

```python
import numpy as np
import jax
import jax.numpy as jnp

def _softmax(x, axis=-1):
    return jax.nn.softmax(x, axis=axis)

def _gelu(x):
    return jax.nn.gelu(x, approximate=True)

def _silu(x):
    return jax.nn.silu(x)

def _sigmoid(x):
    return jax.nn.sigmoid(x)

def _layernorm(x, axis=-1, eps=1e-05):
    m = jnp.mean(x, axis=axis, keepdims=True)
    v = jnp.var(x, axis=axis, keepdims=True)
    return (x - m) / jnp.sqrt(v + eps)

def _scatter_add(tgt, idx, src, axis=0):
    return tgt.at[idx].add(src)

def _segment_sum(src, seg, n):
    return jax.ops.segment_sum(src, seg, n)
kernel_name = 'mk_xattn_ffn_d2_seqx_r8_6d4b62'

def setup_inputs(seed: int=0):
    np.random.seed(seed)
    _w = jnp.asarray

    def _rec_inputs():
        import jax
        import jax.numpy as jnp
        _rk = jax.random.key(seed)
        x = -0.0002928 + 1 * jax.random.normal(jax.random.fold_in(_rk, 1), (16, 128, 128), jnp.float32)
        _lenS = 128 - jax.random.randint(jax.random.fold_in(_rk, 7), (16,), 0, max(1, 128 // 4) + 1, jnp.int32)
        _lenS2 = 128 - jax.random.randint(jax.random.fold_in(_rk, 8), (16,), 0, max(1, 128 // 4) + 1, jnp.int32)
        _ctx_1024P = jax.random.normal(jax.random.fold_in(_rk, 11), (16, 16, 128), jnp.float32)
        _ctx_1024c = jax.random.dirichlet(jax.random.fold_in(_rk, 511), 0.3 * jnp.ones((16,), jnp.float32), (16, 128))
        _ctx_1024t = jnp.einsum('bsk,bkd->bsd', _ctx_1024c, _ctx_1024P)
        _ctx_1024t = _ctx_1024t * jax.lax.rsqrt(jnp.mean(jnp.square(_ctx_1024t)) + 1e-12) * 0.953939
        ctx_1024 = -1.39393e-06 + 0.999914 * (_ctx_1024t + 0.3 * jax.random.normal(jax.random.fold_in(_rk, 611), (16, 128, 128), jnp.float32))
        _validS = jnp.arange(128)[None, :] < _lenS[:, None]
        _validS2 = jnp.arange(128)[None, :] < _lenS2[:, None]
        _causal = jnp.tril(jnp.ones((128, 128), dtype=bool))
        mask_BxSxS2_bf0 = jnp.logical_not(jnp.ones((16, 128, 128), dtype=bool))
        return (x, ctx_1024, mask_BxSxS2_bf0)
    x, ctx_1024, mask_BxSxS2_bf0 = _rec_inputs()

    def _L0_xattn_setup():
        import jax, jax.numpy as jnp
        import numpy as np
        N, T, HID, H = (2, 256, 128, 16)
        D = HID // H
        key = jax.random.key(seed)
        ks = jax.random.split(key, 11)
        s = 1.0 / np.sqrt(HID)
        return {'q': jax.random.normal(ks[0], (N, T, HID), jnp.float32), 'k': jax.random.normal(ks[1], (N, T, HID), jnp.float32), 'v': jax.random.normal(ks[2], (N, T, HID), jnp.float32), 'Wq': jax.random.normal(ks[3], (HID, HID), jnp.float32) * s, 'bq': jnp.zeros((HID,), jnp.float32), 'Wk': jax.random.normal(ks[4], (HID, HID), jnp.float32) * s, 'bk': jnp.zeros((HID,), jnp.float32), 'Wv': jax.random.normal(ks[5], (HID, HID), jnp.float32) * s, 'bv': jnp.zeros((HID,), jnp.float32), 'Wo': jax.random.normal(ks[6], (HID, HID), jnp.float32) * s, 'bo': jnp.zeros((HID,), jnp.float32)}
    _L0_xattn_all = _L0_xattn_setup()
    _L0_xattn_in = {k: v for k, v in _L0_xattn_all.items() if k in ('Wq', 'bq', 'Wk', 'bk', 'Wv', 'bv', 'Wo', 'bo')}
    del _L0_xattn_all

    def _L0_ffn_setup():
        import jax, jax.numpy as jnp
        import numpy as np
        from jax import lax
        D = 128
        H = 512
        E = 8
        TOPK = 2
        key = jax.random.key(seed)
        ks = jax.random.split(key, 7)
        s = 0.02
        return {'x': jax.random.normal(ks[0], (2, 256, D), dtype=jnp.float32), 'W1': jax.random.normal(ks[1], (E, D, H), dtype=jnp.float32) * s, 'b1': jnp.zeros((E, H), dtype=jnp.float32), 'W2': jax.random.normal(ks[2], (E, H, D), dtype=jnp.float32) * s, 'b2': jnp.zeros((E, D), dtype=jnp.float32), 'Wr': jax.random.normal(ks[3], (D, E), dtype=jnp.float32) * s, 'br': jnp.zeros((E,), dtype=jnp.float32)}
    _L0_ffn_all = _L0_ffn_setup()
    _L0_ffn_in = {k: v for k, v in _L0_ffn_all.items() if k in ('W1', 'b1', 'W2', 'b2', 'Wr', 'br')}
    del _L0_ffn_all

    def _L1_xattn_setup():
        import jax, jax.numpy as jnp
        import numpy as np
        B, S, D = (4, 256, 128)
        H, DK, DV = (16, 64, 64)
        key = jax.random.key(seed)
        ks = jax.random.split(key, 12)

        def lin(k, out_d, in_d, std):
            kw, kb = jax.random.split(k)
            w = jax.random.normal(kw, (out_d, in_d), dtype=jnp.float32) * std
            b = jax.random.uniform(kb, (out_d,), dtype=jnp.float32, minval=-1, maxval=1) / np.sqrt(in_d)
            return (w, b)
        std_k = np.sqrt(2.0 / (D + DK)).astype(np.float32)
        std_v = np.sqrt(2.0 / (D + DV)).astype(np.float32)
        wQ_w, wQ_b = lin(ks[0], DK * H, D, std_k)
        wK_w, wK_b = lin(ks[1], DK * H, D, std_k)
        wV_w, wV_b = lin(ks[2], DV * H, D, std_v)
        wOut_w, wOut_b = lin(ks[3], D, DV * H, std_v)
        Q = jax.random.normal(ks[4], (B, S, D), dtype=jnp.float32)
        K = jax.random.normal(ks[5], (B, S, D), dtype=jnp.float32)
        V = jax.random.normal(ks[6], (B, S, D), dtype=jnp.float32)
        attnMask = jnp.zeros((B, S, S), dtype=bool)
        return {'Q': Q, 'K': K, 'V': V, 'attnMask': attnMask, 'wQ_w': wQ_w, 'wQ_b': wQ_b, 'wK_w': wK_w, 'wK_b': wK_b, 'wV_w': wV_w, 'wV_b': wV_b, 'wOut_w': wOut_w, 'wOut_b': wOut_b}
    _L1_xattn_all = _L1_xattn_setup()
    _L1_xattn_in = {k: v for k, v in _L1_xattn_all.items() if k in ('wQ_w', 'wQ_b', 'wK_w', 'wK_b', 'wV_w', 'wV_b', 'wOut_w', 'wOut_b')}
    del _L1_xattn_all

    def _L1_ffn_setup():
        import jax, jax.numpy as jnp
        import numpy as np
        B, L, D, E, K, DFF = (2, 256, 128, 8, 2, 512)
        key = jax.random.key(seed)
        kx, kr, kg, ku, kd = jax.random.split(key, 5)
        scale = 0.02
        return {'x': jax.random.normal(kx, (B, L, D), dtype=jnp.float32), 'Wr': jax.random.normal(kr, (E, D), dtype=jnp.float32) * scale, 'Wg': jax.random.normal(kg, (E, DFF, D), dtype=jnp.float32) * scale, 'Wu': jax.random.normal(ku, (E, DFF, D), dtype=jnp.float32) * scale, 'Wd': jax.random.normal(kd, (E, D, DFF), dtype=jnp.float32) * scale}
    _L1_ffn_all = _L1_ffn_setup()
    _L1_ffn_in = {k: v for k, v in _L1_ffn_all.items() if k in ('Wr', 'Wg', 'Wu', 'Wd')}
    del _L1_ffn_all
    return {'x': x, 'ctx_1024': ctx_1024, 'mask_BxSxS2_bf0': mask_BxSxS2_bf0, 'L0_xattn_Wq': _L0_xattn_in['Wq'], 'L0_xattn_bq': _L0_xattn_in['bq'], 'L0_xattn_Wk': _L0_xattn_in['Wk'], 'L0_xattn_bk': _L0_xattn_in['bk'], 'L0_xattn_Wv': _L0_xattn_in['Wv'], 'L0_xattn_bv': _L0_xattn_in['bv'], 'L0_xattn_Wo': _L0_xattn_in['Wo'], 'L0_xattn_bo': _L0_xattn_in['bo'], 'L0_ffn_W1': _L0_ffn_in['W1'], 'L0_ffn_b1': _L0_ffn_in['b1'], 'L0_ffn_W2': _L0_ffn_in['W2'], 'L0_ffn_b2': _L0_ffn_in['b2'], 'L0_ffn_Wr': _L0_ffn_in['Wr'], 'L0_ffn_br': _L0_ffn_in['br'], 'L1_xattn_wQ_w': _L1_xattn_in['wQ_w'], 'L1_xattn_wQ_b': _L1_xattn_in['wQ_b'], 'L1_xattn_wK_w': _L1_xattn_in['wK_w'], 'L1_xattn_wK_b': _L1_xattn_in['wK_b'], 'L1_xattn_wV_w': _L1_xattn_in['wV_w'], 'L1_xattn_wV_b': _L1_xattn_in['wV_b'], 'L1_xattn_wOut_w': _L1_xattn_in['wOut_w'], 'L1_xattn_wOut_b': _L1_xattn_in['wOut_b'], 'L1_ffn_Wr': _L1_ffn_in['Wr'], 'L1_ffn_Wg': _L1_ffn_in['Wg'], 'L1_ffn_Wu': _L1_ffn_in['Wu'], 'L1_ffn_Wd': _L1_ffn_in['Wd']}

def reference(x, ctx_1024, mask_BxSxS2_bf0, L0_xattn_Wq, L0_xattn_bq, L0_xattn_Wk, L0_xattn_bk, L0_xattn_Wv, L0_xattn_bv, L0_xattn_Wo, L0_xattn_bo, L0_ffn_W1, L0_ffn_b1, L0_ffn_W2, L0_ffn_b2, L0_ffn_Wr, L0_ffn_br, L1_xattn_wQ_w, L1_xattn_wQ_b, L1_xattn_wK_w, L1_xattn_wK_b, L1_xattn_wV_w, L1_xattn_wV_b, L1_xattn_wOut_w, L1_xattn_wOut_b, L1_ffn_Wr, L1_ffn_Wg, L1_ffn_Wu, L1_ffn_Wd):
    import jax
    import jax.numpy as jnp

    def _L0_xattn_ref(q, k, v, Wq, bq, Wk, bk, Wv, bv, Wo, bo):
        import jax, jax.numpy as jnp
        import numpy as np
        N, T, HID, H = (2, 256, 128, 16)
        D = HID // H
        n, t, _ = q.shape
        qh = (q @ Wq + bq).reshape(n, H, t, D)
        kh = (k @ Wk + bk).reshape(n, H, t, D)
        vh = (v @ Wv + bv).reshape(n, H, t, D)
        scores = jnp.einsum('nhtd,nhsd->nhts', qh, kh) / jnp.sqrt(jnp.float32(HID))
        attn = jax.nn.softmax(scores, axis=1)
        out = jnp.einsum('nhts,nhsd->nhtd', attn, vh).reshape(n, t, H * D)
        return out @ Wo + bo

    def _L0_ffn_ref(x, W1, b1, W2, b2, Wr, br):
        import jax, jax.numpy as jnp
        import numpy as np
        from jax import lax
        D = 128
        H = 512
        E = 8
        TOPK = 2
        B, S, _ = x.shape
        xf = x.reshape(-1, D)
        logits = xf @ Wr + br
        topv, _ = lax.top_k(logits, TOPK)
        thresh = topv[:, TOPK - 1:TOPK]
        masked = jnp.where(logits >= thresh, logits, -jnp.inf)
        weights = jax.nn.softmax(masked, axis=-1)
        h = jax.nn.gelu(jnp.einsum('td,edh->eth', xf, W1) + b1[:, None, :], approximate=False)
        expert_out = jnp.einsum('eth,ehd->etd', h, W2) + b2[:, None, :]
        out = jnp.einsum('etd,te->td', expert_out, weights)
        return out.reshape(B, S, D)

    def _L1_xattn_ref(Q, K, V, attnMask, wQ_w, wQ_b, wK_w, wK_b, wV_w, wV_b, wOut_w, wOut_b):
        import jax, jax.numpy as jnp
        import numpy as np
        B, S, D = (4, 256, 128)
        H, DK, DV = (16, 64, 64)
        N = Q.shape[0]
        q = (Q @ wQ_w.T + wQ_b).reshape(N, -1, H, DK).transpose(0, 2, 1, 3)
        k = (K @ wK_w.T + wK_b).reshape(N, -1, H, DK).transpose(0, 2, 1, 3)
        v = (V @ wV_w.T + wV_b).reshape(N, -1, H, DV).transpose(0, 2, 1, 3)
        scale = 1.0 / np.sqrt(DK).astype(np.float32)
        scores = jnp.einsum('bhqd,bhkd->bhqk', q, k) * scale
        scores = jnp.where(attnMask[:, None, :, :], jnp.float32(-10000.0), scores)
        attns = jax.nn.softmax(scores, axis=-1)
        out = jnp.einsum('bhqk,bhkd->bhqd', attns, v)
        out = out.transpose(0, 2, 1, 3).reshape(N, -1, DV * H)
        return out @ wOut_w.T + wOut_b

    def _L1_ffn_ref(x, Wr, Wg, Wu, Wd):
        import jax, jax.numpy as jnp
        import numpy as np
        B, L, D, E, K, DFF = (2, 256, 128, 8, 2, 512)
        Bb, Ll, Dd = x.shape
        T = Bb * Ll
        xt = x.reshape(T, Dd)
        logits = jnp.einsum('td,ed->te', xt, Wr)
        scores = jax.nn.softmax(logits, axis=-1)
        k_scores, k_ids = jax.lax.top_k(scores, K)
        eps = jnp.finfo(x.dtype).eps
        k_w = k_scores / (k_scores.sum(axis=-1, keepdims=True) + eps)
        combine = jnp.sum(jax.nn.one_hot(k_ids, E, dtype=x.dtype) * k_w[..., None], axis=1)
        g = jnp.einsum('td,efd->etf', xt, Wg)
        u = jnp.einsum('td,efd->etf', xt, Wu)
        h = jax.nn.relu(g) * u
        out_e = jnp.einsum('etf,edf->etd', h, Wd)
        out = jnp.einsum('te,etd->td', combine, out_e)
        return out.reshape(Bb, Ll, Dd)
    x = x + _L0_xattn_ref(_layernorm(x, axis=-1), ctx_1024, ctx_1024, L0_xattn_Wq, L0_xattn_bq, L0_xattn_Wk, L0_xattn_bk, L0_xattn_Wv, L0_xattn_bv, L0_xattn_Wo, L0_xattn_bo)
    x = x + _L0_ffn_ref(_layernorm(x, axis=-1), L0_ffn_W1, L0_ffn_b1, L0_ffn_W2, L0_ffn_b2, L0_ffn_Wr, L0_ffn_br)
    x = x + _L1_xattn_ref(_layernorm(x, axis=-1), ctx_1024, ctx_1024, mask_BxSxS2_bf0, L1_xattn_wQ_w, L1_xattn_wQ_b, L1_xattn_wK_w, L1_xattn_wK_b, L1_xattn_wV_w, L1_xattn_wV_b, L1_xattn_wOut_w, L1_xattn_wOut_b)
    x = x + _L1_ffn_ref(_layernorm(x, axis=-1), L1_ffn_Wr, L1_ffn_Wg, L1_ffn_Wu, L1_ffn_Wd)
    return x

_drawn_inputs = setup_inputs


def setup_inputs(seed=0):
    import zlib

    import numpy as np

    out = dict(_drawn_inputs(seed))
    spreads = {'L0_xattn_bq': (0.0, 0.751),
     'L0_xattn_bk': (0.0, 0.56),
     'L0_xattn_bv': (0.0, 0.1),
     'L0_xattn_bo': (0.0, 0.1),
     'L0_ffn_b1': (0.0, 0.8),
     'L0_ffn_b2': (0.0, 0.1),
     'L0_ffn_br': (0.0, 0.1)}
    factors = {'L0_ffn_W1': 3.142,
     'L0_ffn_W2': 2.782,
     'L1_xattn_wK_b': 8.0,
     'L1_xattn_wOut_b': 8.0,
     'L1_ffn_Wr': 8.0,
     'L1_ffn_Wg': 8.0,
     'L1_ffn_Wu': 8.0,
     'L1_ffn_Wd': 8.0}
    for name, (base, spread) in spreads.items():
        noise = np.random.default_rng([zlib.crc32(name.encode()), seed]).standard_normal(out[name].shape)
        drawn = base * np.exp(spread * noise) if base else spread * noise
        out[name] = jnp.asarray(drawn.astype(out[name].dtype))
    for name, factor in factors.items():
        out[name] = (out[name] * factor).astype(out[name].dtype)
    return out
```

```python
from contextlib import ExitStack

import concourse.bass as bass
import numpy as np
from concourse import mybir

F32 = mybir.dt.float32
F32R = mybir.dt.float32r
BF16 = mybir.dt.bfloat16
U8 = mybir.dt.uint8
U32 = mybir.dt.uint32
ALU = mybir.AluOpType
ACT = mybir.ActivationFunctionType
AX = mybir.AxisListType

P = 128
NB = 16
T = 128
D = 128
TOK = NB * T
GB = 4
NG = NB // GB
GT = GB * T
H = 16
DH = D // H
PIECES = D // DH
RT = T // H
E = 8
EPS = 1e-5


class LayerNorm:

    def __init__(self, nc, ctx, name):
        def sb(n, shape, dt=F32):
            return ctx.enter_context(nc.sbuf_tensor(f"{name}_{n}", shape, dt))

        def sem(n):
            return nc.alloc_semaphore(f"{name}_{n}")

        self.stats = sb("stats", [P, NB, 6])
        self.mv = sb("mv", [P, NB, 2])
        self.var_eps = sb("var_eps", [P, NB])
        self.minus_half = sb("minus_half", [P, NB])
        self.rstd = sb("rstd", [P, NB])
        self.xn = sb("xn", [P, NB, D])
        self.stats_done = sem("stats_done")
        self.mv_done = sem("mv_done")
        self.half_set = sem("half_set")
        self.var_done = sem("var_done")
        self.rstd_done = sem("rstd_done")
        self.xn_done = sem("xn_done")
        self.transposed = sem("transposed")
        self.xnT_done = sem("xnT_done")

    def vector(self, v, x, width=D):
        for n in range(NB):
            v.bn_stats(self.stats[:, n, :], x[:, n, :]).then_inc(self.stats_done, 1)
        for n in range(NB):
            v.wait_ge(self.stats_done, n + 1)
            v.bn_aggr(self.mv[:, n, :], self.stats[:, n, :]).then_inc(self.mv_done, 1)
        for n in range(NB):
            if n % GB == 0:
                v.wait_ge(self.rstd_done, n // GB + 1)
            v.tensor_scalar(self.xn[:, n, 0:width], x[:, n, 0:width], self.mv[:, n, 0:1], self.rstd[:, n:n + 1],
                            ALU.subtract, ALU.mult).then_inc(self.xn_done, 1)

    def gpsimd(self, g):
        g.memset(self.minus_half[:], -0.5).then_inc(self.half_set, 1)
        g.wait_ge(self.half_set, 1)
        for k in range(NG):
            g.wait_ge(self.mv_done, GB * (k + 1))
            cols = slice(GB * k, GB * k + GB)
            g.tensor_scalar(self.var_eps[:, cols], self.mv[:, cols, 1], EPS, None,
                            ALU.add).then_inc(self.var_done, 1)
            g.wait_ge(self.var_done, k + 1)
            g.tensor_tensor(self.rstd[:, cols], self.var_eps[:, cols], self.minus_half[:, cols],
                            ALU.pow).then_inc(self.rstd_done, 1)

    def tensor(self, t, psum, ident, k):
        if k >= 2:
            t.wait_ge(self.xnT_done, k - 1)
        for m in range(GB):
            n = GB * k + m
            t.wait_ge(self.xn_done, n + 1)
            ins = t.transpose(psum[:, k % 2, m * T:m * T + T], self.xn[:, n, :], ident)
        ins.then_inc(self.transposed, 1)

    def scalar(self, a, psum, xnT, k):
        a.wait_ge(self.transposed, k + 1)
        a.activation(xnT[:, k * GT:k * GT + GT], psum[:, k % 2, :], ACT.Copy).then_inc(self.xnT_done, 1)


PAIRS = [(0, 0), (0, 1), (1, 0), (1, 1), (0, 2), (2, 0)]
KS = DH * len(PAIRS)


def project_layer0(nc, io, keep):
    with ExitStack() as ctx:
        def sb(n, shape, dt=F32):
            return ctx.enter_context(nc.sbuf_tensor(n, shape, dt))

        def sem(n):
            return nc.alloc_semaphore(n)

        wq, wk, wv = sb("p_wq", [P, D]), sb("p_wk", [P, D]), sb("p_wv", [P, D])
        bq, bk = sb("p_bq", [P, 1]), sb("p_bk", [P, 1])
        bv_rows, bo_rows = sb("p_bv_rows", [P, D]), sb("p_bo_rows", [P, D])
        kf, qf = sb("p_kf", [P, 2, GT]), sb("p_qf", [P, 2, GT])
        kb, qb = sb("p_kb", [P, 3, TOK], BF16), sb("p_qb", [P, 3, TOK], BF16)
        vt = sb("p_vt", [P, NB, D])
        tr_ps = ctx.enter_context(nc.psum_tensor("p_tr", [P, 2, GT], F32))
        q_ps = ctx.enter_context(nc.psum_tensor("p_q", [P, 2, GT], F32))
        k_ps = ctx.enter_context(nc.psum_tensor("p_k", [P, 2, GT], F32))
        v_ps = ctx.enter_context(nc.psum_tensor("p_v", [P, 2, GT], F32))
        ln = LayerNorm(nc, ctx, "p_ln")
        x_in, ctx_in, w_in = sem("p_x_in"), sem("p_ctx_in"), sem("p_w_in")
        ident_zero, ident_done = sem("p_ident_zero"), sem("p_ident_done")
        k_mm, v_mm, q_mm = sem("p_k_mm"), sem("p_v_mm"), sem("p_q_mm")
        k_b1, q_b1 = sem("p_k_b1"), sem("p_q_b1")
        k_r1, q_r1 = sem("p_k_r1"), sem("p_q_r1")
        k_b2, q_b2 = sem("p_k_b2"), sem("p_q_b2")
        k_b3, q_b3 = sem("p_k_b3"), sem("p_q_b3")
        v_done, v_out = sem("p_v_done"), sem("p_v_out")
        ks_done, qs_done, x_bo = sem("p_ks_done"), sem("p_qs_done"), sem("p_x_bo")
        x, ctxT, xnT, ident = keep["x"], keep["ctxT"], keep["xnT"], keep["ident"]
        ks, qs, v_dram = keep["ks"], keep["qs"], keep["v_dram"]

        def stack(eng, dst, parts, which, done):
            for s, pair in enumerate(PAIRS):
                eng.dma_start(dst[s * DH:(s + 1) * DH, :, :],
                              parts[:, pair[which], :]).then_inc(done, 16)

        with nc.Block() as block:
            @block.sync
            def _(sp):
                sp.dma_start(ctxT[:], io["ctxT"]).then_inc(ctx_in, 16)
                sp.dma_start(wk[:], io["Wk0"]).then_inc(w_in, 16)
                sp.dma_start(wv[:], io["Wv0"]).then_inc(w_in, 16)
                sp.dma_start(wq[:], io["Wq0"]).then_inc(w_in, 16)
                sp.dma_start(bk[:], io["bk0"]).then_inc(w_in, 16)
                sp.dma_start(bq[:], io["bq0"]).then_inc(w_in, 16)
                sp.dma_start(bv_rows[:], io["bv0"].broadcast_to([P, D])).then_inc(w_in, 16)
                sp.dma_start(bo_rows[:], io["bo0"].broadcast_to([P, D])).then_inc(w_in, 16)
                sp.wait_ge(k_b3, NG)
                stack(sp, ks, kb, 1, ks_done)
                sp.wait_ge(q_b3, NG)
                stack(sp, qs, qb, 0, qs_done)
                sp.wait_ge(ks_done, 16 * len(PAIRS))
                sp.wait_ge(qs_done, 16 * len(PAIRS))

            @block.gpsimd
            def _(g):
                g.memset(ident[:], 0.0).then_inc(ident_zero, 1)
                g.wait_ge(ident_zero, 1)
                g.affine_select(out=ident[:], in_=ident[:], compare_op=ALU.not_equal, fill=1.0, base=0,
                                pattern=[[-1, P]], channel_multiplier=1).then_inc(ident_done, 1)
                ln.gpsimd(g)
                for k in range(NG):
                    cols = slice(k * GT, k * GT + GT)
                    g.wait_ge(k_b1, 2 * k + 2)
                    g.tensor_tensor(kf[:, k % 2, :], kf[:, k % 2, :], kb[:, 0, cols],
                                    ALU.subtract).then_inc(k_r1, 1)
                    g.wait_ge(k_r1, k + 1)
                    g.tensor_copy(kb[:, 1, cols], kf[:, k % 2, :]).then_inc(k_b2, 1)
                    g.wait_ge(k_b2, k + 1)
                    g.tensor_tensor(kb[:, 2, cols], kf[:, k % 2, :], kb[:, 1, cols],
                                    ALU.subtract).then_inc(k_b3, 1)
                g.wait_ge(ln.xn_done, NB)
                g.wait_ge(w_in, 16 * 7)
                g.tensor_tensor(x[:], x[:], bo_rows[:].unsqueeze(1).broadcast_to([P, NB, D]),
                                ALU.add).then_inc(x_bo, 1)
                g.wait_ge(x_bo, 1)

            @block.tensor
            def _(t):
                t.wait_ge(ctx_in, 16)
                t.wait_ge(w_in, 16 * 7)
                for k in range(NG):
                    if k >= 2:
                        t.wait_ge(k_b1, 2 * (k - 1))
                    t.matmul(k_ps[:, k % 2, :], wk[:], ctxT[:, k * GT:k * GT + GT],
                             start=True, stop=True).then_inc(k_mm, 1)
                t.wait_ge(ident_done, 1)

                def values(k):
                    if k >= 2:
                        t.wait_ge(v_done, k - 1)
                    for m in range(GB):
                        n = GB * k + m
                        ins = t.matmul(v_ps[:, k % 2, m * T:m * T + T], ctxT[:, n * T:n * T + T], wv[:],
                                       start=True, stop=True)
                    ins.then_inc(v_mm, 1)

                def queries(k):
                    t.wait_ge(ln.xnT_done, k + 1)
                    if k >= 2:
                        t.wait_ge(q_b1, 2 * (k - 1))
                    t.matmul(q_ps[:, k % 2, :], wq[:], xnT[:, k * GT:k * GT + GT],
                             start=True, stop=True).then_inc(q_mm, 1)

                for k in range(NG):
                    ln.tensor(t, tr_ps, ident[:], k)
                    values(k)
                    queries(k)

            @block.scalar
            def _(a):
                a.dma_start(x[:], io["x"].rearrange("n t d -> t n d")).then_inc(x_in, 16)

                def parts(ps, bias, full, hi, mm, b1, done, k):
                    a.wait_ge(mm, k + 1)
                    if k >= 2:
                        a.wait_ge(done, k - 1)
                    a.activation(full[:, k % 2, :], ps[:, k % 2, :], ACT.Identity,
                                 bias=bias[:]).then_inc(b1, 1)
                    a.activation(hi[:, 0, k * GT:k * GT + GT], ps[:, k % 2, :], ACT.Identity,
                                 bias=bias[:]).then_inc(b1, 1)

                for k in range(NG):
                    parts(k_ps, bk, kf, kb, k_mm, k_b1, k_b3, k)
                    if k == 1:
                        ln.scalar(a, tr_ps, xnT, 0)
                for k in range(NG):
                    if k:
                        ln.scalar(a, tr_ps, xnT, k)
                    parts(q_ps, bq, qf, qb, q_mm, q_b1, q_b3, k)
                a.wait_ge(v_done, NG)
                a.dma_start(v_dram.rearrange("n t d -> t n d"), vt[:]).then_inc(v_out, 16)
                a.wait_ge(v_out, 16)

            @block.vector
            def _(v):
                v.wait_ge(x_in, 16)
                ln.vector(v, x)
                for k in range(NG):
                    v.wait_ge(v_mm, k + 1)
                    v.tensor_tensor(vt[:, GB * k:GB * k + GB, :],
                                    v_ps[:, k % 2, :].rearrange("p (m d) -> p m d", m=GB),
                                    bv_rows[:].unsqueeze(1).broadcast_to([P, GB, D]),
                                    ALU.add).then_inc(v_done, 1)
                    cols = slice(k * GT, k * GT + GT)
                    v.wait_ge(q_b1, 2 * k + 2)
                    v.tensor_tensor(qf[:, k % 2, :], qf[:, k % 2, :], qb[:, 0, cols],
                                    ALU.subtract).then_inc(q_r1, 1)
                    v.wait_ge(q_r1, k + 1)
                    v.tensor_copy(qb[:, 1, cols], qf[:, k % 2, :]).then_inc(q_b2, 1)
                    v.wait_ge(q_b2, k + 1)
                    v.tensor_tensor(qb[:, 2, cols], qf[:, k % 2, :], qb[:, 1, cols],
                                    ALU.subtract).then_inc(q_b3, 1)


def attend_layer0(nc, io, keep):
    HT = T // 2
    HJ = PIECES // 2
    with ExitStack() as ctx:
        def sb(n, shape, dt=F32):
            return ctx.enter_context(nc.sbuf_tensor(n, shape, dt))

        def sem(n):
            return nc.alloc_semaphore(n)

        ks, qs, v_dram, x, ident = keep["ks"], keep["qs"], keep["v_dram"], keep["x"], keep["ident"]
        wo = sb("a_wo", [P, D])
        kh = sb("a_kh", [P, 2, H, RT, PIECES], BF16)
        qn = sb("a_qn", [P, 2, PIECES, T], BF16)
        val = sb("a_val", [P, 2, H, 32])
        negmax, identr = sb("a_negmax", [P, 2, HT], F32R), sb("a_identr", [P, P], F32R)
        expd = sb("a_expd", [P, 2, 2, H, HT])
        total = sb("a_total", [P, 2, HT])
        rtotal = sb("a_rtotal", [P, 2, HT])
        prob = sb("a_prob", [P, 2, H, T])
        ot = sb("a_ot", [P, 2, PIECES, 4, RT])
        oT = sb("a_oT", [P, 2, T])
        s_ps = ctx.enter_context(nc.psum_tensor("a_s", [P, 2, H, HT], F32))
        o_ps = ctx.enter_context(nc.psum_tensor("a_o", [P, 2, 4, T], F32))
        y_ps = ctx.enter_context(nc.psum_tensor("a_y", [P, 2, GT], F32))
        rows_zero = sem("a_rows_zero")
        wo_in, val_zero, identr_done = sem("a_wo_in"), sem("a_val_zero"), sem("a_identr_done")
        val_in = [sem("a_val_in0"), sem("a_val_in1")]
        keyed, q_in = sem("a_keyed"), [sem("a_q_in0"), sem("a_q_in1")]
        scored, maxed, shifted, exped = sem("a_scored"), sem("a_maxed"), sem("a_shifted"), sem("a_exped")
        summed, inverted, probed = sem("a_summed"), sem("a_inverted"), sem("a_probed")
        mixed, ot_done, yed, x_done = sem("a_mixed"), sem("a_ot_done"), sem("a_yed"), sem("a_x_done")
        oT_in = [sem("a_oT_in0"), sem("a_oT_in1")]


        def loops(eng, body):
            for n in range(4):
                body(n, n % 2)
            with eng.Fori(2, NB // 2 - 1) as pair:
                body(pair * 2, 0)
                body(pair * 2 + 1, 1)
            body(NB - 2, 0)
            body(NB - 1, 1)

        def past(n, k):
            return not isinstance(n, int) or n >= k

        with nc.Block() as block:
            @block.sync
            def _(sp):
                sp.dma_start(wo[:], io["Wo0"]).then_inc(wo_in, 16)

                def load_values(n, b):
                    sp.dma_start(val[:, b, :, 0:DH],
                                 v_dram[bass.ds(n, 1)].rearrange("n (h b) (l d) -> (b l) (n h) d",
                                                                 b=RT, d=DH)).then_inc(val_in[b], 16)

                def load_queries(n, b):
                    sp.dma_start(qn[0:KS, b, :, :], qs[:, :, bass.ds(n * T, T)]).then_inc(q_in[b], 16)

                def shuffle(n, b):
                    sp.wait_ge(ot_done, n + 1)
                    for r in range(4):
                        sp.dma_start(oT[:, b, r * 32:r * 32 + 32],
                                     ot[32 * r:32 * r + DH, b, :, :, :].rearrange("d j q a -> d j (q a)")
                                     ).then_inc(oT_in[b], 16)

                sp.wait_ge(rows_zero, 2)
                load_queries(0, 0)
                load_queries(1, 1)
                sp.wait_ge(val_zero, 1)
                load_values(0, 0)
                load_values(1, 1)

                def body(n, b):
                    if not isinstance(n, int) or n + 2 < NB:
                        sp.wait_ge(scored, 2 * n + 2)
                        load_queries(n + 2, b)
                    if past(n, 2):
                        shuffle(n - 2, b)
                        load_values(n, b)

                loops(sp, body)
                shuffle(NB - 2, 0)
                shuffle(NB - 1, 1)

            @block.tensor
            def _(t):
                t.wait_ge(wo_in, 16)
                t.wait_ge(identr_done, 1)

                def scores(n, b, half):
                    t.wait_ge(keyed, n + 1)
                    t.wait_ge(q_in[b], n * 8 + (16 - 8 * b))
                    for h in range(H):
                        cols = slice(RT * h, RT * h + RT)
                        ins = t.matmul(s_ps[:, half, h, :],
                                       kh[:, b, h, :, :],
                                       qn[:, b, half * HJ:half * HJ + HJ, cols],
                                       start=(h % 8 == 0), stop=False, skip_group_check=True)
                    ins.then_inc(scored, 1)

                def shift(n, half):
                    t.wait_ge(maxed, 2 * n + half + 1)
                    for c in range(2):
                        ins = t.matmul(s_ps[:, half, 8 * c:8 * c + 8, :], identr[:],
                                       negmax[:, half, :].unsqueeze(1).broadcast_to([P, 8, HT]),
                                       start=False, stop=True, skip_group_check=True)
                    ins.then_inc(shifted, 1)

                def mix(n, b, half):
                    t.wait_ge(probed, 2 * n + half + 1)
                    if half == 0:
                        t.wait_ge(val_in[b], n * 8 + (16 - 8 * b))
                        if past(n, 2):
                            t.wait_ge(ot_done, n - 1)
                    cols = slice(half * HT, half * HT + HT)
                    for q in range(4):
                        for r in range(4):
                            ins = t.matmul(o_ps[32 * r:32 * r + 32, b, q, cols], val[:, b, 4 * r + q, :],
                                           prob[:, b, 4 * r + q, cols], start=True, stop=True)
                    ins.then_inc(mixed, 1)

                def project(n, b):
                    t.wait_ge(oT_in[b], n * 32 + (64 - 32 * b))
                    if past(n, 2):
                        t.wait_ge(x_done, n - 1)
                    t.matmul(y_ps[:, b, 0:D], oT[:, b, :], wo[:], start=True, stop=True).then_inc(yed, 1)

                scores(0, 0, 0)
                scores(0, 0, 1)

                def body(n, b):
                    for half in range(2):
                        shift(n, half)
                        if past(n, 1):
                            mix(n - 1, 1 - b, half)
                        if not isinstance(n, int) or n + 1 < NB:
                            t.wait_ge(exped, 2 * n + half + 1)
                            scores(n + 1, 1 - b, half)
                    if past(n, 3):
                        project(n - 3, 1 - b)

                loops(t, body)
                mix(NB - 1, 1, 0)
                mix(NB - 1, 1, 1)
                for n in range(NB - 3, NB):
                    project(n, n % 2)

            @block.vector
            def _(v):
                v.memset(kh[:], 0.0).then_inc(rows_zero, 1)
                v.memset(val[:], 0.0).then_inc(val_zero, 1)

                def maximum(n, half):
                    v.wait_ge(scored, 2 * n + half + 1)
                    if past(n, 1):
                        v.wait_ge(shifted, 2 * n + half - 1)
                    v.tensor_reduce(negmax[:, half, :], s_ps[:, half, :, :].rearrange("p h t -> p t h"),
                                    AX.X, ALU.max, negate=True).then_inc(maxed, 1)

                def totals(n, b, half):
                    v.wait_ge(exped, 2 * n + half + 1)
                    if past(n, 1):
                        v.wait_ge(probed, 2 * n + half - 1)
                    v.tensor_reduce(total[:, half, :], expd[:, b, half, :, :].rearrange("p h t -> p t h"),
                                    AX.X, ALU.add).then_inc(summed, 1)
                    v.wait_ge(summed, 2 * n + half + 1)
                    v.reciprocal(rtotal[:, half, :], total[:, half, :]).then_inc(inverted, 1)

                def residual(n, b):
                    v.wait_ge(yed, n + 1)
                    v.tensor_tensor(x[:, bass.ds(n, 1), :], x[:, bass.ds(n, 1), :],
                                    y_ps[:, bass.ds(b, 1), 0:D], ALU.add).then_inc(x_done, 1)

                def body(n, b):
                    maximum(n, 0)
                    if past(n, 1):
                        totals(n - 1, 1 - b, 1)
                    maximum(n, 1)
                    totals(n, b, 0)
                    if past(n, 4):
                        residual(n - 4, b)

                loops(v, body)
                totals(NB - 1, 1, 1)
                for n in range(NB - 4, NB):
                    residual(n, n % 2)

            @block.scalar
            def _(a):
                def exponentials(n, b, half):
                    a.wait_ge(shifted, 2 * n + half + 1)
                    if past(n, 2):
                        a.wait_ge(probed, 2 * n + half - 3)
                    a.activation(expd[:, b, half, :, :], s_ps[:, half, :, :], ACT.Exp,
                                 scale=float(D) ** -0.5).then_inc(exped, 1)

                def copy_out(n, b):
                    a.wait_ge(mixed, 2 * n + 2)
                    if past(n, 2):
                        a.wait_ge(yed, n - 1)
                    a.activation(ot[:, b, :, :, :].rearrange("p j q a -> p q j a"),
                                 o_ps[:, b, :, :].rearrange("p q (j a) -> p q j a", a=RT),
                                 ACT.Copy).then_inc(ot_done, 1)

                def arrange_keys(n, b):
                    if past(n, 2):
                        a.wait_ge(scored, 2 * n - 2)
                    a.activation(kh[0:KS, b, :, :, :],
                                 ks[:, :, bass.ds(n * T, T)].rearrange("k l (h b) -> k h b l", b=RT),
                                 ACT.Copy).then_inc(keyed, 1)

                a.activation(identr[:], ident[:], ACT.Copy).then_inc(identr_done, 1)
                a.wait_ge(rows_zero, 2)
                arrange_keys(0, 0)
                arrange_keys(1, 1)

                def body(n, b):
                    exponentials(n, b, 0)
                    if past(n, 2):
                        copy_out(n - 2, b)
                    exponentials(n, b, 1)
                    if not isinstance(n, int) or n + 2 < NB:
                        arrange_keys(n + 2, b)

                loops(a, body)
                copy_out(NB - 2, 0)
                copy_out(NB - 1, 1)

            @block.gpsimd
            def _(g):
                g.memset(qn[:], 0.0).then_inc(rows_zero, 1)

                def probabilities(n, b, half):
                    g.wait_ge(inverted, 2 * n + half + 1)
                    if past(n, 2):
                        g.wait_ge(mixed, 2 * n + half - 3)
                    g.tensor_tensor(prob[:, b, :, half * HT:half * HT + HT], expd[:, b, half, :, :],
                                    rtotal[:, half, :].unsqueeze(1).broadcast_to([P, H, HT]),
                                    ALU.mult).then_inc(probed, 1)

                def body(n, b):
                    probabilities(n, b, 0)
                    probabilities(n, b, 1)

                loops(g, body)


class Gate:

    def __init__(self, nc, ctx, name):
        def sb(n, shape, dt=F32):
            return ctx.enter_context(nc.sbuf_tensor(f"{name}_{n}", shape, dt))

        def sem(n):
            return nc.alloc_semaphore(f"{name}_{n}")

        self.wr = sb("wr", [P, E])
        self.logit = sb("logit", [P, NB, E])
        self.top = sb("top", [P, NB, 8])
        self.away = sb("away", [P, NB, E])
        self.expd = sb("expd", [P, NB, E])
        self.kept = sb("kept", [P, NB, E])
        self.total = sb("total", [P, NB])
        self.rtotal = sb("rtotal", [P, NB])
        self.gate = sb("gate", [P, NB, E])
        self.gateT = sb("gateT", [E, TOK])
        self.wr_in, self.logits, self.away_done = sem("wr_in"), sem("logits"), sem("away_done")
        self.exped, self.gated, self.turned = sem("exped"), sem("gated"), sem("turned")
        self.gateT_done, self.gateT_out, self.step = sem("gateT_done"), sem("gateT_out"), sem("step")
        self.steps = 0

    def then(self, v, ins):
        self.steps += 1
        ins.then_inc(self.step, 1)
        v.wait_ge(self.step, self.steps)

    def tensor_logits(self, t, psum, xnT, xnT_done):
        t.wait_ge(self.wr_in, 16)
        for n in range(NB):
            t.wait_ge(xnT_done, n // GB + 1)
            ins = t.matmul(psum[:, n * E:n * E + E], xnT[:, n * T:n * T + T], self.wr[:],
                           start=True, stop=True)
        ins.then_inc(self.logits, 1)

    def tensor_turn(self, t, psum, ident):
        t.wait_ge(self.gated, 1)
        for k in range(NG):
            if k >= 2:
                t.wait_ge(self.gateT_done, k - 1)
            for m in range(GB):
                ins = t.transpose(psum[0:E, k % 2, m * T:m * T + T], self.gate[:, GB * k + m, :], ident)
            ins.then_inc(self.turned, 1)

    def scalar_exp(self, a):
        a.wait_ge(self.away_done, 1)
        a.activation(self.expd[:], self.away[:], ACT.Exp).then_inc(self.exped, 1)

    def scalar_turned(self, a, psum):
        for k in range(NG):
            a.wait_ge(self.turned, k + 1)
            a.activation(self.gateT[:, k * GT:k * GT + GT], psum[0:E, k % 2, :],
                         ACT.Copy).then_inc(self.gateT_done, 1)

    def sync_out(self, sp, gate_dram):
        sp.wait_ge(self.gateT_done, NG)
        sp.dma_start(gate_dram, self.gateT[:]).then_inc(self.gateT_out, 16)
        sp.wait_ge(self.gateT_out, 16)


def split_weights(eng, raw, zeros, hi, lo, hi_done, lo_done, count):
    eng.tensor_tensor(hi, raw, zeros, ALU.add).then_inc(hi_done, 1)
    eng.wait_ge(hi_done, count)
    eng.tensor_tensor(lo, raw, hi.bitcast(F32), ALU.subtract).then_inc(lo_done, 1)


def three_passes(t, out, w_hi, w_lo, x_hi, x_lo, start, stop, **kw):
    t.matmul(out, w_hi, x_hi, start=start, stop=False, **kw)
    t.matmul(out, w_hi, x_lo, start=False, stop=False, **kw)
    return t.matmul(out, w_lo, x_hi, start=False, stop=stop, **kw)


FF = 512
KF = FF // P
UNITS = NG * KF


def experts_layer0(nc, io, keep):
    with ExitStack() as ctx:
        def sb(n, shape, dt=F32):
            return ctx.enter_context(nc.sbuf_tensor(n, shape, dt))

        def sem(n):
            return nc.alloc_semaphore(n)

        x, ident, gate_dram = keep["x"], keep["ident"], keep["gate_dram"]
        xnT = sb("b_xnT", [P, TOK])
        x_hi, x_lo = sb("b_x_hi", [P, TOK], F32R), sb("b_x_lo", [P, TOK], F32R)
        ln = LayerNorm(nc, ctx, "b_ln")
        gate = Gate(nc, ctx, "b_gate")
        br_rows = sb("b_br_rows", [P, E])
        zeros, zeroed = sb("b_zeros", [P, FF]), sem("b_zeroed")
        b1, b2, b1_now = sb("b_b1", [P, E, KF]), sb("b_b2", [P, E]), sb("b_b1_now", [P, 2, KF])
        w1, w2 = sb("b_w1", [P, 2, FF]), sb("b_w2", [P, 2, KF, D])
        w1_hi, w1_lo = sb("b_w1_hi", [P, 2, FF], F32R), sb("b_w1_lo", [P, 2, FF], F32R)
        w2_hi, w2_lo = sb("b_w2_hi", [P, 2, KF, D], F32R), sb("b_w2_lo", [P, 2, KF, D], F32R)
        inner = sb("b_inner", [P, 2, KF, GT])
        in_hi, in_lo = sb("b_in_hi", [P, 2, KF, GT], F32R), sb("b_in_lo", [P, 2, KF, GT], F32R)
        gate_rows = sb("b_gate_rows", [P, 2, TOK])
        part = sb("b_part", [P, 2, GT])
        acc = sb("b_acc", [P, TOK])
        up_ps = ctx.enter_context(nc.psum_tensor("b_up", [P, KF, GT], F32))
        down_ps = ctx.enter_context(nc.psum_tensor("b_down", [P, 2, GT], F32))
        tr_ps = ctx.enter_context(nc.psum_tensor("b_tr", [P, 2, GT], F32))
        small_in, b1_set = sem("b_small_in"), sem("b_b1_set")
        x_hi_done, x_lo_done = sem("b_x_hi_done"), sem("b_x_lo_done")
        w_in = [sem("b_w_in0"), sem("b_w_in1")]
        rows_in = [sem("b_rows_in0"), sem("b_rows_in1")]
        w1_hi_done, w1_lo_done = sem("b_w1_hi_done"), sem("b_w1_lo_done")
        w2_hi_done, w2_lo_done = sem("b_w2_hi_done"), sem("b_w2_lo_done")
        upped, innered, in_hi_done, in_lo_done = (sem("b_upped"), sem("b_innered"), sem("b_in_hi_done"),
                                                  sem("b_in_lo_done"))
        downed, parted, acced = sem("b_downed"), sem("b_parted"), sem("b_acced")
        turned, x_done = sem("b_turned"), sem("b_x_done")

        def experts(eng, body):
            body(0, 0)
            body(1, 1)
            with eng.Fori(1, E // 2) as pair:
                body(pair * 2, 0)
                body(pair * 2 + 1, 1)

        def first(e):
            return isinstance(e, int) and e == 0

        with nc.Block() as block:
            @block.sync
            def _(sp):
                sp.dma_start(gate.wr[:], io["Wr0"]).then_inc(gate.wr_in, 16)
                sp.dma_start(br_rows[:], io["br0"].broadcast_to([P, E])).then_inc(small_in, 16)
                sp.dma_start(b1[:], io["b1"]).then_inc(small_in, 16)
                sp.dma_start(b2[:], io["b2"]).then_inc(small_in, 16)

                def load_weights(e, b):
                    sp.dma_start(w1[:, b, :].unsqueeze(1), io["W1"][bass.ds(e, 1)].rearrange("e c f -> c e f")
                                 ).then_inc(w_in[b], 16)
                    sp.dma_start(w2[:, b, :, :], io["W2"][bass.ds(e, 1)].rearrange("e (k p) d -> p (e k) d", p=P)
                                 ).then_inc(w_in[b], 16)

                def load_rows(e, b):
                    sp.dma_start(gate_rows[:, b, :], gate_dram[bass.ds(e, 1), :].broadcast_to([P, TOK])
                                 ).then_inc(rows_in[b], 16)

                load_weights(0, 0)
                load_weights(1, 1)
                gate.sync_out(sp, gate_dram)
                load_rows(0, 0)
                load_rows(1, 1)

                def refill(e, b):
                    sp.wait_ge(w2_lo_done, e + 1)
                    load_weights(e + 2, b)
                    sp.wait_ge(parted, (e + 1) * NG)
                    load_rows(e + 2, b)

                with sp.Fori(0, E // 2 - 1) as pair:
                    refill(pair * 2, 0)
                    refill(pair * 2 + 1, 1)

            @block.gpsimd
            def _(g):
                ln.gpsimd(g)
                g.memset(zeros[:], 0.0).then_inc(zeroed, 1)
                g.wait_ge(zeroed, 1)

                def body(e, b):
                    g.wait_ge(w_in[b], e * 16 + (32 - 16 * b))
                    if not (isinstance(e, int) and e < 2):
                        g.wait_ge(downed, (e - 1) * NG)
                    split_weights(g, w1[:, b, :], zeros[:], w1_hi[:, b, :], w1_lo[:, b, :],
                                  w1_hi_done, w1_lo_done, e + 1)
                    split_weights(g, w2[:, b, :, :], zeros[:].rearrange("p (k d) -> p k d", k=KF), w2_hi[:, b, :, :], w2_lo[:, b, :, :],
                                  w2_hi_done, w2_lo_done, e + 1)

                experts(g, body)

            @block.tensor
            def _(t):
                for k in range(NG):
                    ln.tensor(t, tr_ps, ident[:], k)
                gate.tensor_logits(t, down_ps[:, 0, :], xnT, ln.xnT_done)

                def up(e, b, k):
                    if k == 0:
                        t.wait_ge(w1_lo_done, e + 1)
                    if first(e):
                        t.wait_ge(x_lo_done, k + 1)
                    for c in range(KF):
                        if not (first(e) and k == 0):
                            t.wait_ge(innered, e * UNITS + (k * KF + c - KF + 1))
                        cols = slice(k * GT, k * GT + GT)
                        chunk = slice(c * P, c * P + P)
                        three_passes(t, up_ps[:, c, :], w1_hi[:, b, chunk], w1_lo[:, b, chunk],
                                     x_hi[:, cols], x_lo[:, cols], True, True).then_inc(upped, 1)

                def down(e, b, k):
                    if k == 0:
                        t.wait_ge(w2_lo_done, e + 1)
                    if not (first(e) and k < 2):
                        t.wait_ge(parted, e * NG + (k - 1))
                    for c in range(KF):
                        t.wait_ge(in_lo_done, e * UNITS + (k * KF + c + 1))
                        ins = three_passes(t, down_ps[:, k % 2, :], w2_hi[:, b, c, :], w2_lo[:, b, c, :],
                                           in_hi[:, k % 2, c, :], in_lo[:, k % 2, c, :],
                                           c == 0, c == KF - 1)
                    ins.then_inc(downed, 1)

                def body(e, b):
                    for k in range(NG):
                        up(e, b, k)
                        if k:
                            down(e, b, k - 1)
                        elif not first(e):
                            down(e - 1, 1 - b, NG - 1)
                        else:
                            gate.tensor_turn(t, tr_ps, ident[:])

                experts(t, body)
                down(E - 1, 1, NG - 1)
                for k in range(NG):
                    t.wait_ge(acced, (E - 1) * NG + k + 1)
                    if k >= 2:
                        t.wait_ge(x_done, k - 1)
                    for m in range(GB):
                        n = GB * k + m
                        ins = t.transpose(tr_ps[:, k % 2, m * T:m * T + T], acc[:, n * T:n * T + T], ident[:])
                    ins.then_inc(turned, 1)

            @block.scalar
            def _(a):
                for k in range(NG):
                    ln.scalar(a, tr_ps, xnT, k)
                    cols = slice(k * GT, k * GT + GT)
                    a.wait_ge(ln.xnT_done, k + 1)
                    a.activation(x_hi[:, cols], xnT[:, cols], ACT.Copy).then_inc(x_hi_done, 1)
                gate.scalar_exp(a)

                def round_inner(e, unit):
                    k, c = unit // KF, unit % KF
                    a.wait_ge(innered, e * UNITS + (unit + 1))
                    if not (first(e) and k < 2):
                        a.wait_ge(downed, e * NG + (k - 1))
                    a.activation(in_hi[:, k % 2, c, :], inner[:, k % 2, c, :], ACT.Copy).then_inc(in_hi_done, 1)

                a.wait_ge(small_in, 48)

                def body(e, b):
                    a.activation(b1_now[:, b, :].unsqueeze(1), b1[:, bass.ds(e, 1), :], ACT.Copy).then_inc(b1_set, 1)
                    a.wait_ge(b1_set, e + 1)
                    for unit in range(UNITS):
                        k, c = unit // KF, unit % KF
                        a.wait_ge(upped, e * UNITS + (unit + 1))
                        if not (first(e) and k < 2):
                            a.wait_ge(in_lo_done, e * UNITS + (unit - 2 * KF + 1))
                        a.activation(inner[:, k % 2, c, :], up_ps[:, c, :], ACT.Gelu,
                                     bias=b1_now[:, b, c:c + 1]).then_inc(innered, 1)
                        if unit:
                            round_inner(e, unit - 1)
                        if first(e) and unit == KF - 1:
                            gate.scalar_turned(a, tr_ps)
                    round_inner(e, UNITS - 1)

                experts(a, body)

            @block.vector
            def _(v):
                ln.vector(v, x)
                for k in range(NG):
                    cols = slice(k * GT, k * GT + GT)
                    v.wait_ge(x_hi_done, k + 1)
                    v.tensor_tensor(x_lo[:, cols], xnT[:, cols], x_hi[:, cols].bitcast(F32),
                                    ALU.subtract).then_inc(x_lo_done, 1)
                v.wait_ge(small_in, 48)
                v.wait_ge(gate.logits, 1)
                gate.then(v, v.tensor_tensor(gate.logit[:], down_ps[:, 0, 0:NB * E].rearrange("p (n e) -> p n e", e=E),
                                             br_rows[:].unsqueeze(1).broadcast_to([P, NB, E]), ALU.add))
                for n in range(NB):
                    ins = v.max(gate.top[:, n, :], gate.logit[:, n, :])
                gate.then(v, ins)
                v.tensor_tensor(gate.away[:], gate.logit[:], gate.top[:, :, 0:1].broadcast_to([P, NB, E]),
                                ALU.subtract).then_inc(gate.away_done, 1)
                gate.then(v, v.tensor_tensor(gate.kept[:], gate.logit[:],
                                             gate.top[:, :, 1:2].broadcast_to([P, NB, E]), ALU.is_ge))
                v.wait_ge(gate.exped, 1)
                gate.then(v, v.tensor_tensor(gate.kept[:], gate.kept[:], gate.expd[:], ALU.mult))
                gate.then(v, v.tensor_reduce(gate.total[:], gate.kept[:], AX.X, ALU.add))
                gate.then(v, v.reciprocal(gate.rtotal[:], gate.total[:]))
                v.tensor_tensor(gate.gate[:], gate.kept[:], gate.rtotal[:].unsqueeze(2).broadcast_to([P, NB, E]),
                                ALU.mult).then_inc(gate.gated, 1)

                def rest_inner(e, unit):
                    k, c = unit // KF, unit % KF
                    v.wait_ge(in_hi_done, e * UNITS + (unit + 1))
                    if not (first(e) and k < 2):
                        v.wait_ge(downed, e * NG + (k - 1))
                    v.tensor_tensor(in_lo[:, k % 2, c, :], inner[:, k % 2, c, :],
                                    in_hi[:, k % 2, c, :].bitcast(F32), ALU.subtract).then_inc(in_lo_done, 1)

                def weigh(e, b, k):
                    cols = slice(k * GT, k * GT + GT)
                    if k == 0:
                        v.wait_ge(rows_in[b], e * 8 + (16 - 8 * b))
                    v.wait_ge(downed, e * NG + (k + 1))
                    if first(e):
                        v.scalar_tensor_tensor(acc[:, cols], down_ps[:, k % 2, :], b2[:, 0:1],
                                               gate_rows[:, b, cols], ALU.add, ALU.mult).then_inc(parted, 1)
                        v.wait_ge(parted, k + 1)
                        v.engine_nop().then_inc(acced, 1)
                        return
                    v.scalar_tensor_tensor(part[:, k % 2, :], down_ps[:, k % 2, :], b2[:, bass.ds(e, 1)],
                                           gate_rows[:, b, cols], ALU.add, ALU.mult).then_inc(parted, 1)
                    v.wait_ge(parted, e * NG + (k + 1))
                    v.wait_ge(acced, (e - 1) * NG + (k + 1))
                    v.tensor_tensor(acc[:, cols], acc[:, cols], part[:, k % 2, :], ALU.add).then_inc(acced, 1)

                def body(e, b):
                    for k in range(NG):
                        for c in range(KF):
                            rest_inner(e, k * KF + c)
                        if k:
                            weigh(e, b, k - 1)
                        elif not first(e):
                            weigh(e - 1, 1 - b, NG - 1)

                experts(v, body)
                weigh(E - 1, 1, NG - 1)
                for k in range(NG):
                    v.wait_ge(turned, k + 1)
                    v.tensor_tensor(x[:, GB * k:GB * k + GB, :], x[:, GB * k:GB * k + GB, :],
                                    tr_ps[:, k % 2, :].rearrange("p (m d) -> p m d", m=GB),
                                    ALU.add).then_inc(x_done, 1)


H1, DK = 16, 64
HQ = 4
NQ = H1 // HQ


def attend_layer1(nc, io, keep):
    with ExitStack() as ctx:
        def sb(n, shape, dt=F32):
            return ctx.enter_context(nc.sbuf_tensor(n, shape, dt))

        def sem(n):
            return nc.alloc_semaphore(n)

        x, ident, ctxT = keep["x"], keep["ident"], keep["ctxT"]
        ln = LayerNorm(nc, ctx, "c_ln")
        wq, wk = sb("c_wq", [DK, H1, D]), sb("c_wk", [DK, H1, D])
        wv, wo = sb("c_wv", [DK, H1, D]), sb("c_wo", [DK, H1, D])
        bq, bk, bv = sb("c_bq", [DK, H1]), sb("c_bk", [DK, H1]), sb("c_bv", [DK, H1])
        bo_rows, bias_rows = sb("c_bo_rows", [P, D]), sb("c_bias_rows", [P, D])
        wq2 = sb("c_wq2", [DK, H1, D])
        foldA = sb("c_foldA", [P, H1, D])
        foldB = sb("c_foldB", [P, H1, D])
        kbias = sb("c_kbias", [P, H1])
        xnT = sb("c_xnT", [P, TOK])
        xq, cq = sb("c_xq", [P, 2, T]), sb("c_cq", [P, 2, T])
        mask = sb("c_mask", [P, 2, T], U8)
        fill = sb("c_fill", [P, 1])
        tick = sb("c_tick", [P, 1])
        key = sb("c_key", [P, 2, H1, T])
        val = sb("c_val", [P, 2, H1, D])
        negmax, total = sb("c_negmax", [P, NQ, HQ]), sb("c_total", [P, NQ, HQ])
        rtotal = sb("c_rtotal", [P, NQ, HQ])
        expd, prob = sb("c_expd", [P, NQ, HQ, T]), sb("c_prob", [P, NQ, HQ, T])
        probT = sb("c_probT", [P, NQ, HQ, T])
        kv_ps = ctx.enter_context(nc.psum_tensor("c_kv", [P, 2, HQ, T], F32))
        s_ps = ctx.enter_context(nc.psum_tensor("c_s", [P, 2, HQ, T], F32))
        t_ps = ctx.enter_context(nc.psum_tensor("c_t", [P, 2, HQ, T], F32))
        o_ps = ctx.enter_context(nc.psum_tensor("c_o", [P, 2, GT], F32))

        w_in, filled, last_one = sem("c_w_in"), sem("c_filled"), sem("c_last_one")
        off_last, wq_done = sem("c_off_last"), sem("c_wq_done")
        folded, fold_out, biased, bias_done = sem("c_folded"), sem("c_fold_out"), sem("c_biased"), sem("c_bias_done")
        x_bias = sem("c_x_bias")
        batch_in = [sem("c_batch_in0"), sem("c_batch_in1")]
        key_mm, keyed, val_mm, valued = sem("c_key_mm"), sem("c_keyed"), sem("c_val_mm"), sem("c_valued")
        scored, masked, maxed, exped = sem("c_scored"), sem("c_masked"), sem("c_maxed"), sem("c_exped")
        inverted, probed, turned, probTed = sem("c_inverted"), sem("c_probed"), sem("c_turned"), sem("c_probTed")
        mixed, x_done = sem("c_mixed"), sem("c_x_done")

        def loops(eng, body):
            for n in range(4):
                body(n, n % 2)
            with eng.Fori(2, NB // 2 - 1) as pair:
                body(pair * 2, 0)
                body(pair * 2 + 1, 1)
            body(NB - 2, 0)
            body(NB - 1, 1)

        def known(n):
            return isinstance(n, int)

        def before(n, b, q, lag):
            back = (lag - q + NQ - 1) // NQ if lag > q else 0
            n, b, q = n - back, (b + back) % 2, q + back * NQ - lag
            return None if known(n) and n < 0 else (n, b, q)

        with nc.Block() as block:
            @block.sync
            def _(sp):
                for dst, src in ((wq, "wQ"), (wk, "wK"), (wv, "wV"), (wo, "wO")):
                    sp.dma_start(dst[:], io[src].rearrange("(h k) c -> k h c", k=DK)).then_inc(w_in, 16)
                for dst, src in ((bq, "bQ"), (bk, "bK"), (bv, "bV")):
                    sp.dma_start(dst[:], io[src]).then_inc(w_in, 16)
                sp.dma_start(bo_rows[:], io["bO"].broadcast_to([P, D])).then_inc(w_in, 16)
                sp.wait_ge(ln.xnT_done, NG)

                def load_batch(n, b):
                    cols = bass.ds(n * T, T)
                    sp.dma_start(xq[:, b, :], xnT[:, cols]).then_inc(batch_in[b], 16)
                    sp.dma_start(cq[:, b, :], ctxT[:, cols]).then_inc(batch_in[b], 16)
                    sp.dma_start(mask[:, b, :].unsqueeze(1), io["mask"][bass.ds(n, 1)].rearrange("n t s -> t n s")
                                 ).then_inc(batch_in[b], 16)

                load_batch(0, 0)
                load_batch(1, 1)
                with sp.Fori(0, NB // 2 - 1) as pair:
                    for b in range(2):
                        n = pair * 2 + b
                        sp.wait_ge(masked, (n + 1) * NQ)
                        load_batch(n + 2, b)

            @block.gpsimd
            def _(g):
                g.memset(fill[:], -10000.0).then_inc(filled, 1)
                g.memset(ln.xn[:, :, D - 1:D], 1.0).then_inc(last_one, 1)
                g.wait_ge(w_in, 16 * 8)
                g.tensor_tensor(wq2[:, :, 0:D - 1], wq[:, :, 0:D - 1],
                                wq[:, :, D - 1:D].broadcast_to([DK, H1, D - 1]), ALU.subtract).then_inc(off_last, 1)
                g.tensor_copy(wq2[:, :, D - 1:D], bq[:].unsqueeze(2)).then_inc(off_last, 1)
                g.wait_ge(off_last, 2)
                g.tensor_scalar(wq2[:], wq2[:], float(DK) ** -0.5, None, ALU.mult).then_inc(wq_done, 1)
                ln.gpsimd(g)
                g.wait_ge(ln.xn_done, NB)
                g.wait_ge(bias_done, 1)
                g.tensor_tensor(x[:], x[:], bias_rows[:].unsqueeze(1).broadcast_to([P, NB, D]),
                                ALU.add).then_inc(x_bias, 1)

                def body(n, b):
                    for q in range(NQ):
                        g.wait_ge(inverted, n * NQ + (q + 1))
                        if not (known(n) and n == 0):
                            g.wait_ge(turned, (n - 1) * NQ + (q + 1))
                        g.tensor_tensor(prob[:, q, :, :], expd[:, q, :, :],
                                        rtotal[:, q, :].unsqueeze(2).broadcast_to([P, HQ, T]),
                                        ALU.mult).then_inc(probed, 1)

                loops(g, body)

            @block.tensor
            def _(t):
                for k in range(NG):
                    ln.tensor(t, kv_ps[:].rearrange("p b h t -> p b (h t)"), ident[:], k)
                t.wait_ge(w_in, 16 * 8)
                t.wait_ge(wq_done, 1)
                for i in range(2 * NQ):
                    q, bank = i % NQ, (s_ps, t_ps)[i // 2 % 2][:, i % 2, :, :]
                    if i >= 4:
                        t.wait_ge(fold_out, i - 3)
                    for j in range(HQ):
                        h = HQ * q + j
                        lhs, rhs = (wk, wq2) if i < NQ else (wv, wo)
                        ins = t.matmul(bank[:, j, :], lhs[:, h, :], rhs[:, h, :], start=True, stop=True)
                    ins.then_inc(folded, 1)
                for h in range(H1):
                    t.matmul(o_ps[:, 0, h:h + 1], wq2[:, h, :], bk[:, h:h + 1], start=True, stop=True)
                for h in range(H1):
                    ins = t.matmul(o_ps[:, 1, 0:D], bv[:, h:h + 1].broadcast_to([DK, P]), wo[:, h, :],
                                   start=(h == 0), stop=(h == H1 - 1))
                ins.then_inc(biased, 1)
                t.wait_ge(fold_out, 2 * NQ)

                def keys(n, b, q):
                    if q == 0:
                        t.wait_ge(batch_in[b], n * 24 + (48 - 24 * b))
                    if not (known(n) and n == 0 and q == 0):
                        t.wait_ge(keyed, n * NQ + q)
                    for j in range(HQ):
                        ins = t.matmul(kv_ps[:, 0, j, :], foldA[:, HQ * q + j, :], cq[:, b, :],
                                       start=True, stop=True)
                    ins.then_inc(key_mm, 1)

                def values(n, b, q):
                    if not (known(n) and n == 0 and q == 0):
                        t.wait_ge(valued, n * NQ + q)
                    t.matmul(kv_ps[:, 1, :, :], cq[:, b, :], foldB[:, HQ * q:HQ * q + HQ, :],
                             start=True, stop=True).then_inc(val_mm, 1)

                def scores(n, b, q):
                    t.wait_ge(keyed, n * NQ + (q + 1))
                    if not (known(n) and n == 0 and q < 2):
                        t.wait_ge(exped, n * NQ + (q - 1))
                    t.matmul(s_ps[:, q % 2, :, :], xq[:, b, :], key[:, b, HQ * q:HQ * q + HQ, :],
                             start=True, stop=True).then_inc(scored, 1)

                def turn(n, b, q):
                    t.wait_ge(probed, n * NQ + (q + 1))
                    if not (known(n) and n == 0 and q < 2):
                        t.wait_ge(probTed, n * NQ + (q - 1))
                    for j in range(HQ):
                        ins = t.transpose(t_ps[:, q % 2, j, :], prob[:, q, j, :], ident[:])
                    ins.then_inc(turned, 1)

                def mix(n, b, q):
                    t.wait_ge(probTed, n * NQ + (q + 1))
                    if q == 0:
                        t.wait_ge(valued, (n + 1) * NQ)
                        if not (known(n) and n < 2):
                            t.wait_ge(x_done, n - 1)
                    for j in range(HQ):
                        h = HQ * q + j
                        ins = t.matmul(o_ps[:, b, 0:D], probT[:, q, j, :], val[:, b, h, :],
                                       start=(h == 0), stop=(h == H1 - 1))
                    ins.then_inc(mixed, 1)

                for q in range(NQ):
                    keys(0, 0, q)
                    values(0, 0, q)

                def body(n, b):
                    for q in range(NQ):
                        scores(n, b, q)
                        if not (known(n) and n + 1 == NB):
                            keys(n + 1, 1 - b, q)
                            values(n + 1, 1 - b, q)
                        for step, lag in ((turn, 2), (mix, 3)):
                            at = before(n, b, q, lag)
                            if at:
                                step(*at)

                loops(t, body)
                for q in range(3):
                    if q < 2:
                        turn(*before(NB, 0, q, 2))
                    mix(*before(NB, 0, q, 3))

            @block.scalar
            def _(a):
                for k in range(NG):
                    ln.scalar(a, kv_ps[:].rearrange("p b h t -> p b (h t)"), xnT, k)
                for i in range(2 * NQ):
                    q, bank = i % NQ, (s_ps, t_ps)[i // 2 % 2][:, i % 2, :, :]
                    a.wait_ge(folded, i + 1)
                    a.activation((foldA, foldB)[i // NQ][:, HQ * q:HQ * q + HQ, :], bank,
                                 ACT.Copy).then_inc(fold_out, 1)
                a.wait_ge(biased, 1)
                a.activation(kbias[:], o_ps[:, 0, 0:H1], ACT.Copy).then_inc(fold_out, 1)

                def copy_values(n, b, q):
                    a.wait_ge(val_mm, n * NQ + (q + 1))
                    if not (known(n) and n < 2):
                        a.wait_ge(mixed, (n - 2) * NQ + (q + 1))
                    a.activation(val[:, b, HQ * q:HQ * q + HQ, :], kv_ps[:, 1, :, :], ACT.Copy).then_inc(valued, 1)

                def exponentials(n, b, q):
                    a.wait_ge(maxed, n * NQ + (q + 1))
                    if not (known(n) and n == 0):
                        a.wait_ge(probed, (n - 1) * NQ + (q + 1))
                    for j in range(HQ):
                        ins = a.activation(expd[:, q, j, :], s_ps[:, q % 2, j, :], ACT.Exp,
                                           bias=negmax[:, q, j:j + 1], accum_out=total[:, q, j:j + 1])
                    ins.then_inc(exped, 1)

                def copy_turned(n, b, q):
                    a.wait_ge(turned, n * NQ + (q + 1))
                    if not (known(n) and n == 0):
                        a.wait_ge(mixed, (n - 1) * NQ + (q + 1))
                    a.activation(probT[:, q, :, :], t_ps[:, q % 2, :, :], ACT.Copy).then_inc(probTed, 1)

                for q in range(NQ):
                    copy_values(0, 0, q)

                def body(n, b):
                    for q in range(NQ):
                        at = before(n, b, q, 1)
                        if at:
                            exponentials(*at)
                        if not (known(n) and n + 1 == NB):
                            copy_values(n + 1, 1 - b, q)
                        at = before(n, b, q, 2)
                        if at:
                            copy_turned(*at)

                loops(a, body)
                exponentials(*before(NB, 0, 0, 1))
                for q in range(2):
                    copy_turned(*before(NB, 0, q, 2))

            @block.vector
            def _(v):
                v.wait_ge(last_one, 1)
                ln.vector(v, x, D - 1)
                v.wait_ge(biased, 1)
                v.wait_ge(w_in, 16 * 8)
                v.tensor_tensor(bias_rows[:], o_ps[:, 1, 0:D], bo_rows[:], ALU.add).then_inc(bias_done, 1)
                v.wait_ge(fold_out, 2 * NQ + 1)
                v.wait_ge(filled, 1)

                def copy_keys(n, b, q):
                    v.wait_ge(key_mm, n * NQ + (q + 1))
                    if not (known(n) and n < 2):
                        v.wait_ge(scored, (n - 2) * NQ + (q + 1))
                    heads = slice(HQ * q, HQ * q + HQ)
                    v.tensor_tensor(key[:, b, heads, :], kv_ps[:, 0, :, :],
                                    kbias[:, heads].unsqueeze(2).broadcast_to([P, HQ, T]),
                                    ALU.add).then_inc(keyed, 1)

                def maximum(n, b, q):
                    v.wait_ge(scored, n * NQ + (q + 1))
                    v.memset(tick[:], 0.0)
                    v.copy_predicated(s_ps[:, q % 2, :, :], mask[:, b, :].unsqueeze(1).broadcast_to([P, HQ, T]),
                                      fill[:].unsqueeze(2).broadcast_to([P, HQ, T])).then_inc(masked, 1)
                    v.wait_ge(masked, n * NQ + (q + 1))
                    if not (known(n) and n == 0):
                        v.wait_ge(exped, (n - 1) * NQ + (q + 1))
                    v.tensor_reduce(negmax[:, q, :], s_ps[:, q % 2, :, :], AX.X, ALU.max,
                                    negate=True).then_inc(maxed, 1)

                def invert(n, b, q):
                    v.wait_ge(exped, n * NQ + (q + 1))
                    if not (known(n) and n == 0):
                        v.wait_ge(probed, (n - 1) * NQ + (q + 1))
                    v.reciprocal(rtotal[:, q, :], total[:, q, :]).then_inc(inverted, 1)

                def residual(n, b):
                    v.wait_ge(mixed, (n + 1) * NQ)
                    v.tensor_tensor(x[:, bass.ds(n, 1), :], x[:, bass.ds(n, 1), :],
                                    o_ps[:, bass.ds(b, 1), 0:D], ALU.add).then_inc(x_done, 1)

                for q in range(NQ):
                    copy_keys(0, 0, q)
                v.wait_ge(x_bias, 1)

                def body(n, b):
                    for q in range(NQ):
                        maximum(n, b, q)
                        if not (known(n) and n + 1 == NB):
                            copy_keys(n + 1, 1 - b, q)
                        at = before(n, b, q, 1)
                        if at:
                            invert(*at)
                        if q == 3 and not (known(n) and n == 0):
                            residual(n - 1, 1 - b)

                loops(v, body)
                invert(*before(NB, 0, 0, 1))
                residual(NB - 1, 1)


def experts_layer1(nc, io, keep):
    with ExitStack() as ctx:
        def sb(n, shape, dt=F32):
            return ctx.enter_context(nc.sbuf_tensor(n, shape, dt))

        def sem(n):
            return nc.alloc_semaphore(n)

        x, ident, gate_dram = keep["x"], keep["ident"], keep["gate_dram"]
        xnT = sb("d_xnT", [P, TOK])
        x_hi, x_lo = sb("d_x_hi", [P, TOK], F32R), sb("d_x_lo", [P, TOK], F32R)
        ln = LayerNorm(nc, ctx, "d_ln")
        gate = Gate(nc, ctx, "d_gate")
        zeros = sb("d_zeros", [P, FF])
        expert_no = sb("d_expert_no", [P, E])
        ids = sb("d_ids", [P, NB, 8], U32)
        idf = sb("d_idf", [P, NB, 8])
        share, pick = sb("d_share", [P, NB, 2]), sb("d_pick", [P, NB, E])
        w = sb("d_w", [P, 2, 3, FF])
        w_hi, w_lo = sb("d_w_hi", [P, 2, 3, FF], F32R), sb("d_w_lo", [P, 2, 3, FF], F32R)
        gate_rows = sb("d_gate_rows", [P, 2, TOK])
        gx = sb("d_gx", [P, 2, GT])
        gx_hi, gx_lo = sb("d_gx_hi", [P, 2, GT], F32R), sb("d_gx_lo", [P, 2, GT], F32R)
        relu = sb("d_relu", [P, 2, GT])
        LAG, RING = 3, 8
        inner = sb("d_inner", [P, KF, GT])
        in_hi, in_lo = sb("d_in_hi", [P, RING, GT], F32R), sb("d_in_lo", [P, RING, GT], F32R)
        acc = sb("d_acc", [P, TOK])
        g_ps = ctx.enter_context(nc.psum_tensor("d_g", [P, 2, GT], F32))
        u_ps = ctx.enter_context(nc.psum_tensor("d_u", [P, 2, GT], F32))
        down_ps = ctx.enter_context(nc.psum_tensor("d_down", [P, NG, GT], F32))
        x_hi_done, x_lo_done = sem("d_x_hi_done"), sem("d_x_lo_done")
        numbered = sem("d_numbered")
        w_in = [sem("d_w_in0"), sem("d_w_in1")]
        rows_in = [sem("d_rows_in0"), sem("d_rows_in1")]
        w_hi_done, w_lo_done = sem("d_w_hi_done"), sem("d_w_lo_done")
        gx_done, gx_hi_done, gx_lo_done = sem("d_gx_done"), sem("d_gx_hi_done"), sem("d_gx_lo_done")
        g_mm, u_mm, relued = sem("d_g_mm"), sem("d_u_mm"), sem("d_relued")
        innered, in_hi_done, in_lo_done = sem("d_innered"), sem("d_in_hi_done"), sem("d_in_lo_done")
        downed, acc_done, turned, x_done = sem("d_downed"), sem("d_acc_done"), sem("d_turned"), sem("d_x_done")

        def experts(eng, body):
            body(0, 0)
            body(1, 1)
            with eng.Fori(1, E // 2 - 1) as pair:
                body(pair * 2, 0)
                body(pair * 2 + 1, 1)
            body(E - 2, 0)
            body(E - 1, 1)

        def first(e):
            return isinstance(e, int) and e == 0

        def after(e, b, k):
            if k + 1 < NG:
                return e, b, k + 1
            return None if isinstance(e, int) and e == E - 1 else (e + 1, 1 - b, 0)

        with nc.Block() as block:
            @block.sync
            def _(sp):
                sp.dma_start(gate.wr[:], io["Wr1"]).then_inc(gate.wr_in, 16)

                def load_weights(e, b):
                    one = bass.ds(e, 1)
                    sp.dma_start(w[:, b, 0, :].unsqueeze(1), io["Wg"][one].rearrange("e c f -> c e f")
                                 ).then_inc(w_in[b], 16)
                    sp.dma_start(w[:, b, 1, :].unsqueeze(1), io["Wu"][one].rearrange("e c f -> c e f")
                                 ).then_inc(w_in[b], 16)
                    sp.dma_start(w[:, b, 2, :].rearrange("p (k d) -> p k d", k=KF),
                                 io["Wd"][one].rearrange("e (k p) d -> p (e k) d", p=P)).then_inc(w_in[b], 16)

                def load_rows(e, b):
                    sp.dma_start(gate_rows[:, b, :], gate_dram[bass.ds(e, 1), :].broadcast_to([P, TOK])
                                 ).then_inc(rows_in[b], 16)

                load_weights(0, 0)
                load_weights(1, 1)
                gate.sync_out(sp, gate_dram)
                load_rows(0, 0)
                load_rows(1, 1)

                def refill(e, b):
                    sp.wait_ge(w_lo_done, e + 1)
                    load_weights(e + 2, b)
                    sp.wait_ge(gx_done, (e + 1) * NG)
                    load_rows(e + 2, b)

                with sp.Fori(0, E // 2 - 1) as pair:
                    refill(pair * 2, 0)
                    refill(pair * 2 + 1, 1)

            @block.gpsimd
            def _(g):
                ln.gpsimd(g)
                for e in range(E):
                    g.memset(expert_no[:, e:e + 1], float(e))
                g.memset(zeros[:], 0.0).then_inc(numbered, 1)
                g.wait_ge(numbered, 1)

                def body(e, b):
                    g.wait_ge(w_in[b], e * 24 + (48 - 24 * b))
                    if not (isinstance(e, int) and e < 2):
                        g.wait_ge(downed, (e - 1) * UNITS)
                    split_weights(g, w[:, b, :, :], zeros[:].unsqueeze(1).broadcast_to([P, 3, FF]), w_hi[:, b, :, :], w_lo[:, b, :, :],
                                  w_hi_done, w_lo_done, e + 1)

                experts(g, body)

            @block.tensor
            def _(t):
                for k in range(NG):
                    ln.tensor(t, down_ps[:, 0:2, :], ident[:], k)
                gate.tensor_logits(t, down_ps[:, 2, :], xnT, ln.xnT_done)

                def up(e, b, k):
                    cols = slice(k * GT, k * GT + GT)
                    if k == 0:
                        t.wait_ge(w_lo_done, e + 1)
                    if first(e):
                        t.wait_ge(x_lo_done, k + 1)
                    for c in range(KF):
                        unit, chunk = k * KF + c, slice(c * P, c * P + P)
                        if not (first(e) and unit < 2):
                            t.wait_ge(relued, e * UNITS + (unit - 1))
                        three_passes(t, g_ps[:, c % 2, :], w_hi[:, b, 0, chunk], w_lo[:, b, 0, chunk],
                                     x_hi[:, cols], x_lo[:, cols], True, True).then_inc(g_mm, 1)
                        if first(e) and unit == 0:
                            gate.tensor_turn(t, down_ps[:, 0:2, :], ident[:])
                        if c == 0:
                            t.wait_ge(gx_lo_done, e * NG + (k + 1))
                        if not (first(e) and unit < 2):
                            t.wait_ge(innered, e * UNITS + (unit - 1))
                        three_passes(t, u_ps[:, c % 2, :], w_hi[:, b, 1, chunk], w_lo[:, b, 1, chunk],
                                     gx_hi[:, k % 2, :], gx_lo[:, k % 2, :], True, True).then_inc(u_mm, 1)
                        if unit >= LAG:
                            down(e, b, unit - LAG)
                        elif not first(e):
                            down(e - 1, 1 - b, UNITS + unit - LAG)

                def down(e, b, unit):
                    k, c = unit // KF, unit % KF
                    t.wait_ge(in_lo_done, e * UNITS + (unit + 1))
                    ins = three_passes(t, down_ps[:, k, :], w_hi[:, b, 2, c * P:c * P + P],
                                       w_lo[:, b, 2, c * P:c * P + P],
                                       in_hi[:, unit % RING, :], in_lo[:, unit % RING, :],
                                       first(e) and c == 0, False, skip_group_check=True)
                    ins.then_inc(downed, 1)

                def body(e, b):
                    for k in range(NG):
                        up(e, b, k)

                experts(t, body)
                for unit in range(UNITS - LAG, UNITS):
                    down(E - 1, 1, unit)
                for k in range(NG):
                    t.wait_ge(acc_done, k + 1)
                    if k >= 2:
                        t.wait_ge(x_done, k - 1)
                    for m in range(GB):
                        n = GB * k + m
                        ins = t.transpose(g_ps[:, k % 2, m * T:m * T + T], acc[:, n * T:n * T + T], ident[:])
                    ins.then_inc(turned, 1)

            @block.scalar
            def _(a):
                for k in range(NG):
                    ln.scalar(a, down_ps[:, 0:2, :], xnT, k)
                    cols = slice(k * GT, k * GT + GT)
                    a.wait_ge(ln.xnT_done, k + 1)
                    a.activation(x_hi[:, cols], xnT[:, cols], ACT.Copy).then_inc(x_hi_done, 1)
                gate.scalar_exp(a)
                gate.scalar_turned(a, down_ps[:, 0:2, :])

                def round_inner(e, unit):
                    k, c = unit // KF, unit % KF
                    a.wait_ge(innered, e * UNITS + (unit + 1))
                    if not (first(e) and unit < RING):
                        a.wait_ge(downed, e * UNITS + (unit - RING + 1))
                    a.activation(in_hi[:, unit % RING, :], inner[:, c, :], ACT.Copy).then_inc(in_hi_done, 1)

                def round_rows(e, b, k):
                    a.wait_ge(gx_done, e * NG + (k + 1))
                    if not (first(e) and k < 2):
                        a.wait_ge(u_mm, e * UNITS + (k - 1) * KF)
                    a.activation(gx_hi[:, k % 2, :], gx[:, k % 2, :], ACT.Copy).then_inc(gx_hi_done, 1)

                round_rows(0, 0, 0)

                def body(e, b):
                    for unit in range(UNITS):
                        k, c = unit // KF, unit % KF
                        if c == 2 and after(e, b, k):
                            round_rows(*after(e, b, k))
                        a.wait_ge(g_mm, e * UNITS + (unit + 1))
                        if not (first(e) and unit < 2):
                            a.wait_ge(innered, e * UNITS + (unit - 1))
                        a.activation(relu[:, c % 2, :], g_ps[:, c % 2, :], ACT.Relu).then_inc(relued, 1)
                        if unit:
                            round_inner(e, unit - 1)
                        elif not first(e):
                            round_inner(e - 1, UNITS - 1)

                experts(a, body)
                round_inner(E - 1, UNITS - 1)
                for k in range(NG):
                    a.wait_ge(downed, (E - 1) * UNITS + (k + 1) * KF)
                    a.activation(acc[:, k * GT:k * GT + GT], down_ps[:, k, :], ACT.Copy).then_inc(acc_done, 1)

            @block.vector
            def _(v):
                ln.vector(v, x)
                for k in range(NG):
                    cols = slice(k * GT, k * GT + GT)
                    v.wait_ge(x_hi_done, k + 1)
                    v.tensor_tensor(x_lo[:, cols], xnT[:, cols], x_hi[:, cols].bitcast(F32),
                                    ALU.subtract).then_inc(x_lo_done, 1)
                all_e = [P, NB, E]
                v.wait_ge(gate.logits, 1)
                gate.then(v, v.tensor_copy(gate.logit[:], down_ps[:, 2, 0:NB * E].rearrange("p (n e) -> p n e", e=E)))
                gate.then(v, v.tensor_reduce(gate.total[:], gate.logit[:], AX.X, ALU.max))
                v.tensor_tensor(gate.away[:], gate.logit[:], gate.total[:].unsqueeze(2).broadcast_to(all_e),
                                ALU.subtract).then_inc(gate.away_done, 1)
                v.wait_ge(gate.exped, 1)
                gate.then(v, v.tensor_reduce(gate.total[:], gate.expd[:], AX.X, ALU.add))
                gate.then(v, v.reciprocal(gate.rtotal[:], gate.total[:]))
                gate.then(v, v.tensor_tensor(gate.kept[:], gate.expd[:],
                                             gate.rtotal[:].unsqueeze(2).broadcast_to(all_e), ALU.mult))
                for n in range(NB):
                    ins = v.max(gate.top[:, n, :], gate.kept[:, n, :])
                gate.then(v, ins)
                for n in range(NB):
                    ins = v.max_index(ids[:, n, :], gate.top[:, n, :], gate.kept[:, n, :])
                gate.then(v, ins)
                gate.then(v, v.tensor_copy(idf[:], ids[:]))
                gate.then(v, v.tensor_tensor(gate.total[:], gate.top[:, :, 0], gate.top[:, :, 1], ALU.add))
                gate.then(v, v.tensor_scalar(gate.total[:], gate.total[:], 2.0 ** -23, None, ALU.add))
                gate.then(v, v.reciprocal(gate.rtotal[:], gate.total[:]))
                gate.then(v, v.tensor_tensor(share[:], gate.top[:, :, 0:2],
                                             gate.rtotal[:].unsqueeze(2).broadcast_to([P, NB, 2]), ALU.mult))
                v.wait_ge(numbered, 1)
                numbers = expert_no[:].unsqueeze(1).broadcast_to(all_e)
                for i, (hit, out) in enumerate(((gate.kept, gate.kept), (pick, pick))):
                    gate.then(v, v.tensor_tensor(hit[:], numbers, idf[:, :, i:i + 1].broadcast_to(all_e),
                                                 ALU.is_equal))
                    gate.then(v, v.tensor_tensor(out[:], hit[:], share[:, :, i:i + 1].broadcast_to(all_e),
                                                 ALU.mult))
                v.tensor_tensor(gate.gate[:], gate.kept[:], pick[:], ALU.add).then_inc(gate.gated, 1)

                def gated_rows(e, b, k):
                    cols = slice(k * GT, k * GT + GT)
                    if k == 0:
                        v.wait_ge(rows_in[b], e * 8 + (16 - 8 * b))
                    v.tensor_tensor(gx[:, k % 2, :], xnT[:, cols], gate_rows[:, b, cols],
                                    ALU.mult).then_inc(gx_done, 1)

                def gated_rest(e, b, k):
                    v.wait_ge(gx_hi_done, e * NG + (k + 1))
                    v.tensor_tensor(gx_lo[:, k % 2, :], gx[:, k % 2, :], gx_hi[:, k % 2, :].bitcast(F32),
                                    ALU.subtract).then_inc(gx_lo_done, 1)

                def multiply(e, unit):
                    k, c = unit // KF, unit % KF
                    v.wait_ge(relued, e * UNITS + (unit + 1))
                    v.wait_ge(u_mm, e * UNITS + (unit + 1))
                    if not (first(e) and k < 1):
                        v.wait_ge(in_lo_done, e * UNITS + (unit - KF + 1))
                    v.tensor_tensor(inner[:, c, :], relu[:, c % 2, :], u_ps[:, c % 2, :],
                                    ALU.mult).then_inc(innered, 1)

                def rest_inner(e, unit):
                    k, c = unit // KF, unit % KF
                    v.wait_ge(in_hi_done, e * UNITS + (unit + 1))
                    if not (first(e) and unit < RING):
                        v.wait_ge(downed, e * UNITS + (unit - RING + 1))
                    v.tensor_tensor(in_lo[:, unit % RING, :], inner[:, c, :],
                                    in_hi[:, unit % RING, :].bitcast(F32), ALU.subtract).then_inc(in_lo_done, 1)

                gated_rows(0, 0, 0)
                gated_rest(0, 0, 0)

                def body(e, b):
                    for unit in range(UNITS):
                        k, c = unit // KF, unit % KF
                        multiply(e, unit)
                        if c == 1 and after(e, b, k):
                            gated_rows(*after(e, b, k))
                        if c == 3 and after(e, b, k):
                            gated_rest(*after(e, b, k))
                        if unit:
                            rest_inner(e, unit - 1)
                        elif not first(e):
                            rest_inner(e - 1, UNITS - 1)

                experts(v, body)
                rest_inner(E - 1, UNITS - 1)
                for k in range(NG):
                    v.wait_ge(turned, k + 1)
                    v.tensor_tensor(x[:, GB * k:GB * k + GB, :], x[:, GB * k:GB * k + GB, :],
                                    g_ps[:, k % 2, :].rearrange("p (m d) -> p m d", m=GB),
                                    ALU.add).then_inc(x_done, 1)


def program(nc, io, out):
    with ExitStack() as ctx:
        def sb(n, shape, dt=F32):
            return ctx.enter_context(nc.sbuf_tensor(n, shape, dt))

        keep = {
            "x": sb("x", [P, NB, D]),
            "ctxT": sb("ctxT_sb", [P, TOK]),
            "ident": sb("ident", [P, P]),
            "gate_dram": nc.dram_tensor("gate_rows", (E, TOK), F32, kind="Internal").ap(),
            "v_dram": nc.dram_tensor("v_rows", (NB, T, D), F32, kind="Internal").ap(),
        }
        with nc.cleanup_on_exit(), ExitStack() as first:
            keep["ks"] = first.enter_context(nc.sbuf_tensor("ks", [KS, PIECES, TOK], BF16))
            keep["qs"] = first.enter_context(nc.sbuf_tensor("qs", [KS, PIECES, TOK], BF16))
            with nc.sbuf_tensor("xnT0", [P, TOK], F32) as xnT:
                keep["xnT"] = xnT
                project_layer0(nc, io, keep)
            attend_layer0(nc, io, keep)
        with nc.cleanup_on_exit():
            experts_layer0(nc, io, keep)
        with nc.cleanup_on_exit():
            attend_layer1(nc, io, keep)
        experts_layer1(nc, io, keep)
        store(nc, keep["x"], out)


def store(nc, x, out):
    with nc.semaphore("stored") as stored, nc.Block() as block:
        @block.sync
        def _(sp):
            sp.dma_start(out.rearrange("n t d -> t n d"), x[:]).then_inc(stored, 16)
            sp.wait_ge(stored, 16)


def layouts(a):
    col = lambda v: v.reshape(-1, 1)
    row = lambda v: v.reshape(1, -1)
    by_d = np.arange(D).reshape(PIECES, DH).T.ravel()
    return {
        "x": a["x"],
        "ctxT": a["ctx_1024"].reshape(TOK, D).T,
        "Wq0": a["L0_xattn_Wq"][:, by_d], "Wk0": a["L0_xattn_Wk"][:, by_d], "Wv0": a["L0_xattn_Wv"],
        "Wo0": a["L0_xattn_Wo"][by_d], "bq0": col(a["L0_xattn_bq"][by_d]), "bk0": col(a["L0_xattn_bk"][by_d]),
        "wQ": a["L1_xattn_wQ_w"], "wK": a["L1_xattn_wK_w"], "wV": a["L1_xattn_wV_w"],
        "wO": a["L1_xattn_wOut_w"].T, "bQ": a["L1_xattn_wQ_b"].reshape(H1, DK).T,
        "bK": a["L1_xattn_wK_b"].reshape(H1, DK).T, "bV": a["L1_xattn_wV_b"].reshape(H1, DK).T,
        "bO": row(a["L1_xattn_wOut_b"]), "mask": a["mask_BxSxS2_bf0"],
        "Wr1": a["L1_ffn_Wr"].T, "Wg": a["L1_ffn_Wg"].transpose(0, 2, 1), "Wu": a["L1_ffn_Wu"].transpose(0, 2, 1),
        "Wd": a["L1_ffn_Wd"].transpose(0, 2, 1),
        "Wr0": a["L0_ffn_Wr"], "br0": row(a["L0_ffn_br"]), "W1": a["L0_ffn_W1"], "W2": a["L0_ffn_W2"],
        "b1": a["L0_ffn_b1"].reshape(E, KF, P).transpose(2, 0, 1), "b2": a["L0_ffn_b2"].T,
        "bv0": row(a["L0_xattn_bv"]), "bo0": row(a["L0_xattn_bo"]),
    }


def kernel(**inputs):
    from concourse import bacc
    from concourse.bass_utils import run_bass_kernel_spmd

    nc = bacc.Bacc("TRN2", target_bir_lowering=False, num_devices=1)
    arrays, io = {}, {}
    for name, a in layouts({name: np.asarray(a) for name, a in inputs.items()}).items():
        a = np.ascontiguousarray(a)
        arrays[f"in_{name}_dram"] = a
        io[name] = nc.dram_tensor(f"in_{name}_dram", a.shape, mybir.dt.from_np(a.dtype), kind="ExternalInput").ap()
    out = nc.dram_tensor("out_0_dram", (NB, T, D), F32, kind="ExternalOutput").ap()
    program(nc, io, out)
    r = run_bass_kernel_spmd(nc, [arrays], core_ids=[0])
    return r.results[0]["out_0_dram"]
```

```python
from contextlib import ExitStack

import concourse.bass as bass
import numpy as np
from concourse import mybir

F32 = mybir.dt.float32
F32R = mybir.dt.float32r
BF16 = mybir.dt.bfloat16
U8 = mybir.dt.uint8
U32 = mybir.dt.uint32
ALU = mybir.AluOpType
ACT = mybir.ActivationFunctionType
AX = mybir.AxisListType

P = 128
NB = 16
T = 128
D = 128
TOK = NB * T
GB = 4
NG = NB // GB
GT = GB * T
H = 16
DH = D // H
PIECES = D // DH
RT = T // H
E = 8
EPS = 1e-5


class LayerNorm:

    def __init__(self, nc, ctx, name):
        def sb(n, shape, dt=F32):
            return ctx.enter_context(nc.sbuf_tensor(f"{name}_{n}", shape, dt))

        def sem(n):
            return nc.alloc_semaphore(f"{name}_{n}")

        self.stats = sb("stats", [P, NB, 6])
        self.mv = sb("mv", [P, NB, 2])
        self.var_eps = sb("var_eps", [P, NB])
        self.minus_half = sb("minus_half", [P, NB])
        self.rstd = sb("rstd", [P, NB])
        self.xn = sb("xn", [P, NB, D])
        self.stats_done = sem("stats_done")
        self.mv_done = sem("mv_done")
        self.half_set = sem("half_set")
        self.var_done = sem("var_done")
        self.rstd_done = sem("rstd_done")
        self.xn_done = sem("xn_done")
        self.transposed = sem("transposed")
        self.xnT_done = sem("xnT_done")

    def vector(self, v, x):
        self.statistics(v, x)
        for k in range(NG):
            self.normalise(v, x, k)

    def statistics(self, v, x):
        for n in range(NB):
            v.bn_stats(self.stats[:, n, :], x[:, n, :]).then_inc(self.stats_done, 1)
        for n in range(NB):
            v.wait_ge(self.stats_done, n + 1)
            v.bn_aggr(self.mv[:, n, :], self.stats[:, n, :]).then_inc(self.mv_done, 1)

    def normalise(self, v, x, k):
        v.wait_ge(self.rstd_done, k + 1)
        for n in range(GB * k, GB * k + GB):
            v.tensor_scalar(self.xn[:, n, :], x[:, n, :], self.mv[:, n, 0:1], self.rstd[:, n:n + 1],
                            ALU.subtract, ALU.mult).then_inc(self.xn_done, 1)

    def gpsimd(self, g):
        g.memset(self.minus_half[:], -0.5).then_inc(self.half_set, 1)
        g.wait_ge(self.half_set, 1)
        for k in range(NG):
            g.wait_ge(self.mv_done, GB * (k + 1))
            cols = slice(GB * k, GB * k + GB)
            g.tensor_scalar(self.var_eps[:, cols], self.mv[:, cols, 1], EPS, None,
                            ALU.add).then_inc(self.var_done, 1)
            g.wait_ge(self.var_done, k + 1)
            g.tensor_tensor(self.rstd[:, cols], self.var_eps[:, cols], self.minus_half[:, cols],
                            ALU.pow).then_inc(self.rstd_done, 1)

    def tensor(self, t, psum, ident, k):
        if k >= 2:
            t.wait_ge(self.xnT_done, k - 1)
        for m in range(GB):
            n = GB * k + m
            t.wait_ge(self.xn_done, n + 1)
            ins = t.transpose(psum[:, k % 2, m * T:m * T + T], self.xn[:, n, :], ident)
        ins.then_inc(self.transposed, 1)

    def scalar(self, a, psum, xnT, k):
        a.wait_ge(self.transposed, k + 1)
        a.activation(xnT[:, k * GT:k * GT + GT], psum[:, k % 2, :], ACT.Copy).then_inc(self.xnT_done, 1)


PARTS = 3
K_COPIES = 2 * PARTS - 1
SENT = 16 * (K_COPIES + PARTS + 1)
KS = DH * PARTS * PARTS


def project_layer0(nc, io, keep):
    with ExitStack() as ctx:
        def sb(n, shape, dt=F32):
            return ctx.enter_context(nc.sbuf_tensor(n, shape, dt))

        def sem(n):
            return nc.alloc_semaphore(n)

        wq, wk, wv = sb("p_wq", [P, D]), sb("p_wk", [P, D]), sb("p_wv", [P, D])
        bq, bk = sb("p_bq", [P, 1]), sb("p_bk", [P, 1])
        bv_rows, bo_rows, wo = sb("p_bv_rows", [P, D]), keep["bo_rows"], keep["wo0"]
        kf, qf = sb("p_kf", [P, NG, GT]), sb("p_qf", [P, NG, GT])
        kb, qb, vt = keep["kb"], keep["qb"], keep["vt"]
        tr_ps = ctx.enter_context(nc.psum_tensor("p_tr", [P, 2, GT], F32))
        q_ps = ctx.enter_context(nc.psum_tensor("p_q", [P, 2, GT], F32))
        k_ps = ctx.enter_context(nc.psum_tensor("p_k", [P, 2, GT], F32))
        v_ps = ctx.enter_context(nc.psum_tensor("p_v", [P, 2, GT], F32))
        ln = LayerNorm(nc, ctx, "p_ln")
        x_in, ctx_in, w_in = sem("p_x_in"), sem("p_ctx_in"), sem("p_w_in")
        ident_zero, ident_done = sem("p_ident_zero"), sem("p_ident_done")
        k_mm, v_mm, q_mm = sem("p_k_mm"), sem("p_v_mm"), sem("p_q_mm")
        k_b1, q_b1 = sem("p_k_b1"), sem("p_q_b1")
        k_r1, q_r1 = sem("p_k_r1"), sem("p_q_r1")
        k_b2, q_b2 = sem("p_k_b2"), sem("p_q_b2")
        k_b3, q_b3 = sem("p_k_b3"), sem("p_q_b3")
        v_done = sem("p_v_done")
        rows_zero, next_in = sem("p_rows_zero"), sem("p_next_in")
        x, ctxT, xnT, ident = keep["x"], keep["ctxT"], keep["xnT"], keep["ident"]
        k_dram, q_dram, v_dram = keep["k_dram"], keep["q_dram"], keep["v_dram"]

        with nc.Block() as block:
            @block.sync
            def _(sp):
                sp.dma_start(ctxT[:], io["ctxT"]).then_inc(ctx_in, 16)
                sp.dma_start(wk[:], io["Wk0"]).then_inc(w_in, 16)
                sp.dma_start(wv[:], io["Wv0"]).then_inc(w_in, 16)
                sp.dma_start(wq[:], io["Wq0"]).then_inc(w_in, 16)
                sp.dma_start(bk[:], io["bk0"]).then_inc(w_in, 16)
                sp.dma_start(bq[:], io["bq0"]).then_inc(w_in, 16)
                sp.dma_start(bv_rows[:], io["bv0"].broadcast_to([P, D])).then_inc(w_in, 16)
                sp.dma_start(bo_rows[:], io["bo0"].broadcast_to([P, D])).then_inc(next_in, 16)
                sp.dma_start(wo[:], io["Wo0"]).then_inc(next_in, 16)
                sp.wait_ge(k_b3, 1)
                sp.wait_ge(q_b3, 1)
                sp.wait_ge(v_done, 1)
                send_group(sp, keep, 0)
                sp.wait_ge(rows_zero, 3)
                sp.wait_ge(next_in, 32)
                sp.wait_ge(keep["kqv_out"][0], SENT)
                for n in range(2):
                    load_keys(sp, keep, n, n)
                    load_queries(sp, keep, n, n)
                    load_values(sp, keep, n, n)
                sp.wait_ge(k_b3, 2)
                sp.wait_ge(q_b3, 2)
                sp.wait_ge(v_done, 2)
                send_group(sp, keep, 1)

            @block.gpsimd
            def _(g):
                g.memset(ident[:], 0.0).then_inc(ident_zero, 1)
                g.wait_ge(ident_zero, 1)
                g.affine_select(out=ident[:], in_=ident[:], compare_op=ALU.not_equal, fill=1.0, base=0,
                                pattern=[[-1, P]], channel_multiplier=1).then_inc(ident_done, 1)
                ln.gpsimd(g)
                def last_part(k):
                    cols = slice(k * GT, k * GT + GT)
                    g.wait_ge(k_b2, k + 1)
                    g.tensor_tensor(kb[:, 2, cols], kf[:, k, :], kb[:, 1, cols],
                                    ALU.subtract).then_inc(k_b3, 1)

                for k in range(NG):
                    cols = slice(k * GT, k * GT + GT)
                    g.wait_ge(k_b1, 2 * k + 2)
                    g.tensor_tensor(kf[:, k, :], kf[:, k, :], kb[:, 0, cols],
                                    ALU.subtract).then_inc(k_r1, 1)
                    if k:
                        last_part(k - 1)
                last_part(NG - 1)

            @block.tensor
            def _(t):
                t.wait_ge(ctx_in, 16)
                t.wait_ge(w_in, 16 * 6)
                for k in range(NG):
                    if k >= 2:
                        t.wait_ge(k_b1, 2 * (k - 1))
                    t.matmul(k_ps[:, k % 2, :], wk[:], ctxT[:, k * GT:k * GT + GT],
                             start=True, stop=True).then_inc(k_mm, 1)
                t.wait_ge(ident_done, 1)

                def values(k):
                    if k >= 2:
                        t.wait_ge(v_done, k - 1)
                    for m in range(GB):
                        n = GB * k + m
                        ins = t.matmul(v_ps[:, k % 2, m * T:m * T + T], ctxT[:, n * T:n * T + T], wv[:],
                                       start=True, stop=True)
                    ins.then_inc(v_mm, 1)

                def queries(k):
                    t.wait_ge(ln.xnT_done, k + 1)
                    if k >= 2:
                        t.wait_ge(q_b1, 2 * (k - 1))
                    t.matmul(q_ps[:, k % 2, :], wq[:], xnT[:, k * GT:k * GT + GT],
                             start=True, stop=True).then_inc(q_mm, 1)

                for k in range(NG):
                    ln.tensor(t, tr_ps, ident[:], k)
                    values(k)
                    queries(k)

            @block.scalar
            def _(a):
                a.dma_start(x[:], io["x"].rearrange("n t d -> t n d")).then_inc(x_in, 16)

                def parts(ps, bias, full, hi, mm, b1, k):
                    a.wait_ge(mm, k + 1)
                    a.activation(full[:, k, :], ps[:, k % 2, :], ACT.Identity,
                                 bias=bias[:]).then_inc(b1, 1)
                    a.activation(hi[:, 0, k * GT:k * GT + GT], ps[:, k % 2, :], ACT.Identity,
                                 bias=bias[:]).then_inc(b1, 1)

                def keys(k):
                    parts(k_ps, bk, kf, kb, k_mm, k_b1, k)

                def second_part(k):
                    a.wait_ge(k_r1, k + 1)
                    a.activation(kb[:, 1, k * GT:k * GT + GT], kf[:, k, :], ACT.Copy).then_inc(k_b2, 1)

                keys(0)
                keys(1)
                for k in range(NG):
                    ln.scalar(a, tr_ps, xnT, k)
                    if k < 2:
                        keys(k + 2)
                    parts(q_ps, bq, qf, qb, q_mm, q_b1, k)
                    second_part(k)

            @block.vector
            def _(v):
                v.memset(keep["qn"][:], 0.0).then_inc(rows_zero, 1)
                v.memset(keep["kh"][:], 0.0).then_inc(rows_zero, 1)
                v.memset(keep["val"][:], 0.0).then_inc(rows_zero, 1)
                v.wait_ge(x_in, 16)
                ln.vector(v, x)
                for k in range(NG):
                    v.wait_ge(v_mm, k + 1)
                    v.tensor_tensor(vt[:, GB * k:GB * k + GB, :],
                                    v_ps[:, k % 2, :].rearrange("p (m d) -> p m d", m=GB),
                                    bv_rows[:].unsqueeze(1).broadcast_to([P, GB, D]),
                                    ALU.add).then_inc(v_done, 1)
                    cols = slice(k * GT, k * GT + GT)
                    v.wait_ge(q_b1, 2 * k + 2)
                    v.tensor_tensor(qf[:, k, :], qf[:, k, :], qb[:, 0, cols],
                                    ALU.subtract).then_inc(q_r1, 1)
                    v.wait_ge(q_r1, k + 1)
                    v.tensor_copy(qb[:, 1, cols], qf[:, k, :]).then_inc(q_b2, 1)
                    v.wait_ge(q_b2, k + 1)
                    v.tensor_tensor(qb[:, 2, cols], qf[:, k, :], qb[:, 1, cols],
                                    ALU.subtract).then_inc(q_b3, 1)


def send_group(eng, keep, k):
    batches, cols, done = slice(GB * k, GB * k + GB), slice(k * GT, k * GT + GT), keep["kqv_out"][k]
    for dst, parts, copies in ((keep["k_dram"], keep["kb"], K_COPIES), (keep["q_dram"], keep["qb"], PARTS)):
        for c in range(copies):
            eng.dma_start(dst[batches, c, :, :].rearrange("n f t -> f n t"),
                          parts[:, c % PARTS, cols].rearrange("f (n t) -> f n t", t=T)).then_inc(done, 16)
    eng.dma_start(keep["v_dram"][batches].rearrange("n t d -> t n d"), keep["vt"][:, batches, :]).then_inc(done, 16)


def load_queries(eng, keep, n, b):
    src = keep["q_dram"][bass.ds(n, 1)].rearrange("n c (d l) t -> n (c d) (l t)", d=DH)
    eng.dma_start(keep["qn"][0:KS, b, :, :], src.broadcast_to([PARTS, PARTS * DH, PIECES * T])
                  ).then_inc(keep["q_in"][b], 16)


def load_values(eng, keep, n, b):
    src = keep["v_dram"][bass.ds(n, 1)].rearrange("n (h b) (l d) -> (b l) (n h) d", b=RT, d=DH)
    eng.dma_start(keep["val"][:, b, :, 0:DH], src).then_inc(keep["val_in"][b], 16)


def load_keys(eng, keep, n, b):
    src = keep["k_dram"][bass.ds(n, 1)]
    rolled = bass.AP(tensor=src.tensor, offset=src.offset,
                     ap=[[D * T, PARTS], [PIECES * T, PARTS * DH], [1, PIECES * T]])
    eng.dma_start(keep["kn"][:, b, :, :], rolled).then_inc(keep["k_in"][b], 16)


def attend_layer0(nc, io, keep):
    HT = T // 2
    HJ = PIECES // 2
    with ExitStack() as ctx:
        def sb(n, shape, dt=F32):
            return ctx.enter_context(nc.sbuf_tensor(n, shape, dt))

        def sem(n):
            return nc.alloc_semaphore(n)

        x, ident, kh, kn, qn, val = (keep[name] for name in ("x", "ident", "kh", "kn", "qn", "val"))
        k_in, q_in, val_in = keep["k_in"], keep["q_in"], keep["val_in"]
        wo, bo_rows = keep["wo0"], keep["bo_rows"]
        negmax, identr = sb("a_negmax", [P, 2, HT], F32R), sb("a_identr", [P, P], F32R)
        expd = sb("a_expd", [P, 2, 2, H, HT])
        total = sb("a_total", [P, 2, HT])
        rtotal = sb("a_rtotal", [P, 2, HT])
        prob = sb("a_prob", [P, 2, H, T])
        ot = sb("a_ot", [P, 2, PIECES, 4, RT])
        oT = sb("a_oT", [P, 2, T])
        s_ps = ctx.enter_context(nc.psum_tensor("a_s", [P, 2, H, HT], F32))
        o_ps = ctx.enter_context(nc.psum_tensor("a_o", [P, 2, 4, T], F32))
        y_ps = ctx.enter_context(nc.psum_tensor("a_y", [P, 2, GT], F32))
        biased, identr_done = sem("a_biased"), sem("a_identr_done")
        keyed = sem("a_keyed")
        scored, maxed, shifted, exped = sem("a_scored"), sem("a_maxed"), sem("a_shifted"), sem("a_exped")
        summed, inverted, probed = sem("a_summed"), sem("a_inverted"), sem("a_probed")
        mixed, ot_done, yed, x_done = sem("a_mixed"), sem("a_ot_done"), sem("a_yed"), sem("a_x_done")
        oT_in = [sem("a_oT_in0"), sem("a_oT_in1")]


        def loops(eng, body):
            for n in range(4):
                body(n, n % 2)
            with eng.Fori(2, NB // 2 - 2) as pair:
                body(pair * 2, 0)
                body(pair * 2 + 1, 1)
            for n in range(NB - 4, NB):
                body(n, n % 2)

        def past(n, k):
            return not isinstance(n, int) or n >= k

        with nc.Block() as block:
            @block.sync
            def _(sp):

                def shuffle(n, b):
                    sp.wait_ge(ot_done, n + 1)
                    for r in range(4):
                        sp.dma_start(oT[:, b, r * 32:r * 32 + 32],
                                     ot[32 * r:32 * r + DH, b, :, :, :].rearrange("d j q a -> d j (q a)")
                                     ).then_inc(oT_in[b], 16)

                sp.wait_ge(keyed, 1)
                load_keys(sp, keep, 2, 0)

                def body(n, b):
                    if isinstance(n, int) and n == 1:
                        sp.wait_ge(keep["kqv_out"][1], SENT)
                    if isinstance(n, int) and n == 3:
                        sp.wait_ge(keep["kqv_out"][2], SENT)
                        sp.wait_ge(keep["kqv_out"][3], SENT)
                    if not isinstance(n, int) or n + 3 < NB:
                        sp.wait_ge(keyed, n + 2)
                        load_keys(sp, keep, n + 3, 1 - b)
                    if not isinstance(n, int) or n + 2 < NB:
                        sp.wait_ge(scored, 2 * n + 2)
                        load_queries(sp, keep, n + 2, b)
                    if past(n, 2):
                        shuffle(n - 2, b)
                        load_values(sp, keep, n, b)
                    if isinstance(n, int) and n < 2:
                        send_group(sp, keep, n + 2)

                loops(sp, body)
                shuffle(NB - 2, 0)
                shuffle(NB - 1, 1)

            @block.tensor
            def _(t):
                t.wait_ge(identr_done, 1)

                def scores(n, b, half):
                    t.wait_ge(keyed, n + 1)
                    t.wait_ge(q_in[b], n * 8 + (16 - 8 * b))
                    for h in range(H):
                        cols = slice(RT * h, RT * h + RT)
                        ins = t.matmul(s_ps[:, half, h, :],
                                       kh[:, b, h, :, :],
                                       qn[:, b, half * HJ:half * HJ + HJ, cols],
                                       start=(h % 8 == 0), stop=False, skip_group_check=True)
                    ins.then_inc(scored, 1)

                def shift(n, half):
                    t.wait_ge(maxed, 2 * n + half + 1)
                    for c in range(2):
                        ins = t.matmul(s_ps[:, half, 8 * c:8 * c + 8, :], identr[:],
                                       negmax[:, half, :].unsqueeze(1).broadcast_to([P, 8, HT]),
                                       start=False, stop=True, skip_group_check=True)
                    ins.then_inc(shifted, 1)

                def mix(n, b, half):
                    t.wait_ge(probed, 2 * n + half + 1)
                    if half == 0:
                        t.wait_ge(val_in[b], n * 8 + (16 - 8 * b))
                        if past(n, 2):
                            t.wait_ge(ot_done, n - 1)
                    cols = slice(half * HT, half * HT + HT)
                    for q in range(4):
                        for r in range(4):
                            ins = t.matmul(o_ps[32 * r:32 * r + 32, b, q, cols], val[:, b, 4 * r + q, :],
                                           prob[:, b, 4 * r + q, cols], start=True, stop=True)
                    ins.then_inc(mixed, 1)

                def project(n, b):
                    t.wait_ge(oT_in[b], n * 32 + (64 - 32 * b))
                    if past(n, 2):
                        t.wait_ge(x_done, n - 1)
                    t.matmul(y_ps[:, b, 0:D], oT[:, b, :], wo[:], start=True, stop=True).then_inc(yed, 1)

                scores(0, 0, 0)
                scores(0, 0, 1)

                def body(n, b):
                    for half in range(2):
                        shift(n, half)
                        if past(n, 1):
                            mix(n - 1, 1 - b, half)
                        if not isinstance(n, int) or n + 1 < NB:
                            t.wait_ge(exped, 2 * n + half + 1)
                            scores(n + 1, 1 - b, half)
                    if past(n, 3):
                        project(n - 3, 1 - b)

                loops(t, body)
                mix(NB - 1, 1, 0)
                mix(NB - 1, 1, 1)
                for n in range(NB - 3, NB):
                    project(n, n % 2)

            @block.vector
            def _(v):
                def maximum(n, half):
                    v.wait_ge(scored, 2 * n + half + 1)
                    if past(n, 1):
                        v.wait_ge(shifted, 2 * n + half - 1)
                    v.tensor_reduce(negmax[:, half, :], s_ps[:, half, :, :].rearrange("p h t -> p t h"),
                                    AX.X, ALU.max, negate=True).then_inc(maxed, 1)

                def totals(n, b, half):
                    v.wait_ge(exped, 2 * n + half + 1)
                    if past(n, 1):
                        v.wait_ge(probed, 2 * n + half - 1)
                    v.tensor_reduce(total[:, half, :], expd[:, b, half, :, :].rearrange("p h t -> p t h"),
                                    AX.X, ALU.add).then_inc(summed, 1)
                    v.wait_ge(summed, 2 * n + half + 1)
                    v.reciprocal(rtotal[:, half, :], total[:, half, :]).then_inc(inverted, 1)

                def residual(n, b):
                    v.wait_ge(yed, n + 1)
                    v.tensor_tensor(x[:, bass.ds(n, 1), :], x[:, bass.ds(n, 1), :],
                                    y_ps[:, bass.ds(b, 1), 0:D], ALU.add).then_inc(x_done, 1)

                def body(n, b):
                    maximum(n, 0)
                    if past(n, 1):
                        totals(n - 1, 1 - b, 1)
                    maximum(n, 1)
                    totals(n, b, 0)
                    if past(n, 4):
                        residual(n - 4, b)

                v.wait_ge(biased, 1)
                loops(v, body)
                totals(NB - 1, 1, 1)
                for n in range(NB - 4, NB):
                    residual(n, n % 2)

            @block.scalar
            def _(a):
                def exponentials(n, b, half):
                    a.wait_ge(shifted, 2 * n + half + 1)
                    if past(n, 2):
                        a.wait_ge(probed, 2 * n + half - 3)
                    a.activation(expd[:, b, half, :, :], s_ps[:, half, :, :], ACT.Exp,
                                 scale=float(D) ** -0.5).then_inc(exped, 1)

                def copy_out(n, b):
                    a.wait_ge(mixed, 2 * n + 2)
                    if past(n, 2):
                        a.wait_ge(yed, n - 1)
                    a.activation(ot[:, b, :, :, :].rearrange("p j q a -> p q j a"),
                                 o_ps[:, b, :, :].rearrange("p q (j a) -> p q j a", a=RT),
                                 ACT.Copy).then_inc(ot_done, 1)

                def arrange_keys(n, b):
                    a.wait_ge(k_in[b], n * 8 + (16 - 8 * b))
                    if past(n, 2):
                        a.wait_ge(scored, 2 * n - 2)
                    a.activation(kh[0:KS, b, :, :, :],
                                 kn[:, b, :, :].rearrange("k l (h b) -> k h b l", b=RT),
                                 ACT.Copy).then_inc(keyed, 1)

                a.activation(identr[:], ident[:], ACT.Copy).then_inc(identr_done, 1)
                arrange_keys(0, 0)
                arrange_keys(1, 1)

                def body(n, b):
                    exponentials(n, b, 0)
                    if past(n, 2):
                        copy_out(n - 2, b)
                    exponentials(n, b, 1)
                    if not isinstance(n, int) or n + 2 < NB:
                        arrange_keys(n + 2, b)

                loops(a, body)
                copy_out(NB - 2, 0)
                copy_out(NB - 1, 1)

            @block.gpsimd
            def _(g):
                g.tensor_tensor(x[:], x[:], bo_rows[:].unsqueeze(1).broadcast_to([P, NB, D]),
                                ALU.add).then_inc(biased, 1)

                def probabilities(n, b, half):
                    g.wait_ge(inverted, 2 * n + half + 1)
                    if past(n, 2):
                        g.wait_ge(mixed, 2 * n + half - 3)
                    g.tensor_tensor(prob[:, b, :, half * HT:half * HT + HT], expd[:, b, half, :, :],
                                    rtotal[:, half, :].unsqueeze(1).broadcast_to([P, H, HT]),
                                    ALU.mult).then_inc(probed, 1)

                def body(n, b):
                    probabilities(n, b, 0)
                    probabilities(n, b, 1)

                loops(g, body)


class Gate:

    def __init__(self, nc, ctx, name):
        def sb(n, shape, dt=F32):
            return ctx.enter_context(nc.sbuf_tensor(f"{name}_{n}", shape, dt))

        def sem(n):
            return nc.alloc_semaphore(f"{name}_{n}")

        self.wr = sb("wr", [P, E])
        self.logit = sb("logit", [P, NB, E])
        self.top = sb("top", [P, NB, 8])
        self.away = sb("away", [P, NB, E])
        self.expd = sb("expd", [P, NB, E])
        self.kept = sb("kept", [P, NB, E])
        self.total = sb("total", [P, NB])
        self.rtotal = sb("rtotal", [P, NB])
        self.gate = sb("gate", [P, NB, E])
        self.gateT = sb("gateT", [E, TOK])
        self.wr_in, self.logits, self.away_done = sem("wr_in"), sem("logits"), sem("away_done")
        self.exped, self.gated, self.turned = sem("exped"), sem("gated"), sem("turned")
        self.gateT_done, self.gateT_out, self.step = sem("gateT_done"), sem("gateT_out"), sem("step")
        self.steps = 0

    def then(self, v, ins):
        self.steps += 1
        ins.then_inc(self.step, 1)
        v.wait_ge(self.step, self.steps)

    def tensor_logits(self, t, psum, xnT, xnT_done):
        t.wait_ge(self.wr_in, 16)
        for n in range(NB):
            t.wait_ge(xnT_done, n // GB + 1)
            ins = t.matmul(psum[:, n * E:n * E + E], xnT[:, n * T:n * T + T], self.wr[:],
                           start=True, stop=True)
        ins.then_inc(self.logits, 1)

    def tensor_turn(self, t, psum, ident):
        t.wait_ge(self.gated, 1)
        for k in range(NG):
            if k >= 2:
                t.wait_ge(self.gateT_done, k - 1)
            for m in range(GB):
                ins = t.transpose(psum[0:E, k % 2, m * T:m * T + T], self.gate[:, GB * k + m, :], ident)
            ins.then_inc(self.turned, 1)

    def scalar_exp(self, a):
        a.wait_ge(self.away_done, 1)
        a.activation(self.expd[:], self.away[:], ACT.Exp).then_inc(self.exped, 1)

    def scalar_turned(self, a, psum):
        for k in range(NG):
            a.wait_ge(self.turned, k + 1)
            a.activation(self.gateT[:, k * GT:k * GT + GT], psum[0:E, k % 2, :],
                         ACT.Copy).then_inc(self.gateT_done, 1)

    def sync_out(self, sp, gate_dram):
        sp.wait_ge(self.gateT_done, NG)
        sp.dma_start(gate_dram, self.gateT[:]).then_inc(self.gateT_out, 16)
        sp.wait_ge(self.gateT_out, 16)


def split_weights(eng, raw, zeros, hi, lo, hi_done, lo_done, count):
    eng.tensor_tensor(hi, raw, zeros, ALU.add).then_inc(hi_done, 1)
    eng.wait_ge(hi_done, count)
    eng.tensor_tensor(lo, raw, hi.bitcast(F32), ALU.subtract).then_inc(lo_done, 1)


def three_passes(t, out, w_hi, w_lo, x_hi, x_lo, start, stop, **kw):
    t.matmul(out, w_hi, x_hi, start=start, stop=False, **kw)
    t.matmul(out, w_hi, x_lo, start=False, stop=False, **kw)
    return t.matmul(out, w_lo, x_hi, start=False, stop=stop, **kw)


FF = 512
KF = FF // P
UNITS = NG * KF


def experts_layer0(nc, io, keep):
    with ExitStack() as ctx:
        def sb(n, shape, dt=F32):
            return ctx.enter_context(nc.sbuf_tensor(n, shape, dt))

        def sem(n):
            return nc.alloc_semaphore(n)

        x, ident, gate_dram = keep["x"], keep["ident"], keep["gate_dram"]
        xnT = sb("b_xnT", [P, TOK])
        x_hi, x_lo = sb("b_x_hi", [P, TOK], F32R), sb("b_x_lo", [P, TOK], F32R)
        ln = LayerNorm(nc, ctx, "b_ln")
        gate = Gate(nc, ctx, "b_gate")
        br_rows = sb("b_br_rows", [P, E])
        zeros, zeroed = sb("b_zeros", [P, FF]), sem("b_zeroed")
        b1, b2, b1_now = sb("b_b1", [P, E, KF]), sb("b_b2", [P, E]), sb("b_b1_now", [P, 2, KF])
        w1, w2 = sb("b_w1", [P, 2, FF]), sb("b_w2", [P, 2, KF, D])
        w1_hi, w1_lo = sb("b_w1_hi", [P, 2, FF], F32R), sb("b_w1_lo", [P, 2, FF], F32R)
        w2_hi, w2_lo = sb("b_w2_hi", [P, 2, KF, D], F32R), sb("b_w2_lo", [P, 2, KF, D], F32R)
        inner = sb("b_inner", [P, 2, KF, GT])
        in_hi, in_lo = sb("b_in_hi", [P, 2, KF, GT], F32R), sb("b_in_lo", [P, 2, KF, GT], F32R)
        gate_rows = sb("b_gate_rows", [P, 2, TOK])
        part = sb("b_part", [P, 2, GT])
        acc = sb("b_acc", [P, TOK])
        up_ps = ctx.enter_context(nc.psum_tensor("b_up", [P, KF, GT], F32))
        down_ps = ctx.enter_context(nc.psum_tensor("b_down", [P, 2, GT], F32))
        tr_ps = ctx.enter_context(nc.psum_tensor("b_tr", [P, 2, GT], F32))
        small_in, b1_set = sem("b_small_in"), sem("b_b1_set")
        x_hi_done, x_lo_done = sem("b_x_hi_done"), sem("b_x_lo_done")
        w_in = [sem("b_w_in0"), sem("b_w_in1")]
        rows_in = [sem("b_rows_in0"), sem("b_rows_in1")]
        w1_hi_done, w1_lo_done = sem("b_w1_hi_done"), sem("b_w1_lo_done")
        w2_hi_done, w2_lo_done = sem("b_w2_hi_done"), sem("b_w2_lo_done")
        upped, innered, in_hi_done, in_lo_done = (sem("b_upped"), sem("b_innered"), sem("b_in_hi_done"),
                                                  sem("b_in_lo_done"))
        downed, parted, acced = sem("b_downed"), sem("b_parted"), sem("b_acced")
        turned, x_done = sem("b_turned"), sem("b_x_done")

        def experts(eng, body):
            body(0, 0)
            body(1, 1)
            with eng.Fori(1, E // 2) as pair:
                body(pair * 2, 0)
                body(pair * 2 + 1, 1)

        def first(e):
            return isinstance(e, int) and e == 0

        with nc.Block() as block:
            @block.sync
            def _(sp):
                sp.dma_start(gate.wr[:], io["Wr0"]).then_inc(gate.wr_in, 16)
                sp.dma_start(br_rows[:], io["br0"].broadcast_to([P, E])).then_inc(small_in, 16)
                sp.dma_start(b1[:], io["b1"]).then_inc(small_in, 16)
                sp.dma_start(b2[:], io["b2"]).then_inc(small_in, 16)

                def load_weights(e, b):
                    sp.dma_start(w1[:, b, :].unsqueeze(1), io["W1"][bass.ds(e, 1)].rearrange("e c f -> c e f")
                                 ).then_inc(w_in[b], 16)
                    sp.dma_start(w2[:, b, :, :], io["W2"][bass.ds(e, 1)].rearrange("e (k p) d -> p (e k) d", p=P)
                                 ).then_inc(w_in[b], 16)

                def load_rows(e, b):
                    sp.dma_start(gate_rows[:, b, :], gate_dram[bass.ds(e, 1), :].broadcast_to([P, TOK])
                                 ).then_inc(rows_in[b], 16)

                load_weights(0, 0)
                load_weights(1, 1)
                gate.sync_out(sp, gate_dram)
                load_rows(0, 0)
                load_rows(1, 1)

                def refill(e, b):
                    sp.wait_ge(w2_lo_done, e + 1)
                    load_weights(e + 2, b)
                    sp.wait_ge(parted, (e + 1) * NG)
                    load_rows(e + 2, b)

                with sp.Fori(0, E // 2 - 1) as pair:
                    refill(pair * 2, 0)
                    refill(pair * 2 + 1, 1)

            @block.gpsimd
            def _(g):
                ln.gpsimd(g)
                g.memset(zeros[:], 0.0).then_inc(zeroed, 1)
                g.wait_ge(zeroed, 1)

                def body(e, b):
                    g.wait_ge(w_in[b], e * 16 + (32 - 16 * b))
                    if not (isinstance(e, int) and e < 2):
                        g.wait_ge(downed, (e - 1) * NG)
                    split_weights(g, w1[:, b, :], zeros[:], w1_hi[:, b, :], w1_lo[:, b, :],
                                  w1_hi_done, w1_lo_done, e + 1)
                    split_weights(g, w2[:, b, :, :], zeros[:].rearrange("p (k d) -> p k d", k=KF), w2_hi[:, b, :, :], w2_lo[:, b, :, :],
                                  w2_hi_done, w2_lo_done, e + 1)

                experts(g, body)

            @block.tensor
            def _(t):
                for k in range(NG):
                    ln.tensor(t, tr_ps, ident[:], k)
                gate.tensor_logits(t, down_ps[:, 0, :], xnT, ln.xnT_done)

                def up(e, b, k):
                    if k == 0:
                        t.wait_ge(w1_lo_done, e + 1)
                    if first(e):
                        t.wait_ge(x_lo_done, k + 1)
                    for c in range(KF):
                        if not (first(e) and k == 0):
                            t.wait_ge(innered, e * UNITS + (k * KF + c - KF + 1))
                        cols = slice(k * GT, k * GT + GT)
                        chunk = slice(c * P, c * P + P)
                        three_passes(t, up_ps[:, c, :], w1_hi[:, b, chunk], w1_lo[:, b, chunk],
                                     x_hi[:, cols], x_lo[:, cols], True, True).then_inc(upped, 1)

                def down(e, b, k):
                    if k == 0:
                        t.wait_ge(w2_lo_done, e + 1)
                    if not (first(e) and k < 2):
                        t.wait_ge(parted, e * NG + (k - 1))
                    for c in range(KF):
                        t.wait_ge(in_lo_done, e * UNITS + (k * KF + c + 1))
                        ins = three_passes(t, down_ps[:, k % 2, :], w2_hi[:, b, c, :], w2_lo[:, b, c, :],
                                           in_hi[:, k % 2, c, :], in_lo[:, k % 2, c, :],
                                           c == 0, c == KF - 1)
                    ins.then_inc(downed, 1)

                def body(e, b):
                    for k in range(NG):
                        up(e, b, k)
                        if k:
                            down(e, b, k - 1)
                        elif not first(e):
                            down(e - 1, 1 - b, NG - 1)
                        else:
                            gate.tensor_turn(t, tr_ps, ident[:])

                experts(t, body)
                down(E - 1, 1, NG - 1)
                for k in range(NG):
                    t.wait_ge(acced, (E - 1) * NG + k + 1)
                    if k >= 2:
                        t.wait_ge(x_done, k - 1)
                    for m in range(GB):
                        n = GB * k + m
                        ins = t.transpose(tr_ps[:, k % 2, m * T:m * T + T], acc[:, n * T:n * T + T], ident[:])
                    ins.then_inc(turned, 1)

            @block.scalar
            def _(a):
                for k in range(NG):
                    ln.scalar(a, tr_ps, xnT, k)
                    cols = slice(k * GT, k * GT + GT)
                    a.wait_ge(ln.xnT_done, k + 1)
                    a.activation(x_hi[:, cols], xnT[:, cols], ACT.Copy).then_inc(x_hi_done, 1)
                gate.scalar_exp(a)

                def round_inner(e, unit):
                    k, c = unit // KF, unit % KF
                    a.wait_ge(innered, e * UNITS + (unit + 1))
                    if not (first(e) and k < 2):
                        a.wait_ge(downed, e * NG + (k - 1))
                    a.activation(in_hi[:, k % 2, c, :], inner[:, k % 2, c, :], ACT.Copy).then_inc(in_hi_done, 1)

                a.wait_ge(small_in, 48)

                def body(e, b):
                    a.activation(b1_now[:, b, :].unsqueeze(1), b1[:, bass.ds(e, 1), :], ACT.Copy).then_inc(b1_set, 1)
                    a.wait_ge(b1_set, e + 1)
                    for unit in range(UNITS):
                        k, c = unit // KF, unit % KF
                        a.wait_ge(upped, e * UNITS + (unit + 1))
                        if not (first(e) and k < 2):
                            a.wait_ge(in_lo_done, e * UNITS + (unit - 2 * KF + 1))
                        a.activation(inner[:, k % 2, c, :], up_ps[:, c, :], ACT.Gelu,
                                     bias=b1_now[:, b, c:c + 1]).then_inc(innered, 1)
                        if unit:
                            round_inner(e, unit - 1)
                        if first(e) and unit == KF - 1:
                            gate.scalar_turned(a, tr_ps)
                    round_inner(e, UNITS - 1)

                experts(a, body)

            @block.vector
            def _(v):
                ln.vector(v, x)
                for k in range(NG):
                    cols = slice(k * GT, k * GT + GT)
                    v.wait_ge(x_hi_done, k + 1)
                    v.tensor_tensor(x_lo[:, cols], xnT[:, cols], x_hi[:, cols].bitcast(F32),
                                    ALU.subtract).then_inc(x_lo_done, 1)
                v.wait_ge(small_in, 48)
                v.wait_ge(gate.logits, 1)
                gate.then(v, v.tensor_tensor(gate.logit[:], down_ps[:, 0, 0:NB * E].rearrange("p (n e) -> p n e", e=E),
                                             br_rows[:].unsqueeze(1).broadcast_to([P, NB, E]), ALU.add))
                for n in range(NB):
                    ins = v.max(gate.top[:, n, :], gate.logit[:, n, :])
                gate.then(v, ins)
                v.tensor_tensor(gate.away[:], gate.logit[:], gate.top[:, :, 0:1].broadcast_to([P, NB, E]),
                                ALU.subtract).then_inc(gate.away_done, 1)
                gate.then(v, v.tensor_tensor(gate.kept[:], gate.logit[:],
                                             gate.top[:, :, 1:2].broadcast_to([P, NB, E]), ALU.is_ge))
                v.wait_ge(gate.exped, 1)
                gate.then(v, v.tensor_tensor(gate.kept[:], gate.kept[:], gate.expd[:], ALU.mult))
                gate.then(v, v.tensor_reduce(gate.total[:], gate.kept[:], AX.X, ALU.add))
                gate.then(v, v.reciprocal(gate.rtotal[:], gate.total[:]))
                v.tensor_tensor(gate.gate[:], gate.kept[:], gate.rtotal[:].unsqueeze(2).broadcast_to([P, NB, E]),
                                ALU.mult).then_inc(gate.gated, 1)

                def rest_inner(e, unit):
                    k, c = unit // KF, unit % KF
                    v.wait_ge(in_hi_done, e * UNITS + (unit + 1))
                    if not (first(e) and k < 2):
                        v.wait_ge(downed, e * NG + (k - 1))
                    v.tensor_tensor(in_lo[:, k % 2, c, :], inner[:, k % 2, c, :],
                                    in_hi[:, k % 2, c, :].bitcast(F32), ALU.subtract).then_inc(in_lo_done, 1)

                def weigh(e, b, k):
                    cols = slice(k * GT, k * GT + GT)
                    if k == 0:
                        v.wait_ge(rows_in[b], e * 8 + (16 - 8 * b))
                    v.wait_ge(downed, e * NG + (k + 1))
                    if first(e):
                        v.scalar_tensor_tensor(acc[:, cols], down_ps[:, k % 2, :], b2[:, 0:1],
                                               gate_rows[:, b, cols], ALU.add, ALU.mult).then_inc(parted, 1)
                        v.wait_ge(parted, k + 1)
                        v.engine_nop().then_inc(acced, 1)
                        return
                    v.scalar_tensor_tensor(part[:, k % 2, :], down_ps[:, k % 2, :], b2[:, bass.ds(e, 1)],
                                           gate_rows[:, b, cols], ALU.add, ALU.mult).then_inc(parted, 1)
                    v.wait_ge(parted, e * NG + (k + 1))
                    v.wait_ge(acced, (e - 1) * NG + (k + 1))
                    v.tensor_tensor(acc[:, cols], acc[:, cols], part[:, k % 2, :], ALU.add).then_inc(acced, 1)

                def body(e, b):
                    for k in range(NG):
                        for c in range(KF):
                            rest_inner(e, k * KF + c)
                        if k:
                            weigh(e, b, k - 1)
                        elif not first(e):
                            weigh(e - 1, 1 - b, NG - 1)

                experts(v, body)
                weigh(E - 1, 1, NG - 1)
                for k in range(NG):
                    v.wait_ge(turned, k + 1)
                    v.tensor_tensor(x[:, GB * k:GB * k + GB, :], x[:, GB * k:GB * k + GB, :],
                                    tr_ps[:, k % 2, :].rearrange("p (m d) -> p m d", m=GB),
                                    ALU.add).then_inc(x_done, 1)


H1, DK = 16, 64
HD = H1 * DK
NC = HD // P
HQ = 4
NQ = H1 // HQ


def head(q, j):
    return 2 * HQ * (q // 2) + 2 * j + q % 2


def project_layer1(nc, io, keep):
    with ExitStack() as ctx:
        def sb(n, shape, dt=F32):
            return ctx.enter_context(nc.sbuf_tensor(n, shape, dt))

        def sem(n):
            return nc.alloc_semaphore(n)

        x, ident, kT, qT = (keep[name] for name in ("x", "ident", "kT", "qT"))
        wv_hi, wv_lo, wo = keep["wv_hi"], keep["wv_lo"], keep["wo1"]
        ctxT, ctx_in = sb("c_ctxT", [P, TOK]), [sem(f"c_ctx_in{k}") for k in range(NG)]
        ln = LayerNorm(nc, ctx, "c_ln")
        wk, wq, wv = sb("c_wk", [P, HD]), sb("c_wq", [P, HD]), sb("c_wv", [P, HD])
        wk_hi, wk_lo = sb("c_wk_hi", [P, HD], F32R), sb("c_wk_lo", [P, HD], F32R)
        wq_hi, wq_lo = sb("c_wq_hi", [P, HD], F32R), sb("c_wq_lo", [P, HD], F32R)
        bq, bk, bv, bq8 = sb("c_bq", [P, NC]), sb("c_bk", [P, NC]), sb("c_bv", [P, NC]), sb("c_bq8", [P, NC])
        bo_rows, bias_rows = sb("c_bo_rows", [P, D]), sb("c_bias_rows", [P, D])
        hi, lo = sb("c_hi", [P, 2, GT], F32R), sb("c_lo", [P, 2, GT], F32R)
        tr_ps = ctx.enter_context(nc.psum_tensor("c_tr", [P, 2, GT], F32))
        out_ps = ctx.enter_context(nc.psum_tensor("c_out", [P, 4, GT], F32))
        bias_ps = ctx.enter_context(nc.psum_tensor("c_bias", [P, GT], F32))
        wk_in, w_in = sem("c_wk_in"), sem("c_w_in")
        wk_hi_done, wk_lo_done = sem("c_wk_hi_done"), sem("c_wk_lo_done")
        wq_hi_done, wq_lo_done = sem("c_wq_hi_done"), sem("c_wq_lo_done")
        wv_hi_done, wv_lo_done = sem("c_wv_hi_done"), sem("c_wv_lo_done")
        bq8_done = sem("c_bq8_done")
        hi_done, lo_done, group_mm, unit_mm = sem("c_hi_done"), sem("c_lo_done"), sem("c_group_mm"), sem("c_unit_mm")
        odd_out, even_out = sem("c_odd_out"), sem("c_even_out")
        biased, bias_done, x_bias = sem("c_biased"), sem("c_bias_done"), sem("c_x_bias")

        def units(i):
            return [(i * NC + m, m) for m in range(NC)]

        def target(i, m):
            return (kT if i < NG else qT)[:, m, i % NG * GT:i % NG * GT + GT]

        with nc.Block() as block:
            @block.sync
            def _(sp):
                def load_ctx(k):
                    cols = slice(k * GT, k * GT + GT)
                    sp.dma_start(ctxT[:, cols], io["ctxT"][:, cols]).then_inc(ctx_in[k], 16)

                sp.dma_start(wk[:], io["wK"]).then_inc(wk_in, 16)
                load_ctx(0)
                load_ctx(1)
                for dst, src in ((wq, "wQ"), (bq, "bQ"), (bk, "bK"), (bv, "bV"), (wv, "wV")):
                    sp.dma_start(dst[:], io[src]).then_inc(w_in, 16)
                sp.dma_start(wo[:], io["wO"].rearrange("(m p) o -> p m o", p=P)).then_inc(w_in, 16)
                sp.dma_start(bo_rows[:], io["bO"].broadcast_to([P, D])).then_inc(w_in, 16)
                load_ctx(2)
                load_ctx(3)

            @block.gpsimd
            def _(g):
                g.wait_ge(wk_hi_done, 1)
                g.tensor_tensor(wk_lo[:], wk[:], wk_hi[:].bitcast(F32), ALU.subtract).then_inc(wk_lo_done, 1)
                ln.gpsimd(g)
                g.wait_ge(wq_hi_done, 1)
                g.tensor_tensor(wq_lo[:], wq[:], wq_hi[:].bitcast(F32), ALU.subtract).then_inc(wq_lo_done, 1)
                g.wait_ge(wv_hi_done, 1)
                g.tensor_tensor(wv_lo[:], wv[:], wv_hi[:].bitcast(F32), ALU.subtract).then_inc(wv_lo_done, 1)
                g.wait_ge(ln.xn_done, NB)
                g.wait_ge(bias_done, 1)
                g.tensor_tensor(x[:], x[:], bias_rows[:].unsqueeze(1).broadcast_to([P, NB, D]),
                                ALU.add).then_inc(x_bias, 1)

            @block.tensor
            def _(t):
                def group(i):
                    w_hi, w_lo = (wk_hi, wk_lo) if i < NG else (wq_hi, wq_lo)
                    if i == 0:
                        t.wait_ge(wk_lo_done, 1)
                    if i == NG:
                        t.wait_ge(wq_lo_done, 1)
                    t.wait_ge(lo_done, i + 1)
                    for u, m in units(i):
                        if u >= 4:
                            t.wait_ge(odd_out if u % 2 else even_out, (u - 4) // 2 + 1)
                        chunk = slice(m * P, m * P + P)
                        three_passes(t, out_ps[:, u % 4, :], w_hi[:, chunk], w_lo[:, chunk],
                                     hi[:, i % 2, :], lo[:, i % 2, :], True, True).then_inc(unit_mm, 1)

                def turn(k):
                    if k >= 2:
                        t.wait_ge(lo_done, NG + k - 1)
                    for m in range(GB):
                        n = GB * k + m
                        t.wait_ge(ln.xn_done, n + 1)
                        ins = t.transpose(tr_ps[:, k % 2, m * T:m * T + T], ln.xn[:, n, :], ident[:])
                    ins.then_inc(ln.transposed, 1)

                group(0)
                group(1)
                t.wait_ge(w_in, 16 * 7)
                for m in range(NC):
                    ins = t.matmul(bias_ps[:, 0:D], bv[:, m:m + 1].broadcast_to([P, P]), wo[:, m, :],
                                   start=(m == 0), stop=(m == NC - 1))
                ins.then_inc(biased, 1)
                for k in range(NG):
                    if k < 2:
                        group(k + 2)
                    turn(k)
                    if k:
                        group(NG + k - 1)
                group(2 * NG - 1)

            @block.scalar
            def _(a):
                a.wait_ge(wk_in, 16)
                a.activation(wk_hi[:], wk[:], ACT.Copy).then_inc(wk_hi_done, 1)

                def round_group(i):
                    if i >= 2:
                        a.wait_ge(unit_mm, (i - 1) * NC)
                    if i < NG:
                        a.wait_ge(ctx_in[i], 16)
                        src = ctxT[:, i * GT:i * GT + GT]
                    else:
                        a.wait_ge(ln.transposed, i - NG + 1)
                        src = tr_ps[:, i % 2, :]
                    a.activation(hi[:, i % 2, :], src, ACT.Copy).then_inc(hi_done, 1)

                def odd_units(i):
                    for u, m in units(i)[1::2]:
                        a.wait_ge(unit_mm, u + 1)
                        if i < NG:
                            a.activation(target(i, m), out_ps[:, u % 4, :], ACT.Identity,
                                         bias=bk[:, m:m + 1]).then_inc(odd_out, 1)
                        else:
                            a.activation(target(i, m), out_ps[:, u % 4, :], ACT.Identity, bias=bq8[:, m:m + 1],
                                         scale=float(DK) ** -0.5).then_inc(odd_out, 1)

                round_group(0)
                round_group(1)
                a.wait_ge(w_in, 16 * 7)
                a.activation(wq_hi[:], wq[:], ACT.Copy).then_inc(wq_hi_done, 1)
                a.activation(wv_hi[:], wv[:], ACT.Copy).then_inc(wv_hi_done, 1)
                a.activation(bq8[:], bq[:], ACT.Copy, scale=float(DK) ** -0.5).then_inc(bq8_done, 1)
                a.wait_ge(bq8_done, 1)
                for i in range(2 * NG):
                    odd_units(i)
                    if i + 2 < 2 * NG:
                        round_group(i + 2)

            @block.vector
            def _(v):
                def rest_group(i):
                    src = ctxT[:, i * GT:i * GT + GT] if i < NG else tr_ps[:, i % 2, :]
                    v.wait_ge(hi_done, i + 1)
                    v.tensor_tensor(lo[:, i % 2, :], src, hi[:, i % 2, :].bitcast(F32),
                                    ALU.subtract).then_inc(lo_done, 1)

                def even_units(i):
                    for u, m in units(i)[0::2]:
                        v.wait_ge(unit_mm, u + 1)
                        if i < NG:
                            v.tensor_scalar(target(i, m), out_ps[:, u % 4, :], bk[:, m:m + 1], None,
                                            ALU.add).then_inc(even_out, 1)
                        else:
                            v.tensor_scalar(target(i, m), out_ps[:, u % 4, :], bq[:, m:m + 1], float(DK) ** -0.5,
                                            ALU.add, ALU.mult).then_inc(even_out, 1)

                ln.statistics(v, x)
                rest_group(0)
                rest_group(1)
                v.wait_ge(w_in, 16 * 7)
                for i in range(2 * NG):
                    even_units(i)
                    if i < NG:
                        ln.normalise(v, x, i)
                    if i == 1:
                        v.wait_ge(biased, 1)
                        v.tensor_tensor(bias_rows[:], bias_ps[:, 0:D], bo_rows[:], ALU.add).then_inc(bias_done, 1)
                    if i + 2 < 2 * NG:
                        rest_group(i + 2)


def attend_layer1(nc, io, keep):
    with ExitStack() as ctx:
        def sb(n, shape, dt=F32):
            return ctx.enter_context(nc.sbuf_tensor(n, shape, dt))

        def sem(n):
            return nc.alloc_semaphore(n)

        x, ident, kT, qT = (keep[name] for name in ("x", "ident", "kT", "qT"))
        wv_hi, wv_lo, wo = keep["wv_hi"], keep["wv_lo"], keep["wo1"]
        q_now, k_now = sb("f_q_now", [P, 2, NC, T]), sb("f_k_now", [P, 2, NC, T])
        cq = sb("f_cq", [P, 2, T])
        cq_hi, cq_lo = sb("f_cq_hi", [P, 2, T], F32R), sb("f_cq_lo", [P, 2, T], F32R)
        zeros, tick = sb("f_zeros", [P, T]), sb("f_tick", [P, 1])
        mask, fill = sb("f_mask", [P, 2, T], U8), sb("f_fill", [P, 1])
        val = sb("f_val", [P, 2, HD])
        negmax, total = sb("f_negmax", [P, NQ, HQ]), sb("f_total", [P, NQ, HQ])
        rtotal = sb("f_rtotal", [P, NQ, HQ])
        expd, prob = sb("f_expd", [P, NQ, HQ, T]), sb("f_prob", [P, 2, HQ, T])
        probT = sb("f_probT", [P, NQ, HQ, T])
        outT = sb("f_outT", [P, 2, NC // 2, T])
        s_ps = ctx.enter_context(nc.psum_tensor("f_s", [P, 2, HQ, T], F32))
        t_ps = ctx.enter_context(nc.psum_tensor("f_t", [P, 2, HQ, T], F32))
        o_ps = ctx.enter_context(nc.psum_tensor("f_o", [P, 2, NC // 2, T], F32))
        v_ps = ctx.enter_context(nc.psum_tensor("f_v", [P, GT], F32))
        y_ps = ctx.enter_context(nc.psum_tensor("f_y", [P, GT], F32))
        filled = sem("f_filled")
        batch_in = [sem("f_batch_in0"), sem("f_batch_in1")]
        cq_hi_done, cq_lo_done = sem("f_cq_hi_done"), sem("f_cq_lo_done")
        val_mm, valued = sem("f_val_mm"), sem("f_valued")
        scored, masked, maxed, exped = sem("f_scored"), sem("f_masked"), sem("f_maxed"), sem("f_exped")
        inverted, probed, turned, probTed = sem("f_inverted"), sem("f_probed"), sem("f_turned"), sem("f_probTed")
        mixed, outTed, yed, x_done = sem("f_mixed"), sem("f_outTed"), sem("f_yed"), sem("f_x_done")

        def loops(eng, body):
            for n in range(4):
                body(n, n % 2)
            with eng.Fori(2, NB // 2 - 1) as pair:
                body(pair * 2, 0)
                body(pair * 2 + 1, 1)
            body(NB - 2, 0)
            body(NB - 1, 1)

        def known(n):
            return isinstance(n, int)

        def before(n, b, q, lag):
            back = (lag - q + NQ - 1) // NQ if lag > q else 0
            n, b, q = n - back, (b + back) % 2, q + back * NQ - lag
            return None if known(n) and n < 0 else (n, b, q)

        with nc.Block() as block:
            @block.sync
            def _(sp):
                def load_batch(n, b):
                    cols = bass.ds(n * T, T)
                    sp.dma_start(q_now[:, b, :, :], qT[:, :, cols]).then_inc(batch_in[b], 16)
                    sp.dma_start(k_now[:, b, :, :], kT[:, :, cols]).then_inc(batch_in[b], 16)
                    sp.dma_start(cq[:, b, :], io["ctxT"][:, cols]).then_inc(batch_in[b], 16)
                    sp.dma_start(mask[:, b, :].unsqueeze(1), io["mask"][bass.ds(n, 1)].rearrange("n t s -> t n s")
                                 ).then_inc(batch_in[b], 16)

                load_batch(0, 0)
                load_batch(1, 1)
                with sp.Fori(0, NB // 2 - 1) as pair:
                    for b in range(2):
                        n = pair * 2 + b
                        sp.wait_ge(masked, (n + 1) * NQ)
                        load_batch(n + 2, b)

            @block.gpsimd
            def _(g):
                g.memset(fill[:], -10000.0).then_inc(filled, 1)
                g.memset(zeros[:], 0.0).then_inc(filled, 1)
                g.wait_ge(filled, 2)

                def columns(n, b):
                    g.wait_ge(batch_in[b], n * 32 + (64 - 32 * b))
                    if not (known(n) and n < 2):
                        g.wait_ge(val_mm, (n - 1) * 2)
                    split_weights(g, cq[:, b, :], zeros[:], cq_hi[:, b, :], cq_lo[:, b, :],
                                  cq_hi_done, cq_lo_done, n + 1)

                columns(0, 0)

                def body(n, b):
                    if not (known(n) and n + 1 == NB):
                        columns(n + 1, 1 - b)
                    for q in range(NQ):
                        g.wait_ge(inverted, n * NQ + (q + 1))
                        if not (known(n) and n == 0 and q < 2):
                            g.wait_ge(turned, n * NQ + (q - 1))
                        g.tensor_tensor(prob[:, q % 2, :, :], expd[:, q, :, :],
                                        rtotal[:, q, :].unsqueeze(2).broadcast_to([P, HQ, T]),
                                        ALU.mult).then_inc(probed, 1)

                loops(g, body)

            @block.tensor
            def _(t):
                def values(n, b, half):
                    if half == 0:
                        t.wait_ge(cq_lo_done, n + 1)
                    if not (known(n) and n == 0 and half == 0):
                        t.wait_ge(valued, 2 * n + half)
                    cols = slice(half * GT, half * GT + GT)
                    three_passes(t, v_ps[:], cq_hi[:, b, :], cq_lo[:, b, :], wv_hi[:, cols], wv_lo[:, cols],
                                 True, True).then_inc(val_mm, 1)

                def scores(n, b, q):
                    if q == 0:
                        t.wait_ge(batch_in[b], n * 32 + (64 - 32 * b))
                    if not (known(n) and n == 0 and q < 2):
                        t.wait_ge(exped, n * NQ + (q - 1))
                    for j in range(HQ):
                        m, rows = head(q, j) // 2, slice(q % 2 * DK, q % 2 * DK + DK)
                        ins = t.matmul(s_ps[:, q % 2, j, :], q_now[rows, b, m, :], k_now[rows, b, m, :],
                                       start=True, stop=True)
                    ins.then_inc(scored, 1)

                def turn(n, b, q):
                    t.wait_ge(probed, n * NQ + (q + 1))
                    if not (known(n) and n == 0 and q < 2):
                        t.wait_ge(probTed, n * NQ + (q - 1))
                    for j in range(HQ):
                        ins = t.transpose(t_ps[:, q % 2, j, :], prob[:, q % 2, j, :], ident[:])
                    ins.then_inc(turned, 1)

                def mix(n, b, half):
                    t.wait_ge(probTed, n * NQ + (2 * half + 2))
                    if half == 0:
                        t.wait_ge(valued, 2 * n + 2)
                    if not (known(n) and n == 0):
                        t.wait_ge(outTed, 2 * n + half - 1)
                    for j in range(HQ):
                        for side in range(2):
                            h = head(2 * half + side, j)
                            ins = t.matmul(o_ps[side * DK:side * DK + DK, half, j, :],
                                           val[:, b, h * DK:h * DK + DK], probT[:, 2 * half + side, j, :],
                                           start=True, stop=True)
                    ins.then_inc(mixed, 1)

                def project(n):
                    t.wait_ge(outTed, 2 * n + 2)
                    if not (known(n) and n == 0):
                        t.wait_ge(x_done, n)
                    for m in range(NC):
                        ins = t.matmul(y_ps[:, 0:D], outT[:, m // (NC // 2), m % (NC // 2), :], wo[:, m, :],
                                       start=(m == 0), stop=(m == NC - 1))
                    ins.then_inc(yed, 1)

                values(0, 0, 0)
                values(0, 0, 1)

                def body(n, b):
                    for q in range(NQ):
                        scores(n, b, q)
                        if q >= 2 and not (known(n) and n + 1 == NB):
                            values(n + 1, 1 - b, q - 2)
                        at = before(n, b, q, 2)
                        if at:
                            turn(*at)
                        if q % 2 == 0 and not (known(n) and n == 0):
                            mix(n - 1, 1 - b, q // 2)
                        if q == 3 and not (known(n) and n == 0):
                            project(n - 1)

                loops(t, body)
                turn(NB - 1, 1, 2)
                mix(NB - 1, 1, 0)
                turn(NB - 1, 1, 3)
                mix(NB - 1, 1, 1)
                project(NB - 1)

            @block.scalar
            def _(a):
                def exponentials(n, b, q):
                    a.wait_ge(maxed, n * NQ + (q + 1))
                    if not (known(n) and n == 0):
                        a.wait_ge(probed, (n - 1) * NQ + (q + 1))
                    for j in range(HQ):
                        ins = a.activation(expd[:, q, j, :], s_ps[:, q % 2, j, :], ACT.Exp,
                                           bias=negmax[:, q, j:j + 1], accum_out=total[:, q, j:j + 1])
                    ins.then_inc(exped, 1)

                def copy_turned(n, b, q):
                    a.wait_ge(turned, n * NQ + (q + 1))
                    if not (known(n) and n == 0):
                        a.wait_ge(mixed, 2 * n + (q // 2 - 1))
                    a.activation(probT[:, q, :, :], t_ps[:, q % 2, :, :], ACT.Copy).then_inc(probTed, 1)

                def copy_out(n, half):
                    a.wait_ge(mixed, 2 * n + half + 1)
                    if not (known(n) and n == 0):
                        a.wait_ge(yed, n)
                    a.activation(outT[:, half, :, :], o_ps[:, half, :, :], ACT.Copy).then_inc(outTed, 1)

                def body(n, b):
                    for q in range(NQ):
                        at = before(n, b, q, 1)
                        if at:
                            exponentials(*at)
                        at = before(n, b, q, 2)
                        if at:
                            copy_turned(*at)
                        if q % 2 == 0 and not (known(n) and n == 0):
                            copy_out(n - 1, q // 2)

                loops(a, body)
                exponentials(NB - 1, 1, 3)
                copy_turned(NB - 1, 1, 2)
                copy_out(NB - 1, 0)
                copy_turned(NB - 1, 1, 3)
                copy_out(NB - 1, 1)

            @block.vector
            def _(v):
                v.wait_ge(filled, 2)

                def copy_values(n, b, half):
                    v.wait_ge(val_mm, 2 * n + half + 1)
                    if not (known(n) and n < 2):
                        v.wait_ge(mixed, 2 * n + half - 3)
                    v.tensor_copy(val[:, b, half * GT:half * GT + GT], v_ps[:]).then_inc(valued, 1)

                def maximum(n, b, q):
                    v.wait_ge(scored, n * NQ + (q + 1))
                    v.memset(tick[:], 0.0)
                    v.copy_predicated(s_ps[:, q % 2, :, :], mask[:, b, :].unsqueeze(1).broadcast_to([P, HQ, T]),
                                      fill[:].unsqueeze(2).broadcast_to([P, HQ, T])).then_inc(masked, 1)
                    v.wait_ge(masked, n * NQ + (q + 1))
                    if not (known(n) and n == 0):
                        v.wait_ge(exped, (n - 1) * NQ + (q + 1))
                    v.tensor_reduce(negmax[:, q, :], s_ps[:, q % 2, :, :], AX.X, ALU.max,
                                    negate=True).then_inc(maxed, 1)

                def invert(n, b, q):
                    v.wait_ge(exped, n * NQ + (q + 1))
                    if not (known(n) and n == 0):
                        v.wait_ge(probed, (n - 1) * NQ + (q + 1))
                    v.reciprocal(rtotal[:, q, :], total[:, q, :]).then_inc(inverted, 1)

                def residual(n):
                    v.wait_ge(yed, n + 1)
                    v.tensor_tensor(x[:, bass.ds(n, 1), :], x[:, bass.ds(n, 1), :],
                                    y_ps[:, 0:D].unsqueeze(1), ALU.add).then_inc(x_done, 1)

                copy_values(0, 0, 0)
                copy_values(0, 0, 1)

                def body(n, b):
                    for q in range(NQ):
                        maximum(n, b, q)
                        at = before(n, b, q, 1)
                        if at:
                            invert(*at)
                        if q >= 2 and not (known(n) and n + 1 == NB):
                            copy_values(n + 1, 1 - b, q - 2)
                        if q == 0 and not (known(n) and n < 2):
                            residual(n - 2)

                loops(v, body)
                invert(NB - 1, 1, 3)
                residual(NB - 2)
                residual(NB - 1)


def experts_layer1(nc, io, keep):
    with ExitStack() as ctx:
        def sb(n, shape, dt=F32):
            return ctx.enter_context(nc.sbuf_tensor(n, shape, dt))

        def sem(n):
            return nc.alloc_semaphore(n)

        x, ident, gate_dram = keep["x"], keep["ident"], keep["gate_dram"]
        xnT = sb("d_xnT", [P, TOK])
        x_hi, x_lo = sb("d_x_hi", [P, TOK], F32R), sb("d_x_lo", [P, TOK], F32R)
        ln = LayerNorm(nc, ctx, "d_ln")
        gate = Gate(nc, ctx, "d_gate")
        zeros = sb("d_zeros", [P, FF])
        expert_no = sb("d_expert_no", [P, E])
        ids = sb("d_ids", [P, NB, 8], U32)
        idf = sb("d_idf", [P, NB, 8])
        share, pick = sb("d_share", [P, NB, 2]), sb("d_pick", [P, NB, E])
        w = sb("d_w", [P, 2, 3, FF])
        w_hi, w_lo = sb("d_w_hi", [P, 2, 3, FF], F32R), sb("d_w_lo", [P, 2, 3, FF], F32R)
        gate_rows = sb("d_gate_rows", [P, 2, TOK])
        gx = sb("d_gx", [P, 2, GT])
        gx_hi, gx_lo = sb("d_gx_hi", [P, 2, GT], F32R), sb("d_gx_lo", [P, 2, GT], F32R)
        relu = sb("d_relu", [P, 2, GT])
        LAG, RING = 3, 8
        inner = sb("d_inner", [P, KF, GT])
        in_hi, in_lo = sb("d_in_hi", [P, RING, GT], F32R), sb("d_in_lo", [P, RING, GT], F32R)
        acc = sb("d_acc", [P, TOK])
        g_ps = ctx.enter_context(nc.psum_tensor("d_g", [P, 2, GT], F32))
        u_ps = ctx.enter_context(nc.psum_tensor("d_u", [P, 2, GT], F32))
        down_ps = ctx.enter_context(nc.psum_tensor("d_down", [P, NG, GT], F32))
        x_hi_done, x_lo_done = sem("d_x_hi_done"), sem("d_x_lo_done")
        numbered = sem("d_numbered")
        w_in = [sem("d_w_in0"), sem("d_w_in1")]
        rows_in = [sem("d_rows_in0"), sem("d_rows_in1")]
        w_hi_done, w_lo_done = sem("d_w_hi_done"), sem("d_w_lo_done")
        gx_done, gx_hi_done, gx_lo_done = sem("d_gx_done"), sem("d_gx_hi_done"), sem("d_gx_lo_done")
        g_mm, u_mm, relued = sem("d_g_mm"), sem("d_u_mm"), sem("d_relued")
        innered, in_hi_done, in_lo_done = sem("d_innered"), sem("d_in_hi_done"), sem("d_in_lo_done")
        downed, acc_done, turned, x_done = sem("d_downed"), sem("d_acc_done"), sem("d_turned"), sem("d_x_done")

        def experts(eng, body):
            body(0, 0)
            body(1, 1)
            with eng.Fori(1, E // 2 - 1) as pair:
                body(pair * 2, 0)
                body(pair * 2 + 1, 1)
            body(E - 2, 0)
            body(E - 1, 1)

        def first(e):
            return isinstance(e, int) and e == 0

        def after(e, b, k):
            if k + 1 < NG:
                return e, b, k + 1
            return None if isinstance(e, int) and e == E - 1 else (e + 1, 1 - b, 0)

        with nc.Block() as block:
            @block.sync
            def _(sp):
                sp.dma_start(gate.wr[:], io["Wr1"]).then_inc(gate.wr_in, 16)

                def load_weights(e, b):
                    one = bass.ds(e, 1)
                    sp.dma_start(w[:, b, 0, :].unsqueeze(1), io["Wg"][one].rearrange("e c f -> c e f")
                                 ).then_inc(w_in[b], 16)
                    sp.dma_start(w[:, b, 1, :].unsqueeze(1), io["Wu"][one].rearrange("e c f -> c e f")
                                 ).then_inc(w_in[b], 16)
                    sp.dma_start(w[:, b, 2, :].rearrange("p (k d) -> p k d", k=KF),
                                 io["Wd"][one].rearrange("e (k p) d -> p (e k) d", p=P)).then_inc(w_in[b], 16)

                def load_rows(e, b):
                    sp.dma_start(gate_rows[:, b, :], gate_dram[bass.ds(e, 1), :].broadcast_to([P, TOK])
                                 ).then_inc(rows_in[b], 16)

                load_weights(0, 0)
                load_weights(1, 1)
                gate.sync_out(sp, gate_dram)
                load_rows(0, 0)
                load_rows(1, 1)

                def refill(e, b):
                    sp.wait_ge(w_lo_done, e + 1)
                    load_weights(e + 2, b)
                    sp.wait_ge(gx_done, (e + 1) * NG)
                    load_rows(e + 2, b)

                with sp.Fori(0, E // 2 - 1) as pair:
                    refill(pair * 2, 0)
                    refill(pair * 2 + 1, 1)

            @block.gpsimd
            def _(g):
                ln.gpsimd(g)
                for e in range(E):
                    g.memset(expert_no[:, e:e + 1], float(e))
                g.memset(zeros[:], 0.0).then_inc(numbered, 1)
                g.wait_ge(numbered, 1)

                def body(e, b):
                    g.wait_ge(w_in[b], e * 24 + (48 - 24 * b))
                    if not (isinstance(e, int) and e < 2):
                        g.wait_ge(downed, (e - 1) * UNITS)
                    split_weights(g, w[:, b, :, :], zeros[:].unsqueeze(1).broadcast_to([P, 3, FF]), w_hi[:, b, :, :], w_lo[:, b, :, :],
                                  w_hi_done, w_lo_done, e + 1)

                experts(g, body)

            @block.tensor
            def _(t):
                for k in range(NG):
                    ln.tensor(t, down_ps[:, 0:2, :], ident[:], k)
                gate.tensor_logits(t, down_ps[:, 2, :], xnT, ln.xnT_done)

                def up(e, b, k):
                    cols = slice(k * GT, k * GT + GT)
                    if k == 0:
                        t.wait_ge(w_lo_done, e + 1)
                    if first(e):
                        t.wait_ge(x_lo_done, k + 1)
                    for c in range(KF):
                        unit, chunk = k * KF + c, slice(c * P, c * P + P)
                        if not (first(e) and unit < 2):
                            t.wait_ge(relued, e * UNITS + (unit - 1))
                        three_passes(t, g_ps[:, c % 2, :], w_hi[:, b, 0, chunk], w_lo[:, b, 0, chunk],
                                     x_hi[:, cols], x_lo[:, cols], True, True).then_inc(g_mm, 1)
                        if first(e) and unit == 0:
                            gate.tensor_turn(t, down_ps[:, 0:2, :], ident[:])
                        if c == 0:
                            t.wait_ge(gx_lo_done, e * NG + (k + 1))
                        if not (first(e) and unit < 2):
                            t.wait_ge(innered, e * UNITS + (unit - 1))
                        three_passes(t, u_ps[:, c % 2, :], w_hi[:, b, 1, chunk], w_lo[:, b, 1, chunk],
                                     gx_hi[:, k % 2, :], gx_lo[:, k % 2, :], True, True).then_inc(u_mm, 1)
                        if unit >= LAG:
                            down(e, b, unit - LAG)
                        elif not first(e):
                            down(e - 1, 1 - b, UNITS + unit - LAG)

                def down(e, b, unit):
                    k, c = unit // KF, unit % KF
                    t.wait_ge(in_lo_done, e * UNITS + (unit + 1))
                    ins = three_passes(t, down_ps[:, k, :], w_hi[:, b, 2, c * P:c * P + P],
                                       w_lo[:, b, 2, c * P:c * P + P],
                                       in_hi[:, unit % RING, :], in_lo[:, unit % RING, :],
                                       first(e) and c == 0, False, skip_group_check=True)
                    ins.then_inc(downed, 1)

                def body(e, b):
                    for k in range(NG):
                        up(e, b, k)

                experts(t, body)
                for unit in range(UNITS - LAG, UNITS):
                    down(E - 1, 1, unit)
                for k in range(NG):
                    t.wait_ge(acc_done, k + 1)
                    if k >= 2:
                        t.wait_ge(x_done, k - 1)
                    for m in range(GB):
                        n = GB * k + m
                        ins = t.transpose(g_ps[:, k % 2, m * T:m * T + T], acc[:, n * T:n * T + T], ident[:])
                    ins.then_inc(turned, 1)

            @block.scalar
            def _(a):
                for k in range(NG):
                    ln.scalar(a, down_ps[:, 0:2, :], xnT, k)
                    cols = slice(k * GT, k * GT + GT)
                    a.wait_ge(ln.xnT_done, k + 1)
                    a.activation(x_hi[:, cols], xnT[:, cols], ACT.Copy).then_inc(x_hi_done, 1)
                gate.scalar_exp(a)
                gate.scalar_turned(a, down_ps[:, 0:2, :])

                def round_inner(e, unit):
                    k, c = unit // KF, unit % KF
                    a.wait_ge(innered, e * UNITS + (unit + 1))
                    if not (first(e) and unit < RING):
                        a.wait_ge(downed, e * UNITS + (unit - RING + 1))
                    a.activation(in_hi[:, unit % RING, :], inner[:, c, :], ACT.Copy).then_inc(in_hi_done, 1)

                def round_rows(e, b, k):
                    a.wait_ge(gx_done, e * NG + (k + 1))
                    if not (first(e) and k < 2):
                        a.wait_ge(u_mm, e * UNITS + (k - 1) * KF)
                    a.activation(gx_hi[:, k % 2, :], gx[:, k % 2, :], ACT.Copy).then_inc(gx_hi_done, 1)

                round_rows(0, 0, 0)

                def body(e, b):
                    for unit in range(UNITS):
                        k, c = unit // KF, unit % KF
                        if c == 2 and after(e, b, k):
                            round_rows(*after(e, b, k))
                        a.wait_ge(g_mm, e * UNITS + (unit + 1))
                        if not (first(e) and unit < 2):
                            a.wait_ge(innered, e * UNITS + (unit - 1))
                        a.activation(relu[:, c % 2, :], g_ps[:, c % 2, :], ACT.Relu).then_inc(relued, 1)
                        if unit:
                            round_inner(e, unit - 1)
                        elif not first(e):
                            round_inner(e - 1, UNITS - 1)

                experts(a, body)
                round_inner(E - 1, UNITS - 1)
                for k in range(NG):
                    a.wait_ge(downed, (E - 1) * UNITS + (k + 1) * KF)
                    a.activation(acc[:, k * GT:k * GT + GT], down_ps[:, k, :], ACT.Copy).then_inc(acc_done, 1)

            @block.vector
            def _(v):
                ln.vector(v, x)
                for k in range(NG):
                    cols = slice(k * GT, k * GT + GT)
                    v.wait_ge(x_hi_done, k + 1)
                    v.tensor_tensor(x_lo[:, cols], xnT[:, cols], x_hi[:, cols].bitcast(F32),
                                    ALU.subtract).then_inc(x_lo_done, 1)
                all_e = [P, NB, E]
                v.wait_ge(gate.logits, 1)
                gate.then(v, v.tensor_copy(gate.logit[:], down_ps[:, 2, 0:NB * E].rearrange("p (n e) -> p n e", e=E)))
                gate.then(v, v.tensor_reduce(gate.total[:], gate.logit[:], AX.X, ALU.max))
                v.tensor_tensor(gate.away[:], gate.logit[:], gate.total[:].unsqueeze(2).broadcast_to(all_e),
                                ALU.subtract).then_inc(gate.away_done, 1)
                v.wait_ge(gate.exped, 1)
                gate.then(v, v.tensor_reduce(gate.total[:], gate.expd[:], AX.X, ALU.add))
                gate.then(v, v.reciprocal(gate.rtotal[:], gate.total[:]))
                gate.then(v, v.tensor_tensor(gate.kept[:], gate.expd[:],
                                             gate.rtotal[:].unsqueeze(2).broadcast_to(all_e), ALU.mult))
                for n in range(NB):
                    ins = v.max(gate.top[:, n, :], gate.kept[:, n, :])
                gate.then(v, ins)
                for n in range(NB):
                    ins = v.max_index(ids[:, n, :], gate.top[:, n, :], gate.kept[:, n, :])
                gate.then(v, ins)
                gate.then(v, v.tensor_copy(idf[:], ids[:]))
                gate.then(v, v.tensor_tensor(gate.total[:], gate.top[:, :, 0], gate.top[:, :, 1], ALU.add))
                gate.then(v, v.tensor_scalar(gate.total[:], gate.total[:], 2.0 ** -23, None, ALU.add))
                gate.then(v, v.reciprocal(gate.rtotal[:], gate.total[:]))
                gate.then(v, v.tensor_tensor(share[:], gate.top[:, :, 0:2],
                                             gate.rtotal[:].unsqueeze(2).broadcast_to([P, NB, 2]), ALU.mult))
                v.wait_ge(numbered, 1)
                numbers = expert_no[:].unsqueeze(1).broadcast_to(all_e)
                for i, (hit, out) in enumerate(((gate.kept, gate.kept), (pick, pick))):
                    gate.then(v, v.tensor_tensor(hit[:], numbers, idf[:, :, i:i + 1].broadcast_to(all_e),
                                                 ALU.is_equal))
                    gate.then(v, v.tensor_tensor(out[:], hit[:], share[:, :, i:i + 1].broadcast_to(all_e),
                                                 ALU.mult))
                v.tensor_tensor(gate.gate[:], gate.kept[:], pick[:], ALU.add).then_inc(gate.gated, 1)

                def gated_rows(e, b, k):
                    cols = slice(k * GT, k * GT + GT)
                    if k == 0:
                        v.wait_ge(rows_in[b], e * 8 + (16 - 8 * b))
                    v.tensor_tensor(gx[:, k % 2, :], xnT[:, cols], gate_rows[:, b, cols],
                                    ALU.mult).then_inc(gx_done, 1)

                def gated_rest(e, b, k):
                    v.wait_ge(gx_hi_done, e * NG + (k + 1))
                    v.tensor_tensor(gx_lo[:, k % 2, :], gx[:, k % 2, :], gx_hi[:, k % 2, :].bitcast(F32),
                                    ALU.subtract).then_inc(gx_lo_done, 1)

                def multiply(e, unit):
                    k, c = unit // KF, unit % KF
                    v.wait_ge(relued, e * UNITS + (unit + 1))
                    v.wait_ge(u_mm, e * UNITS + (unit + 1))
                    if not (first(e) and k < 1):
                        v.wait_ge(in_lo_done, e * UNITS + (unit - KF + 1))
                    v.tensor_tensor(inner[:, c, :], relu[:, c % 2, :], u_ps[:, c % 2, :],
                                    ALU.mult).then_inc(innered, 1)

                def rest_inner(e, unit):
                    k, c = unit // KF, unit % KF
                    v.wait_ge(in_hi_done, e * UNITS + (unit + 1))
                    if not (first(e) and unit < RING):
                        v.wait_ge(downed, e * UNITS + (unit - RING + 1))
                    v.tensor_tensor(in_lo[:, unit % RING, :], inner[:, c, :],
                                    in_hi[:, unit % RING, :].bitcast(F32), ALU.subtract).then_inc(in_lo_done, 1)

                gated_rows(0, 0, 0)
                gated_rest(0, 0, 0)

                def body(e, b):
                    for unit in range(UNITS):
                        k, c = unit // KF, unit % KF
                        multiply(e, unit)
                        if c == 1 and after(e, b, k):
                            gated_rows(*after(e, b, k))
                        if c == 3 and after(e, b, k):
                            gated_rest(*after(e, b, k))
                        if unit:
                            rest_inner(e, unit - 1)
                        elif not first(e):
                            rest_inner(e - 1, UNITS - 1)

                experts(v, body)
                rest_inner(E - 1, UNITS - 1)
                for k in range(NG):
                    v.wait_ge(turned, k + 1)
                    v.tensor_tensor(x[:, GB * k:GB * k + GB, :], x[:, GB * k:GB * k + GB, :],
                                    g_ps[:, k % 2, :].rearrange("p (m d) -> p m d", m=GB),
                                    ALU.add).then_inc(x_done, 1)


def program(nc, io, out):
    with ExitStack() as ctx:
        def sb(n, shape, dt=F32):
            return ctx.enter_context(nc.sbuf_tensor(n, shape, dt))

        keep = {
            "x": sb("x", [P, NB, D]),
            "ident": sb("ident", [P, P]),
            "gate_dram": nc.dram_tensor("gate_rows", (E, TOK), F32, kind="Internal").ap(),
            "v_dram": nc.dram_tensor("v_rows", (NB, T, D), F32, kind="Internal").ap(),
        }
        with nc.cleanup_on_exit(), ExitStack() as first:
            keep["k_dram"] = nc.dram_tensor("k_parts", (NB, K_COPIES, D, T), BF16, kind="Internal").ap()
            keep["q_dram"] = nc.dram_tensor("q_parts", (NB, PARTS, D, T), BF16, kind="Internal").ap()
            for name, shape, dt in (
                    ("kn", [KS, 2, PIECES, T], BF16),
                    ("kh", [P, 2, H, RT, PIECES], BF16),
                    ("qn", [P, 2, PIECES, T], BF16),
                    ("val", [P, 2, H, 32], F32)):
                keep[name] = first.enter_context(nc.sbuf_tensor(name, shape, dt))
            for name in ("kb", "qb"):
                keep[name] = first.enter_context(nc.sbuf_tensor(name, [P, PARTS, TOK], BF16))
            keep["vt"] = first.enter_context(nc.sbuf_tensor("vt", [P, NB, D], F32))
            keep["kqv_out"] = [nc.alloc_semaphore(f"kqv_out{k}") for k in range(NG)]
            keep["wo0"] = first.enter_context(nc.sbuf_tensor("wo0", [P, D], F32))
            keep["bo_rows"] = first.enter_context(nc.sbuf_tensor("bo_rows", [P, D], F32))
            for name in ("k_in", "q_in", "val_in"):
                keep[name] = [nc.alloc_semaphore(f"{name}{b}") for b in range(2)]
            with nc.sbuf_tensor("xnT0", [P, TOK], F32) as xnT, nc.sbuf_tensor("ctxT0", [P, TOK], F32) as ctxT:
                keep["xnT"], keep["ctxT"] = xnT, ctxT
                project_layer0(nc, io, keep)
            attend_layer0(nc, io, keep)
        with nc.cleanup_on_exit():
            experts_layer0(nc, io, keep)
        with nc.cleanup_on_exit(), ExitStack() as second:
            for name, shape, dt in (
                    ("kT", [P, NC, TOK], F32), ("qT", [P, NC, TOK], F32),
                    ("wv_hi", [P, HD], F32R), ("wv_lo", [P, HD], F32R), ("wo1", [P, NC, D], F32)):
                keep[name] = second.enter_context(nc.sbuf_tensor(name, shape, dt))
            project_layer1(nc, io, keep)
            attend_layer1(nc, io, keep)
        experts_layer1(nc, io, keep)
        store(nc, keep["x"], out)


def store(nc, x, out):
    with nc.semaphore("stored") as stored, nc.Block() as block:
        @block.sync
        def _(sp):
            sp.dma_start(out.rearrange("n t d -> t n d"), x[:]).then_inc(stored, 16)
            sp.wait_ge(stored, 16)


def layouts(a):
    col = lambda v: v.reshape(-1, 1)
    row = lambda v: v.reshape(1, -1)
    by_d = np.arange(D).reshape(PIECES, DH).T.ravel()
    return {
        "x": a["x"],
        "ctxT": a["ctx_1024"].reshape(TOK, D).T,
        "Wq0": a["L0_xattn_Wq"][:, by_d], "Wk0": a["L0_xattn_Wk"][:, by_d], "Wv0": a["L0_xattn_Wv"],
        "Wo0": a["L0_xattn_Wo"][by_d], "bq0": col(a["L0_xattn_bq"][by_d]), "bk0": col(a["L0_xattn_bk"][by_d]),
        "wQ": a["L1_xattn_wQ_w"].T, "wK": a["L1_xattn_wK_w"].T, "wV": a["L1_xattn_wV_w"].T,
        "wO": a["L1_xattn_wOut_w"].T, "bQ": a["L1_xattn_wQ_b"].reshape(NC, P).T,
        "bK": a["L1_xattn_wK_b"].reshape(NC, P).T, "bV": a["L1_xattn_wV_b"].reshape(NC, P).T,
        "bO": row(a["L1_xattn_wOut_b"]), "mask": a["mask_BxSxS2_bf0"],
        "Wr1": a["L1_ffn_Wr"].T, "Wg": a["L1_ffn_Wg"].transpose(0, 2, 1), "Wu": a["L1_ffn_Wu"].transpose(0, 2, 1),
        "Wd": a["L1_ffn_Wd"].transpose(0, 2, 1),
        "Wr0": a["L0_ffn_Wr"], "br0": row(a["L0_ffn_br"]), "W1": a["L0_ffn_W1"], "W2": a["L0_ffn_W2"],
        "b1": a["L0_ffn_b1"].reshape(E, KF, P).transpose(2, 0, 1), "b2": a["L0_ffn_b2"].T,
        "bv0": row(a["L0_xattn_bv"]), "bo0": row(a["L0_xattn_bo"]),
    }


def kernel(**inputs):
    from concourse import bacc
    from concourse.bass_utils import run_bass_kernel_spmd

    nc = bacc.Bacc("TRN2", target_bir_lowering=False, num_devices=1)
    arrays, io = {}, {}
    for name, a in layouts({name: np.asarray(a) for name, a in inputs.items()}).items():
        a = np.ascontiguousarray(a)
        arrays[f"in_{name}_dram"] = a
        io[name] = nc.dram_tensor(f"in_{name}_dram", a.shape, mybir.dt.from_np(a.dtype), kind="ExternalInput").ap()
    out = nc.dram_tensor("out_0_dram", (NB, T, D), F32, kind="ExternalOutput").ap()
    program(nc, io, out)
    r = run_bass_kernel_spmd(nc, [arrays], core_ids=[0])
    return r.results[0]["out_0_dram"]
```

```python
from contextlib import ExitStack

import concourse.bass as bass
import numpy as np
from concourse import mybir

F32 = mybir.dt.float32
F32R = mybir.dt.float32r
BF16 = mybir.dt.bfloat16
U8 = mybir.dt.uint8
U32 = mybir.dt.uint32
ALU = mybir.AluOpType
ACT = mybir.ActivationFunctionType
AX = mybir.AxisListType

P = 128
NB = 16
T = 128
D = 128
TOK = NB * T
GB = 4
NG = NB // GB
GT = GB * T
H = 16
DH = D // H
PIECES = D // DH
RT = T // H
E = 8
EPS = 1e-5


class LayerNorm:

    def __init__(self, nc, ctx, name):
        def sb(n, shape, dt=F32):
            return ctx.enter_context(nc.sbuf_tensor(f"{name}_{n}", shape, dt))

        def sem(n):
            return nc.alloc_semaphore(f"{name}_{n}")

        self.name = name
        self.stats = sb("stats", [P, NB, 6])
        self.mv = sb("mv", [P, NB, 2])
        self.var_eps = sb("var_eps", [P, NB])
        self.minus_half = sb("minus_half", [P, NB])
        self.rstd = sb("rstd", [P, NB])
        self.stats_done = sem("stats_done")
        self.mv_done = sem("mv_done")
        self.half_set = sem("half_set")
        self.var_done = sem("var_done")
        self.rstd_done = sem("rstd_done")
        self.xn_done = sem("xn_done")
        self.transposed = sem("transposed")
        self.xnT_done = sem("xnT_done")

    def place_xn(self, nc, ctx):
        self.xn = ctx.enter_context(nc.sbuf_tensor(f"{self.name}_xn", [P, NB, D], F32))

    def statistics(self, v, x, n0=0, n1=NB):
        for n in range(n0, n1):
            v.bn_stats(self.stats[:, n, :], x[:, n, :]).then_inc(self.stats_done, 1)
        for n in range(n0, n1):
            v.wait_ge(self.stats_done, n + 1)
            v.bn_aggr(self.mv[:, n, :], self.stats[:, n, :]).then_inc(self.mv_done, 1)

    def normalise(self, v, x, k):
        v.wait_ge(self.rstd_done, k + 1)
        for n in range(GB * k, GB * k + GB):
            v.tensor_scalar(self.xn[:, n, :], x[:, n, :], self.mv[:, n, 0:1], self.rstd[:, n:n + 1],
                            ALU.subtract, ALU.mult).then_inc(self.xn_done, 1)

    def gpsimd(self, g, k0=0, k1=NG):
        if k0 == 0:
            g.memset(self.minus_half[:], -0.5).then_inc(self.half_set, 1)
            g.wait_ge(self.half_set, 1)
        for k in range(k0, k1):
            g.wait_ge(self.mv_done, GB * (k + 1))
            cols = slice(GB * k, GB * k + GB)
            g.tensor_scalar(self.var_eps[:, cols], self.mv[:, cols, 1], EPS, None,
                            ALU.add).then_inc(self.var_done, 1)
            g.wait_ge(self.var_done, k + 1)
            g.tensor_tensor(self.rstd[:, cols], self.var_eps[:, cols], self.minus_half[:, cols],
                            ALU.pow).then_inc(self.rstd_done, 1)

    def tensor(self, t, psum, ident, k):
        if k >= 2:
            t.wait_ge(self.xnT_done, k - 1)
        for m in range(GB):
            n = GB * k + m
            t.wait_ge(self.xn_done, n + 1)
            ins = t.transpose(psum[:, k % 2, m * T:m * T + T], self.xn[:, n, :], ident)
        ins.then_inc(self.transposed, 1)

    def scalar(self, a, psum, xnT, k):
        a.wait_ge(self.transposed, k + 1)
        a.activation(xnT[:, k * GT:k * GT + GT], psum[:, k % 2, :], ACT.Copy).then_inc(self.xnT_done, 1)


PARTS = 3
K_COPIES = 2 * PARTS - 1
SEGMENTS = [(0, GB), (GB, 2 * GB), (2 * GB, NB)]
SENT = 16 * (K_COPIES + PARTS + 1)
KS = DH * PARTS * PARTS


def project_layer0(nc, io, keep):
    with ExitStack() as ctx:
        def sb(n, shape, dt=F32):
            return ctx.enter_context(nc.sbuf_tensor(n, shape, dt))

        def sem(n):
            return nc.alloc_semaphore(n)

        wq, wk, wv = sb("p_wq", [P, D]), sb("p_wk", [P, D]), sb("p_wv", [P, D])
        bq, bk = sb("p_bq", [P, 1]), sb("p_bk", [P, 1])
        bv_rows, bo_rows, wo = sb("p_bv_rows", [P, D]), keep["bo_rows"], keep["wo0"]
        kf, qf = sb("p_kf", [P, NG, GT]), sb("p_qf", [P, NG, GT])
        kb, qb, vt = keep["kb"], keep["qb"], keep["vt"]
        tr_ps = ctx.enter_context(nc.psum_tensor("p_tr", [P, 2, GT], F32))
        q_ps = ctx.enter_context(nc.psum_tensor("p_q", [P, 2, GT], F32))
        k_ps = ctx.enter_context(nc.psum_tensor("p_k", [P, 2, GT], F32))
        v_ps = ctx.enter_context(nc.psum_tensor("p_v", [P, 2, GT], F32))
        ln = LayerNorm(nc, ctx, "p_ln")
        ln.place_xn(nc, ctx)
        x_in, ctx_in, w_in = [sem(f"p_x_in{k}") for k in range(NG)], sem("p_ctx_in"), sem("p_w_in")
        ident_zero, ident_done = sem("p_ident_zero"), sem("p_ident_done")
        k_mm, v_mm, q_mm = sem("p_k_mm"), sem("p_v_mm"), sem("p_q_mm")
        k_b1, q_b1 = sem("p_k_b1"), sem("p_q_b1")
        k_r1, q_r1 = sem("p_k_r1"), sem("p_q_r1")
        k_b2, q_b2 = sem("p_k_b2"), sem("p_q_b2")
        k_b3, q_b3 = sem("p_k_b3"), sem("p_q_b3")
        v_done = sem("p_v_done")
        rows_zero, next_in = sem("p_rows_zero"), sem("p_next_in")
        x, ctxT, xnT, ident = keep["x"], keep["ctxT"], keep["xnT"], keep["ident"]

        with nc.Block() as block:
            @block.sync
            def _(sp):
                sp.dma_start(ctxT[:], io["ctxT"]).then_inc(ctx_in, 16)
                sp.dma_start(wk[:], io["Wk0"]).then_inc(w_in, 16)
                sp.dma_start(wv[:], io["Wv0"]).then_inc(w_in, 16)
                sp.dma_start(wq[:], io["Wq0"]).then_inc(w_in, 16)
                sp.dma_start(bk[:], io["bk0"]).then_inc(w_in, 16)
                sp.dma_start(bq[:], io["bq0"]).then_inc(w_in, 16)
                sp.dma_start(bv_rows[:], io["bv0"].broadcast_to([P, D])).then_inc(w_in, 16)
                sp.dma_start(bo_rows[:], io["bo0"].broadcast_to([P, D])).then_inc(next_in, 16)
                sp.dma_start(wo[:], io["Wo0"]).then_inc(next_in, 16)
                sp.wait_ge(k_b3, 1)
                send(sp, keep, 0, "k")
                sp.wait_ge(q_b3, 1)
                sp.wait_ge(v_done, 1)
                send(sp, keep, 0, "q")
                send(sp, keep, 0, "v")
                sp.wait_ge(rows_zero, 3)
                sp.wait_ge(next_in, 32)
                sp.wait_ge(keep["kqv_out"][0], SENT)
                for n in range(2):
                    load_keys(sp, keep, n, n)
                    load_queries(sp, keep, n, n)
                    load_values(sp, keep, n, n)

            @block.gpsimd
            def _(g):
                g.memset(ident[:], 0.0).then_inc(ident_zero, 1)
                g.wait_ge(ident_zero, 1)
                g.affine_select(out=ident[:], in_=ident[:], compare_op=ALU.not_equal, fill=1.0, base=0,
                                pattern=[[-1, P]], channel_multiplier=1).then_inc(ident_done, 1)
                ln.gpsimd(g)
                def last_part(k):
                    cols = slice(k * GT, k * GT + GT)
                    g.wait_ge(k_b2, k + 1)
                    g.tensor_tensor(kb[:, 2, cols], kf[:, k, :], kb[:, 1, cols],
                                    ALU.subtract).then_inc(k_b3, 1)

                for k in range(NG):
                    cols = slice(k * GT, k * GT + GT)
                    g.wait_ge(k_b1, 2 * k + 2)
                    g.tensor_tensor(kf[:, k, :], kf[:, k, :], kb[:, 0, cols],
                                    ALU.subtract).then_inc(k_r1, 1)
                    if k:
                        last_part(k - 1)
                last_part(NG - 1)

            @block.tensor
            def _(t):
                t.wait_ge(ctx_in, 16)
                t.wait_ge(w_in, 16 * 6)
                for k in range(NG):
                    if k >= 2:
                        t.wait_ge(k_b1, 2 * (k - 1))
                    t.matmul(k_ps[:, k % 2, :], wk[:], ctxT[:, k * GT:k * GT + GT],
                             start=True, stop=True).then_inc(k_mm, 1)
                t.wait_ge(ident_done, 1)

                def values(k):
                    if k >= 2:
                        t.wait_ge(v_done, k - 1)
                    for m in range(GB):
                        n = GB * k + m
                        ins = t.matmul(v_ps[:, k % 2, m * T:m * T + T], ctxT[:, n * T:n * T + T], wv[:],
                                       start=True, stop=True)
                    ins.then_inc(v_mm, 1)

                def queries(k):
                    t.wait_ge(ln.xnT_done, k + 1)
                    if k >= 2:
                        t.wait_ge(q_b1, 2 * (k - 1))
                    t.matmul(q_ps[:, k % 2, :], wq[:], xnT[:, k * GT:k * GT + GT],
                             start=True, stop=True).then_inc(q_mm, 1)

                for k in range(NG):
                    ln.tensor(t, tr_ps, ident[:], k)
                    values(k)
                    queries(k)

            @block.scalar
            def _(a):
                for k in range(NG):
                    rows = slice(GB * k, GB * k + GB)
                    a.dma_start(x[:, rows, :], io["x"][rows].rearrange("n t d -> t n d")).then_inc(x_in[k], 16)

                def parts(ps, bias, full, hi, mm, b1, k):
                    a.wait_ge(mm, k + 1)
                    a.activation(full[:, k, :], ps[:, k % 2, :], ACT.Identity,
                                 bias=bias[:]).then_inc(b1, 1)
                    a.activation(hi[:, 0, k * GT:k * GT + GT], ps[:, k % 2, :], ACT.Identity,
                                 bias=bias[:]).then_inc(b1, 1)

                def keys(k):
                    parts(k_ps, bk, kf, kb, k_mm, k_b1, k)

                def second_part(k):
                    a.wait_ge(k_r1, k + 1)
                    a.activation(kb[:, 1, k * GT:k * GT + GT], kf[:, k, :], ACT.Copy).then_inc(k_b2, 1)

                keys(0)
                keys(1)
                for k in range(NG):
                    ln.scalar(a, tr_ps, xnT, k)
                    if k < 2:
                        keys(k + 2)
                    parts(q_ps, bq, qf, qb, q_mm, q_b1, k)
                    second_part(k)

            @block.vector
            def _(v):
                v.memset(keep["qn"][:], 0.0).then_inc(rows_zero, 1)
                v.memset(keep["kh"][:], 0.0).then_inc(rows_zero, 1)
                v.memset(keep["val"][:], 0.0).then_inc(rows_zero, 1)
                for k in range(NG):
                    v.wait_ge(x_in[k], 16)
                    ln.statistics(v, x, GB * k, GB * k + GB)
                for k in range(NG):
                    ln.normalise(v, x, k)
                for k in range(NG):
                    v.wait_ge(v_mm, k + 1)
                    v.tensor_tensor(vt[:, GB * k:GB * k + GB, :],
                                    v_ps[:, k % 2, :].rearrange("p (m d) -> p m d", m=GB),
                                    bv_rows[:].unsqueeze(1).broadcast_to([P, GB, D]),
                                    ALU.add).then_inc(v_done, 1)
                    cols = slice(k * GT, k * GT + GT)
                    v.wait_ge(q_b1, 2 * k + 2)
                    v.tensor_tensor(qf[:, k, :], qf[:, k, :], qb[:, 0, cols],
                                    ALU.subtract).then_inc(q_r1, 1)
                    v.wait_ge(q_r1, k + 1)
                    v.tensor_copy(qb[:, 1, cols], qf[:, k, :]).then_inc(q_b2, 1)
                    v.wait_ge(q_b2, k + 1)
                    v.tensor_tensor(qb[:, 2, cols], qf[:, k, :], qb[:, 1, cols],
                                    ALU.subtract).then_inc(q_b3, 1)


def send(eng, keep, seg, what):
    n0, n1 = SEGMENTS[seg]
    done, cols = keep["kqv_out"][seg], slice(n0 * T, n1 * T)
    if what == "v":
        eng.dma_start(keep["v_dram"][n0:n1].rearrange("n t d -> t n d"), keep["vt"][:, n0:n1, :]).then_inc(done, 16)
        return
    for c in range(K_COPIES if what == "k" else PARTS):
        eng.dma_start(keep[what + "_dram"][n0:n1, c, :, :].rearrange("n f t -> f n t"),
                      keep[what + "b"][:, c % PARTS, cols].rearrange("f (n t) -> f n t", t=T)).then_inc(done, 16)


def load_queries(eng, keep, n, b):
    src = keep["q_dram"][bass.ds(n, 1)].rearrange("n c (d l) t -> (c d) n (l t)", d=DH)
    eng.dma_start(keep["qn"][0:KS, b, :, :], src.broadcast_to([PARTS * DH, PARTS, PIECES * T])
                  ).then_inc(keep["q_in"][b], 16)


def load_values(eng, keep, n, b):
    src = keep["v_dram"][bass.ds(n, 1)].rearrange("n (h b) (l d) -> (b l) (n h) d", b=RT, d=DH)
    eng.dma_start(keep["val"][:, b, :, 0:DH], src).then_inc(keep["val_in"][b], 16)


def load_keys(eng, keep, n, b):
    src = keep["k_dram"][bass.ds(n, 1)]
    rolled = bass.AP(tensor=src.tensor, offset=src.offset,
                     ap=[[PIECES * T, PARTS * DH], [D * T, PARTS], [1, PIECES * T]])
    eng.dma_start(keep["kn"][:, b, :, :], rolled).then_inc(keep["k_in"][b], 16)


def attend_layer0(nc, io, keep):
    HT = T // 2
    HJ = PIECES // 2
    with ExitStack() as ctx:
        def sb(n, shape, dt=F32):
            return ctx.enter_context(nc.sbuf_tensor(n, shape, dt))

        def sem(n):
            return nc.alloc_semaphore(n)

        x, ident, kh, kn, qn, val = (keep[name] for name in ("x", "ident", "kh", "kn", "qn", "val"))
        k_in, q_in, val_in = keep["k_in"], keep["q_in"], keep["val_in"]
        wo, bo_rows = keep["wo0"], keep["bo_rows"]
        negmax, identr = sb("a_negmax", [P, 2, HT], F32R), sb("a_identr", [P, P], F32R)
        expd = sb("a_expd", [P, 2, 2, H, HT])
        total = sb("a_total", [P, 2, HT])
        rtotal = sb("a_rtotal", [P, 2, HT])
        prob = sb("a_prob", [P, 2, H, T])
        ot = sb("a_ot", [P, 2, PIECES, 4, RT])
        oT = sb("a_oT", [P, 2, T])
        s_ps = ctx.enter_context(nc.psum_tensor("a_s", [P, 2, H, HT], F32))
        o_ps = ctx.enter_context(nc.psum_tensor("a_o", [P, 2, 4, T], F32))
        y_ps = ctx.enter_context(nc.psum_tensor("a_y", [P, 2, GT], F32))
        rows = keep["rows0"]
        rows_ps = s_ps[:, 0, :, :].rearrange("p (c h) t -> p c (h t)", c=2)
        biased, identr_done = sem("a_biased"), sem("a_identr_done")
        keyed = sem("a_keyed")
        scored, maxed, shifted, exped = sem("a_scored"), sem("a_maxed"), sem("a_shifted"), sem("a_exped")
        summed, inverted, probed = sem("a_summed"), sem("a_inverted"), sem("a_probed")
        mixed, ot_done, yed, x_done = sem("a_mixed"), sem("a_ot_done"), sem("a_yed"), sem("a_x_done")
        oT_in = [sem("a_oT_in0"), sem("a_oT_in1")]


        def loops(eng, body):
            for n in range(4):
                body(n, n % 2)
            with eng.Fori(2, NB // 2 - 2) as pair:
                body(pair * 2, 0)
                body(pair * 2 + 1, 1)
            for n in range(NB - 4, NB):
                body(n, n % 2)

        def past(n, k):
            return not isinstance(n, int) or n >= k

        with nc.Block() as block:
            @block.sync
            def _(sp):
                def shuffle(n, b):
                    sp.wait_ge(ot_done, n + 1)
                    for r in range(4):
                        sp.dma_start(oT[:, b, r * 32:r * 32 + 32],
                                     ot[32 * r:32 * r + DH, b, :, :, :].rearrange("d j q a -> d j (q a)")
                                     ).then_inc(oT_in[b], 16)

                for what in "kqv":
                    send(sp, keep, 1, what)
                sp.wait_ge(keyed, 1)
                load_keys(sp, keep, 2, 0)

                def body(n, b):
                    if isinstance(n, int) and n == 1:
                        sp.wait_ge(keep["kqv_out"][1], SENT)
                    if not isinstance(n, int) or n + 3 < NB:
                        sp.wait_ge(keyed, n + 2)
                        load_keys(sp, keep, n + 3, 1 - b)
                    if not isinstance(n, int) or n + 2 < NB:
                        sp.wait_ge(scored, 2 * n + 2)
                        load_queries(sp, keep, n + 2, b)
                    if past(n, 2):
                        shuffle(n - 2, b)
                        load_values(sp, keep, n, b)
                    if isinstance(n, int) and n < 3:
                        send(sp, keep, 2, "kqv"[n])
                    if isinstance(n, int) and n == 3:
                        sp.wait_ge(keep["kqv_out"][2], SENT)
                    if isinstance(n, int) and n == NB - GB:
                        w_first, w_first_in = keep["w_first"], keep["w_first_in"]
                        sp.dma_start(w_first[:, 0, :], io["W1"][0]).then_inc(w_first_in, 16)
                        sp.dma_start(w_first[:, 1, :].rearrange("p (k d) -> p k d", k=KF),
                                     io["W2"][0].rearrange("(k p) d -> p k d", p=P)).then_inc(w_first_in, 16)

                loops(sp, body)
                shuffle(NB - 2, 0)
                shuffle(NB - 1, 1)

            @block.tensor
            def _(t):
                t.wait_ge(identr_done, 1)

                def scores(n, b, half):
                    t.wait_ge(keyed, n + 1)
                    t.wait_ge(q_in[b], n * 8 + (16 - 8 * b))
                    for h in range(H):
                        cols = slice(RT * h, RT * h + RT)
                        ins = t.matmul(s_ps[:, half, h, :],
                                       kh[:, b, h, :, :],
                                       qn[:, b, half * HJ:half * HJ + HJ, cols],
                                       start=(h % 8 == 0), stop=False, skip_group_check=True)
                    ins.then_inc(scored, 1)

                def shift(n, half):
                    t.wait_ge(maxed, 2 * n + half + 1)
                    for c in range(2):
                        ins = t.matmul(s_ps[:, half, 8 * c:8 * c + 8, :], identr[:],
                                       negmax[:, half, :].unsqueeze(1).broadcast_to([P, 8, HT]),
                                       start=False, stop=True, skip_group_check=True)
                    ins.then_inc(shifted, 1)

                def mix(n, b, half):
                    t.wait_ge(probed, 2 * n + half + 1)
                    if half == 0:
                        t.wait_ge(val_in[b], n * 8 + (16 - 8 * b))
                        if past(n, 2):
                            t.wait_ge(ot_done, n - 1)
                    cols = slice(half * HT, half * HT + HT)
                    for q in range(4):
                        for r in range(4):
                            ins = t.matmul(o_ps[32 * r:32 * r + 32, b, q, cols], val[:, b, 4 * r + q, :],
                                           prob[:, b, 4 * r + q, cols], start=True, stop=True)
                    ins.then_inc(mixed, 1)

                def project(n, b):
                    t.wait_ge(oT_in[b], n * 32 + (64 - 32 * b))
                    if past(n, 2):
                        t.wait_ge(x_done, n - 1)
                    t.matmul(y_ps[:, b, 0:D], oT[:, b, :], wo[:], start=True, stop=True).then_inc(yed, 1)

                scores(0, 0, 0)
                scores(0, 0, 1)

                def body(n, b):
                    for half in range(2):
                        shift(n, half)
                        if past(n, 1):
                            mix(n - 1, 1 - b, half)
                        if not isinstance(n, int) or n + 1 < NB:
                            t.wait_ge(exped, 2 * n + half + 1)
                            scores(n + 1, 1 - b, half)
                    if past(n, 3):
                        project(n - 3, 1 - b)

                loops(t, body)
                mix(NB - 1, 1, 0)
                mix(NB - 1, 1, 1)
                project(NB - 3, 1)
                project(NB - 2, 0)
                t.wait_ge(exped, 2 * NB)
                for k in range(NG - 1):
                    rows.ln.tensor(t, rows_ps, ident[:], k)
                project(NB - 1, 1)

            @block.vector
            def _(v):
                def maximum(n, half):
                    v.wait_ge(scored, 2 * n + half + 1)
                    if past(n, 1):
                        v.wait_ge(shifted, 2 * n + half - 1)
                    v.tensor_reduce(negmax[:, half, :], s_ps[:, half, :, :].rearrange("p h t -> p t h"),
                                    AX.X, ALU.max, negate=True).then_inc(maxed, 1)

                def totals(n, b, half):
                    v.wait_ge(exped, 2 * n + half + 1)
                    if past(n, 1):
                        v.wait_ge(probed, 2 * n + half - 1)
                    v.tensor_reduce(total[:, half, :], expd[:, b, half, :, :].rearrange("p h t -> p t h"),
                                    AX.X, ALU.add).then_inc(summed, 1)
                    v.wait_ge(summed, 2 * n + half + 1)
                    v.reciprocal(rtotal[:, half, :], total[:, half, :]).then_inc(inverted, 1)

                def residual(n, b):
                    v.wait_ge(yed, n + 1)
                    v.tensor_tensor(x[:, bass.ds(n, 1), :], x[:, bass.ds(n, 1), :],
                                    y_ps[:, bass.ds(b, 1), 0:D], ALU.add).then_inc(x_done, 1)

                def body(n, b):
                    maximum(n, 0)
                    if past(n, 1):
                        totals(n - 1, 1 - b, 1)
                    maximum(n, 1)
                    totals(n, b, 0)
                    if past(n, 4):
                        residual(n - 4, b)

                v.wait_ge(biased, 1)
                loops(v, body)
                totals(NB - 1, 1, 1)
                v.wait_ge(x_done, NB - GB)
                rows.ln.statistics(v, x, 0, NB - GB)
                residual(NB - 4, 0)
                residual(NB - 3, 1)
                rows.ln.normalise(v, x, 0)
                residual(NB - 2, 0)
                rows.ln.normalise(v, x, 1)
                rows.ln.normalise(v, x, 2)
                for k in range(NG - 1):
                    rows.vector(v, k)
                residual(NB - 1, 1)

            @block.scalar
            def _(a):
                def exponentials(n, b, half):
                    a.wait_ge(shifted, 2 * n + half + 1)
                    if past(n, 2):
                        a.wait_ge(probed, 2 * n + half - 3)
                    a.activation(expd[:, b, half, :, :], s_ps[:, half, :, :], ACT.Exp,
                                 scale=float(D) ** -0.5).then_inc(exped, 1)

                def copy_out(n, b):
                    a.wait_ge(mixed, 2 * n + 2)
                    if past(n, 2):
                        a.wait_ge(yed, n - 1)
                    a.activation(ot[:, b, :, :, :].rearrange("p j q a -> p q j a"),
                                 o_ps[:, b, :, :].rearrange("p q (j a) -> p q j a", a=RT),
                                 ACT.Copy).then_inc(ot_done, 1)

                def arrange_keys(n, b):
                    a.wait_ge(k_in[b], n * 8 + (16 - 8 * b))
                    if past(n, 2):
                        a.wait_ge(scored, 2 * n - 2)
                    a.activation(kh[0:KS, b, :, :, :],
                                 kn[:, b, :, :].rearrange("k l (h b) -> k h b l", b=RT),
                                 ACT.Copy).then_inc(keyed, 1)

                a.activation(identr[:], ident[:], ACT.Copy).then_inc(identr_done, 1)
                arrange_keys(0, 0)
                arrange_keys(1, 1)

                def body(n, b):
                    exponentials(n, b, 0)
                    if past(n, 2):
                        copy_out(n - 2, b)
                    exponentials(n, b, 1)
                    if not isinstance(n, int) or n + 2 < NB:
                        arrange_keys(n + 2, b)

                loops(a, body)
                copy_out(NB - 2, 0)
                copy_out(NB - 1, 1)
                for k in range(NG - 1):
                    rows.scalar(a, rows_ps, k)

            @block.gpsimd
            def _(g):
                g.tensor_tensor(x[:], x[:], bo_rows[:].unsqueeze(1).broadcast_to([P, NB, D]),
                                ALU.add).then_inc(biased, 1)

                def probabilities(n, b, half):
                    g.wait_ge(inverted, 2 * n + half + 1)
                    if past(n, 2):
                        g.wait_ge(mixed, 2 * n + half - 3)
                    g.tensor_tensor(prob[:, b, :, half * HT:half * HT + HT], expd[:, b, half, :, :],
                                    rtotal[:, half, :].unsqueeze(1).broadcast_to([P, H, HT]),
                                    ALU.mult).then_inc(probed, 1)

                def body(n, b):
                    probabilities(n, b, 0)
                    probabilities(n, b, 1)

                loops(g, body)
                rows.ln.gpsimd(g, 0, NG - 1)
                cut, w_first = keep["cut"], keep["w_first"]
                g.memset(cut.zeros[:], 0.0).then_inc(cut.zeroed, 1)
                g.wait_ge(cut.zeroed, 1)
                g.wait_ge(keep["w_first_in"], 32)
                split_weights(g, w_first[:, 0, :], cut.zeros[:], cut.w1_hi[:, 0, :], cut.w1_lo[:, 0, :],
                              cut.w1_hi_done, cut.w1_lo_done, 1)
                split_weights(g, w_first[:, 1, :].rearrange("p (k d) -> p k d", k=KF),
                              cut.zeros[:].rearrange("p (k d) -> p k d", k=KF),
                              cut.w2_hi[:, 0, :, :], cut.w2_lo[:, 0, :, :], cut.w2_hi_done, cut.w2_lo_done, 1)


GATE_ROWS = P // NG


class Gate:

    def __init__(self, nc, ctx, name):
        def sb(n, shape, dt=F32):
            return ctx.enter_context(nc.sbuf_tensor(f"{name}_{n}", shape, dt))

        def sem(n):
            return nc.alloc_semaphore(f"{name}_{n}")

        self.wr = sb("wr", [P, E])
        self.logit = sb("logit", [P, NB, E])
        self.top = sb("top", [P, NB, 8])
        self.away = sb("away", [P, NB, E])
        self.expd = sb("expd", [P, NB, E])
        self.kept = sb("kept", [P, NB, E])
        self.total = sb("total", [P, NB])
        self.rtotal = sb("rtotal", [P, NB])
        self.gate = sb("gate", [P, NB, GATE_ROWS])
        self.gateT = sb("gateT", [P, GT])
        self.cleared = sem("cleared")
        self.wr_in, self.logits, self.away_done = sem("wr_in"), sem("logits"), sem("away_done")
        self.exped, self.gated, self.turned = sem("exped"), sem("gated"), sem("turned")
        self.gateT_done, self.gateT_out, self.step = sem("gateT_done"), sem("gateT_out"), sem("step")
        self.steps = 0

    def then(self, v, ins):
        self.steps += 1
        ins.then_inc(self.step, 1)
        v.wait_ge(self.step, self.steps)

    def tensor_logits(self, t, psum, xnT, xnT_done, k):
        t.wait_ge(self.wr_in, 16)
        t.wait_ge(xnT_done, k + 1)
        for n in range(GB * k, GB * k + GB):
            ins = t.matmul(psum[:, n * E:n * E + E], xnT[:, n * T:n * T + T], self.wr[:],
                           start=True, stop=True)
        ins.then_inc(self.logits, 1)

    def gpsimd_clear(self, g):
        g.memset(self.gate[:], 0.0).then_inc(self.cleared, 1)

    def tensor_turn(self, t, bank, ident):
        t.wait_ge(self.gated, 1)
        for n in range(NB):
            rows = slice(n // GB * GATE_ROWS, (n // GB + 1) * GATE_ROWS)
            ins = t.matmul(bank[rows, n % GB * T:n % GB * T + T], self.gate[:, n, :], ident,
                           start=True, stop=True)
        ins.then_inc(self.turned, 1)

    def scalar_exp(self, a):
        a.wait_ge(self.away_done, 1)
        a.activation(self.expd[:], self.away[:], ACT.Exp).then_inc(self.exped, 1)

    def scalar_turned(self, a, bank):
        a.wait_ge(self.turned, 1)
        a.activation(self.gateT[:], bank, ACT.Copy).then_inc(self.gateT_done, 1)

    def sync_out(self, sp, gate_dram):
        sp.wait_ge(self.gateT_done, 1)
        sp.dma_start(gate_dram, self.gateT[:]).then_inc(self.gateT_out, 16)
        sp.wait_ge(self.gateT_out, 16)


def load_gate_row(eng, gate_dram, e, dst, done):
    row = gate_dram.rearrange("(k r) t -> r k t", r=GATE_ROWS)[bass.ds(e, 1)]
    eng.dma_start(dst.rearrange("p (k t) -> p k t", k=NG), row.broadcast_to([P, NG, GT])).then_inc(done, 16)


def split_weights(eng, raw, zeros, hi, lo, hi_done, lo_done, count):
    eng.tensor_tensor(hi, raw, zeros, ALU.add).then_inc(hi_done, 1)
    eng.wait_ge(hi_done, count)
    eng.tensor_tensor(lo, raw, hi.bitcast(F32), ALU.subtract).then_inc(lo_done, 1)


def three_passes(t, out, w_hi, w_lo, x_hi, x_lo, start, stop, **kw):
    t.matmul(out, w_hi, x_hi, start=start, stop=False, **kw)
    t.matmul(out, w_hi, x_lo, start=False, stop=False, **kw)
    return t.matmul(out, w_lo, x_hi, start=False, stop=stop, **kw)


class CutWeights:

    def __init__(self, nc, ctx):
        def sb(n, shape, dt=F32R):
            return ctx.enter_context(nc.sbuf_tensor(f"b_{n}", shape, dt))

        self.zeros, self.zeroed = sb("zeros", [P, FF], F32), nc.alloc_semaphore("b_zeroed")
        self.w1_hi, self.w1_lo = sb("w1_hi", [P, 2, FF]), sb("w1_lo", [P, 2, FF])
        self.w2_hi, self.w2_lo = sb("w2_hi", [P, 2, KF, D]), sb("w2_lo", [P, 2, KF, D])
        self.w1_hi_done, self.w1_lo_done = nc.alloc_semaphore("b_w1_hi_done"), nc.alloc_semaphore("b_w1_lo_done")
        self.w2_hi_done, self.w2_lo_done = nc.alloc_semaphore("b_w2_hi_done"), nc.alloc_semaphore("b_w2_lo_done")


class Rows:

    def __init__(self, nc, ctx, name, ln):
        self.ln = ln
        self.xnT = ctx.enter_context(nc.sbuf_tensor(f"{name}_xnT", [P, TOK], F32))
        self.hi = ctx.enter_context(nc.sbuf_tensor(f"{name}_x_hi", [P, TOK], F32R))
        self.lo = ctx.enter_context(nc.sbuf_tensor(f"{name}_x_lo", [P, TOK], F32R))
        self.hi_done = nc.alloc_semaphore(f"{name}_x_hi_done")
        self.lo_done = nc.alloc_semaphore(f"{name}_x_lo_done")

    def scalar(self, a, psum, k):
        cols = slice(k * GT, k * GT + GT)
        self.ln.scalar(a, psum, self.xnT, k)
        a.wait_ge(self.ln.xnT_done, k + 1)
        a.activation(self.hi[:, cols], self.xnT[:, cols], ACT.Copy).then_inc(self.hi_done, 1)

    def vector(self, v, k):
        cols = slice(k * GT, k * GT + GT)
        v.wait_ge(self.hi_done, k + 1)
        v.tensor_tensor(self.lo[:, cols], self.xnT[:, cols], self.hi[:, cols].bitcast(F32),
                        ALU.subtract).then_inc(self.lo_done, 1)


FF = 512
KF = FF // P
UNITS = NG * KF


def experts_layer0(nc, io, keep):
    with ExitStack() as ctx:
        def sb(n, shape, dt=F32):
            return ctx.enter_context(nc.sbuf_tensor(n, shape, dt))

        def sem(n):
            return nc.alloc_semaphore(n)

        x, ident, gate_dram = keep["x"], keep["ident"], keep["gate_dram"]
        rows, ln, w_first, cut = keep["rows0"], keep["ln_experts0"], keep["w_first"], keep["cut"]
        xnT, x_hi, x_lo = rows.xnT, rows.hi, rows.lo
        gate = Gate(nc, ctx, "b_gate")
        br_rows = sb("b_br_rows", [P, E])
        zeros = cut.zeros
        b1, b2, b1_now = sb("b_b1", [P, E, KF]), sb("b_b2", [P, E]), sb("b_b1_now", [P, 2, KF])
        w1, w2 = sb("b_w1", [P, 2, FF]), sb("b_w2", [P, 2, KF, D])
        w1_hi, w1_lo, w2_hi, w2_lo = cut.w1_hi, cut.w1_lo, cut.w2_hi, cut.w2_lo
        inner = sb("b_inner", [P, 2, KF, GT])
        in_hi, in_lo = sb("b_in_hi", [P, 2, KF, GT], F32R), sb("b_in_lo", [P, 2, KF, GT], F32R)
        gate_rows = sb("b_gate_rows", [P, 2, TOK])
        part = sb("b_part", [P, 2, GT])
        acc = sb("b_acc", [P, TOK])
        up_ps = ctx.enter_context(nc.psum_tensor("b_up", [P, KF, GT], F32))
        down_ps = ctx.enter_context(nc.psum_tensor("b_down", [P, 2, GT], F32))
        tr_ps = ctx.enter_context(nc.psum_tensor("b_tr", [P, 2, GT], F32))
        small_in, b1_set = sem("b_small_in"), sem("b_b1_set")
        w_in = [sem("b_w_in0"), sem("b_w_in1")]
        rows_in = [sem("b_rows_in0"), sem("b_rows_in1")]
        w1_hi_done, w1_lo_done, w2_hi_done, w2_lo_done = cut.w1_hi_done, cut.w1_lo_done, cut.w2_hi_done, cut.w2_lo_done
        upped, innered, in_hi_done, in_lo_done = (sem("b_upped"), sem("b_innered"), sem("b_in_hi_done"),
                                                  sem("b_in_lo_done"))
        downed, parted, acced = sem("b_downed"), sem("b_parted"), sem("b_acced")
        turned, x_done = sem("b_turned"), sem("b_x_done")

        def experts(eng, body):
            body(0, 0)
            body(1, 1)
            with eng.Fori(1, E // 2 - 1) as pair:
                body(pair * 2, 0)
                body(pair * 2 + 1, 1)
            body(E - 2, 0)
            body(E - 1, 1)

        def first(e):
            return isinstance(e, int) and e == 0

        def last(e):
            return isinstance(e, int) and e == E - 1

        with nc.Block() as block:
            @block.sync
            def _(sp):
                sp.dma_start(gate.wr[:], io["Wr0"]).then_inc(gate.wr_in, 16)
                sp.dma_start(br_rows[:], io["br0"].broadcast_to([P, E])).then_inc(small_in, 16)
                sp.dma_start(b1[:], io["b1"]).then_inc(small_in, 16)
                sp.dma_start(b2[:], io["b2"]).then_inc(small_in, 16)

                def load_weights(e, b):
                    sp.dma_start(w1[:, b, :].unsqueeze(1), io["W1"][bass.ds(e, 1)].rearrange("e c f -> c e f")
                                 ).then_inc(w_in[b], 16)
                    sp.dma_start(w2[:, b, :, :], io["W2"][bass.ds(e, 1)].rearrange("e (k p) d -> p (e k) d", p=P)
                                 ).then_inc(w_in[b], 16)

                def load_rows(e, b):
                    load_gate_row(sp, gate_dram, e, gate_rows[:, b, :], rows_in[b])

                load_weights(1, 1)
                load_weights(2, 0)
                gate.sync_out(sp, gate_dram)
                load_rows(0, 0)
                load_rows(1, 1)
                sp.wait_ge(w2_lo_done, 1)
                sp.dma_start(w_first[:], io["wK"].rearrange("c (i f) -> c i f", i=2)).then_inc(keep["wk_in"], 16)

                def refill(e, b):
                    if not first(e):
                        sp.wait_ge(w2_lo_done, e + 1)
                        load_weights(e + 2, b)
                    if first(e):
                        sp.wait_ge(acced, NG)
                    else:
                        sp.wait_ge(parted, (e + 1) * NG)
                    load_rows(e + 2, b)

                refill(0, 0)
                refill(1, 1)
                with sp.Fori(1, E // 2 - 1) as pair:
                    refill(pair * 2, 0)
                    refill(pair * 2 + 1, 1)

            @block.gpsimd
            def _(g):
                zeros2 = zeros[:].rearrange("p (k d) -> p k d", k=KF)
                ln.gpsimd(g, NG - 1)
                gate.gpsimd_clear(g)

                def body(e, b):
                    if first(e):
                        return
                    g.wait_ge(w_in[b], e * 16 + 16 * b)
                    if not (isinstance(e, int) and e < 2):
                        g.wait_ge(downed, (e - 1) * NG)
                    split_weights(g, w1[:, b, :], zeros[:], w1_hi[:, b, :], w1_lo[:, b, :],
                                  w1_hi_done, w1_lo_done, e + 1)
                    split_weights(g, w2[:, b, :, :], zeros2, w2_hi[:, b, :, :], w2_lo[:, b, :, :],
                                  w2_hi_done, w2_lo_done, e + 1)

                experts(g, body)

            @block.tensor
            def _(t):
                def up(e, b, k):
                    if k == 0:
                        t.wait_ge(w1_lo_done, e + 1)
                    if first(e):
                        t.wait_ge(rows.lo_done, k + 1)
                    for c in range(KF):
                        if not (first(e) and k == 0):
                            t.wait_ge(innered, e * UNITS + (k * KF + c - KF + 1))
                        cols = slice(k * GT, k * GT + GT)
                        chunk = slice(c * P, c * P + P)
                        three_passes(t, up_ps[:, c, :], w1_hi[:, b, chunk], w1_lo[:, b, chunk],
                                     x_hi[:, cols], x_lo[:, cols], True, True).then_inc(upped, 1)

                def down(e, b, k):
                    if k == 0:
                        t.wait_ge(w2_lo_done, e + 1)
                    if not (first(e) and k < 2):
                        t.wait_ge(parted, e * NG + (k - 1))
                    for c in range(KF):
                        t.wait_ge(in_lo_done, e * UNITS + (k * KF + c + 1))
                        ins = three_passes(t, down_ps[:, k % 2, :], w2_hi[:, b, c, :], w2_lo[:, b, c, :],
                                           in_hi[:, k % 2, c, :], in_lo[:, k % 2, c, :],
                                           c == 0, c == KF - 1)
                    ins.then_inc(downed, 1)

                def turn_back(k):
                    t.wait_ge(acced, (E - 1) * NG + k + 1)
                    if k >= 2:
                        t.wait_ge(x_done, k - 1)
                    for m in range(GB):
                        n = GB * k + m
                        ins = t.transpose(tr_ps[:, k % 2, m * T:m * T + T], acc[:, n * T:n * T + T], ident[:])
                    ins.then_inc(turned, 1)

                def body(e, b):
                    for k in range(NG):
                        up(e, b, k)
                        if first(e) and k == 0:
                            ln.tensor(t, tr_ps, ident[:], NG - 1)
                            for j in range(NG):
                                gate.tensor_logits(t, tr_ps[:, 0, :], xnT, ln.xnT_done, j)
                        if k:
                            down(e, b, k - 1)
                        if first(e) and k == 1:
                            gate.tensor_turn(t, tr_ps[:, 1, :], ident[:])
                        if k == 0 and not first(e):
                            down(e - 1, 1 - b, NG - 1)
                        if last(e) and k >= 2:
                            turn_back(k - 2)

                experts(t, body)
                down(E - 1, 1, NG - 1)
                turn_back(NG - 2)
                turn_back(NG - 1)

            @block.scalar
            def _(a):
                def round_inner(e, unit):
                    k, c = unit // KF, unit % KF
                    a.wait_ge(innered, e * UNITS + (unit + 1))
                    if not (first(e) and k < 2):
                        a.wait_ge(downed, e * NG + (k - 1))
                    a.activation(in_hi[:, k % 2, c, :], inner[:, k % 2, c, :], ACT.Copy).then_inc(in_hi_done, 1)

                a.wait_ge(small_in, 48)

                def body(e, b):
                    a.activation(b1_now[:, b, :].unsqueeze(1), b1[:, bass.ds(e, 1), :], ACT.Copy).then_inc(b1_set, 1)
                    a.wait_ge(b1_set, e + 1)
                    for unit in range(UNITS):
                        k, c = unit // KF, unit % KF
                        a.wait_ge(upped, e * UNITS + (unit + 1))
                        if not (first(e) and k < 2):
                            a.wait_ge(in_lo_done, e * UNITS + (unit - 2 * KF + 1))
                        a.activation(inner[:, k % 2, c, :], up_ps[:, c, :], ACT.Gelu,
                                     bias=b1_now[:, b, c:c + 1]).then_inc(innered, 1)
                        if unit and not (first(e) and unit == KF):
                            round_inner(e, unit - 1)
                        if first(e) and unit == KF - 1:
                            round_inner(e, unit)
                            rows.scalar(a, tr_ps, NG - 1)
                            gate.scalar_exp(a)
                        if first(e) and unit == 2 * KF + 1:
                            gate.scalar_turned(a, tr_ps[:, 1, :])
                    round_inner(e, UNITS - 1)

                experts(a, body)

            @block.vector
            def _(v):
                ln.statistics(v, x, NB - GB)
                ln.normalise(v, x, NG - 1)

                def gate_weights():
                    v.wait_ge(small_in, 48)
                    v.wait_ge(gate.logits, NG)
                    logits = tr_ps[:, 0, 0:NB * E].rearrange("p (n e) -> p n e", e=E)
                    gate.then(v, v.tensor_tensor(gate.logit[:], logits,
                                                 br_rows[:].unsqueeze(1).broadcast_to([P, NB, E]), ALU.add))
                    for n in range(NB):
                        ins = v.max(gate.top[:, n, :], gate.logit[:, n, :])
                    gate.then(v, ins)
                    v.tensor_tensor(gate.away[:], gate.logit[:], gate.top[:, :, 0:1].broadcast_to([P, NB, E]),
                                    ALU.subtract).then_inc(gate.away_done, 1)
                    gate.then(v, v.tensor_tensor(gate.kept[:], gate.logit[:],
                                                 gate.top[:, :, 1:2].broadcast_to([P, NB, E]), ALU.is_ge))
                    v.wait_ge(gate.exped, 1)
                    gate.then(v, v.tensor_tensor(gate.kept[:], gate.kept[:], gate.expd[:], ALU.mult))
                    gate.then(v, v.tensor_reduce(gate.total[:], gate.kept[:], AX.X, ALU.add))
                    gate.then(v, v.reciprocal(gate.rtotal[:], gate.total[:]))
                    v.wait_ge(gate.cleared, 1)
                    v.tensor_tensor(gate.gate[:, :, 0:E], gate.kept[:],
                                    gate.rtotal[:].unsqueeze(2).broadcast_to([P, NB, E]),
                                    ALU.mult).then_inc(gate.gated, 1)

                def rest_inner(e, unit):
                    k, c = unit // KF, unit % KF
                    v.wait_ge(in_hi_done, e * UNITS + (unit + 1))
                    if not (first(e) and k < 2):
                        v.wait_ge(downed, e * NG + (k - 1))
                    v.tensor_tensor(in_lo[:, k % 2, c, :], inner[:, k % 2, c, :],
                                    in_hi[:, k % 2, c, :].bitcast(F32), ALU.subtract).then_inc(in_lo_done, 1)

                def weigh_first(k):
                    cols = slice(k * GT, k * GT + GT)
                    v.wait_ge(rows_in[0], 16)
                    v.wait_ge(parted, k + 1)
                    v.tensor_tensor(acc[:, cols], acc[:, cols], gate_rows[:, 0, cols],
                                    ALU.mult).then_inc(acced, 1)

                def weigh(e, b, k):
                    cols = slice(k * GT, k * GT + GT)
                    v.wait_ge(downed, e * NG + (k + 1))
                    if first(e):
                        v.tensor_scalar(acc[:, cols], down_ps[:, k % 2, :], b2[:, 0:1], None,
                                        ALU.add).then_inc(parted, 1)
                        return
                    if k == 0:
                        v.wait_ge(rows_in[b], e * 8 + (16 - 8 * b))
                    v.scalar_tensor_tensor(part[:, k % 2, :], down_ps[:, k % 2, :], b2[:, bass.ds(e, 1)],
                                           gate_rows[:, b, cols], ALU.add, ALU.mult).then_inc(parted, 1)
                    v.wait_ge(parted, e * NG + (k + 1))
                    v.wait_ge(acced, (e - 1) * NG + (k + 1))
                    v.tensor_tensor(acc[:, cols], acc[:, cols], part[:, k % 2, :], ALU.add).then_inc(acced, 1)

                def add_to_x(k):
                    v.wait_ge(turned, k + 1)
                    v.tensor_tensor(x[:, GB * k:GB * k + GB, :], x[:, GB * k:GB * k + GB, :],
                                    tr_ps[:, k % 2, :].rearrange("p (m d) -> p m d", m=GB),
                                    ALU.add).then_inc(x_done, 1)

                def body(e, b):
                    for k in range(NG):
                        for c in range(KF):
                            rest_inner(e, k * KF + c)
                        if first(e) and k == 0:
                            rows.vector(v, NG - 1)
                            gate_weights()
                        if k:
                            weigh(e, b, k - 1)
                        elif not first(e):
                            weigh(e - 1, 1 - b, NG - 1)
                        if isinstance(e, int) and e == 1 and k == 0:
                            for j in range(NG):
                                weigh_first(j)

                        if last(e) and k == NG - 1:
                            add_to_x(0)

                experts(v, body)
                add_to_x(1)
                weigh(E - 1, 1, NG - 1)
                add_to_x(2)
                add_to_x(3)


H1, DK = 16, 64
HD = H1 * DK
NC = HD // P
HQ = 4
NQ = H1 // HQ


def head(q, j):
    return 2 * HQ * (q // 2) + 2 * j + q % 2


class Batch1:

    def __init__(self, nc, ctx):
        def sb(n, shape, dt=F32):
            return ctx.enter_context(nc.sbuf_tensor(f"f_{n}", shape, dt))

        self.q, self.k = sb("q_now", [P, 2, NC, T]), sb("k_now", [P, 2, NC, T])
        self.cq, self.mask = sb("cq", [P, 2, T]), sb("mask", [P, 2, T], U8)
        self.cq_hi, self.cq_lo = sb("cq_hi", [P, 2, T], F32R), sb("cq_lo", [P, 2, T], F32R)
        self.zeros, self.zeroed = sb("zeros", [P, T]), nc.alloc_semaphore("f_zeroed")
        self.loaded = [nc.alloc_semaphore(f"f_batch_in{b}") for b in range(2)]
        self.hi_done, self.lo_done = nc.alloc_semaphore("f_cq_hi_done"), nc.alloc_semaphore("f_cq_lo_done")

    def load(self, sp, io, keep, n, b):
        cols = bass.ds(n * T, T)
        sp.dma_start(self.q[:, b, :, :], keep["qT"][:, :, cols]).then_inc(self.loaded[b], 16)
        sp.dma_start(self.k[:, b, :, :], keep["kT"][:, :, cols]).then_inc(self.loaded[b], 16)
        sp.dma_start(self.cq[:, b, :], io["ctxT"][:, cols]).then_inc(self.loaded[b], 16)
        sp.dma_start(self.mask[:, b, :].unsqueeze(1), io["mask"][bass.ds(n, 1)].rearrange("n t s -> t n s")
                     ).then_inc(self.loaded[b], 16)

    def wait_loaded(self, eng, n, b):
        eng.wait_ge(self.loaded[b], n * 32 + (64 - 32 * b))

    def cut_columns(self, g, n, b):
        self.wait_loaded(g, n, b)
        split_weights(g, self.cq[:, b, :], self.zeros[:], self.cq_hi[:, b, :], self.cq_lo[:, b, :],
                      self.hi_done, self.lo_done, n + 1)


def project_layer1(nc, io, keep):
    with ExitStack() as ctx:
        def sb(n, shape, dt=F32):
            return ctx.enter_context(nc.sbuf_tensor(n, shape, dt))

        def sem(n):
            return nc.alloc_semaphore(n)

        x, ident, kT, qT = (keep[name] for name in ("x", "ident", "kT", "qT"))
        wv_hi, wv_lo, wo = keep["wv_hi"], keep["wv_lo"], keep["wo1"]
        ctxT = keep["batch1"].q[:].rearrange("p b m t -> p (b m t)")
        wq = keep["batch1"].k[:, 0, :, :].rearrange("p m t -> p (m t)")
        ctx_in = [sem(f"c_ctx_in{k}") for k in range(NG)]
        ln = LayerNorm(nc, ctx, "c_ln")
        ln.place_xn(nc, ctx)
        wk, wk_in = keep["w_first"][:].rearrange("p i f -> p (i f)"), keep["wk_in"]
        wv = wk
        wk_hi, wk_lo = sb("c_wk_hi", [P, HD], F32R), sb("c_wk_lo", [P, HD], F32R)
        wq_hi, wq_lo = sb("c_wq_hi", [P, HD], F32R), sb("c_wq_lo", [P, HD], F32R)
        bq, bk, bv, bq8 = sb("c_bq", [P, NC]), sb("c_bk", [P, NC]), sb("c_bv", [P, NC]), sb("c_bq8", [P, NC])
        bo_rows, bias_rows = sb("c_bo_rows", [P, D]), sb("c_bias_rows", [P, D])
        hi, lo = sb("c_hi", [P, 2, GT], F32R), sb("c_lo", [P, 2, GT], F32R)
        tr_ps = ctx.enter_context(nc.psum_tensor("c_tr", [P, 2, GT], F32))
        out_ps = ctx.enter_context(nc.psum_tensor("c_out", [P, 4, GT], F32))
        bias_ps = ctx.enter_context(nc.psum_tensor("c_bias", [P, GT], F32))
        w_in, wv_in = sem("c_w_in"), sem("c_wv_in")
        wk_hi_done, wk_lo_done = sem("c_wk_hi_done"), sem("c_wk_lo_done")
        wq_hi_done, wq_lo_done = sem("c_wq_hi_done"), sem("c_wq_lo_done")
        wv_hi_done, wv_lo_done = sem("c_wv_hi_done"), sem("c_wv_lo_done")
        bq8_done = sem("c_bq8_done")
        hi_done, lo_done, unit_mm = sem("c_hi_done"), sem("c_lo_done"), sem("c_unit_mm")
        odd_out, even_out = sem("c_odd_out"), sem("c_even_out")
        biased, bias_done, x_bias = sem("c_biased"), sem("c_bias_done"), sem("c_x_bias")

        def units(i):
            return [(i * NC + m, m) for m in range(NC)]

        def target(i, m):
            return (kT if i < NG else qT)[:, m, i % NG * GT:i % NG * GT + GT]

        with nc.Block() as block:
            @block.sync
            def _(sp):
                def load_ctx(k):
                    cols = slice(k * GT, k * GT + GT)
                    sp.dma_start(ctxT[:, cols], io["ctxT"][:, cols]).then_inc(ctx_in[k], 16)

                load_ctx(0)
                load_ctx(1)
                for dst, src in ((wq, "wQ"), (bq[:], "bQ"), (bk[:], "bK"), (bv[:], "bV")):
                    sp.dma_start(dst, io[src]).then_inc(w_in, 16)
                sp.dma_start(wo[:], io["wO"].rearrange("(m p) o -> p m o", p=P)).then_inc(w_in, 16)
                sp.dma_start(bo_rows[:], io["bO"].broadcast_to([P, D])).then_inc(w_in, 16)
                load_ctx(2)
                load_ctx(3)
                sp.wait_ge(wk_lo_done, 1)
                sp.dma_start(wv, io["wV"]).then_inc(wv_in, 16)
                sp.wait_ge(odd_out, (NG + 1) * NC // 2)
                sp.wait_ge(even_out, (NG + 1) * NC // 2)
                for n in range(2):
                    keep["batch1"].load(sp, io, keep, n, n)

            @block.gpsimd
            def _(g):
                ln.gpsimd(g)
                g.wait_ge(wq_hi_done, 1)
                g.tensor_tensor(wq_lo[:], wq, wq_hi[:].bitcast(F32), ALU.subtract).then_inc(wq_lo_done, 1)
                g.wait_ge(wv_hi_done, 1)
                g.tensor_tensor(wv_lo[:], wv, wv_hi[:].bitcast(F32), ALU.subtract).then_inc(wv_lo_done, 1)
                g.wait_ge(ln.xn_done, NB)
                g.wait_ge(bias_done, 1)
                g.tensor_tensor(x[:], x[:], bias_rows[:].unsqueeze(1).broadcast_to([P, NB, D]),
                                ALU.add).then_inc(x_bias, 1)
                batch = keep["batch1"]
                g.memset(batch.zeros[:], 0.0).then_inc(batch.zeroed, 1)
                g.wait_ge(batch.zeroed, 1)
                batch.cut_columns(g, 0, 0)

            @block.tensor
            def _(t):
                def group(i):
                    w_hi, w_lo = (wk_hi, wk_lo) if i < NG else (wq_hi, wq_lo)
                    if i == 0:
                        t.wait_ge(wk_lo_done, 1)
                    if i == NG:
                        t.wait_ge(wq_lo_done, 1)
                    t.wait_ge(lo_done, i + 1)
                    for u, m in units(i):
                        if u >= 4:
                            t.wait_ge(odd_out if u % 2 else even_out, (u - 4) // 2 + 1)
                        chunk = slice(m * P, m * P + P)
                        three_passes(t, out_ps[:, u % 4, :], w_hi[:, chunk], w_lo[:, chunk],
                                     hi[:, i % 2, :], lo[:, i % 2, :], True, True).then_inc(unit_mm, 1)

                def turn(k):
                    if k >= 2:
                        t.wait_ge(lo_done, NG + k - 1)
                    for m in range(GB):
                        n = GB * k + m
                        t.wait_ge(ln.xn_done, n + 1)
                        ins = t.transpose(tr_ps[:, k % 2, m * T:m * T + T], ln.xn[:, n, :], ident[:])
                    ins.then_inc(ln.transposed, 1)

                group(0)
                group(1)
                t.wait_ge(w_in, 16 * 6)
                for m in range(NC):
                    ins = t.matmul(bias_ps[:, 0:D], bv[:, m:m + 1].broadcast_to([P, P]), wo[:, m, :],
                                   start=(m == 0), stop=(m == NC - 1))
                ins.then_inc(biased, 1)
                for k in range(NG):
                    if k < 2:
                        group(k + 2)
                    turn(k)
                    if k:
                        group(NG + k - 1)
                group(2 * NG - 1)

            @block.scalar
            def _(a):
                a.wait_ge(wk_in, 16)
                a.activation(wk_hi[:], wk, ACT.Copy).then_inc(wk_hi_done, 1)

                def round_group(i):
                    if i >= 2:
                        a.wait_ge(unit_mm, (i - 1) * NC)
                    if i < NG:
                        a.wait_ge(ctx_in[i], 16)
                        src = ctxT[:, i * GT:i * GT + GT]
                    else:
                        a.wait_ge(ln.transposed, i - NG + 1)
                        src = tr_ps[:, i % 2, :]
                    a.activation(hi[:, i % 2, :], src, ACT.Copy).then_inc(hi_done, 1)

                def odd_units(i):
                    for u, m in units(i)[1::2]:
                        a.wait_ge(unit_mm, u + 1)
                        if i < NG:
                            a.activation(target(i, m), out_ps[:, u % 4, :], ACT.Identity,
                                         bias=bk[:, m:m + 1]).then_inc(odd_out, 1)
                        else:
                            a.activation(target(i, m), out_ps[:, u % 4, :], ACT.Identity, bias=bq8[:, m:m + 1],
                                         scale=float(DK) ** -0.5).then_inc(odd_out, 1)

                round_group(0)
                round_group(1)
                a.wait_ge(w_in, 16 * 6)
                a.activation(wq_hi[:], wq, ACT.Copy).then_inc(wq_hi_done, 1)
                a.activation(bq8[:], bq[:], ACT.Copy, scale=float(DK) ** -0.5).then_inc(bq8_done, 1)
                a.wait_ge(bq8_done, 1)
                for i in range(2 * NG):
                    odd_units(i)
                    if i == 1:
                        a.wait_ge(wv_in, 16)
                        a.activation(wv_hi[:], wv, ACT.Copy).then_inc(wv_hi_done, 1)
                    if i + 2 < 2 * NG:
                        round_group(i + 2)

            @block.vector
            def _(v):
                def rest_group(i):
                    src = ctxT[:, i * GT:i * GT + GT] if i < NG else tr_ps[:, i % 2, :]
                    v.wait_ge(hi_done, i + 1)
                    v.tensor_tensor(lo[:, i % 2, :], src, hi[:, i % 2, :].bitcast(F32),
                                    ALU.subtract).then_inc(lo_done, 1)

                def even_units(i):
                    for u, m in units(i)[0::2]:
                        v.wait_ge(unit_mm, u + 1)
                        if i < NG:
                            v.tensor_scalar(target(i, m), out_ps[:, u % 4, :], bk[:, m:m + 1], None,
                                            ALU.add).then_inc(even_out, 1)
                        else:
                            v.tensor_scalar(target(i, m), out_ps[:, u % 4, :], bq[:, m:m + 1], float(DK) ** -0.5,
                                            ALU.add, ALU.mult).then_inc(even_out, 1)

                v.wait_ge(wk_hi_done, 1)
                v.tensor_tensor(wk_lo[:], wk, wk_hi[:].bitcast(F32), ALU.subtract).then_inc(wk_lo_done, 1)
                rest_group(0)
                ln.statistics(v, x)
                rest_group(1)
                v.wait_ge(w_in, 16 * 6)
                for i in range(2 * NG):
                    even_units(i)
                    if i < NG:
                        ln.normalise(v, x, i)
                    if i == 1:
                        v.wait_ge(biased, 1)
                        v.tensor_tensor(bias_rows[:], bias_ps[:, 0:D], bo_rows[:], ALU.add).then_inc(bias_done, 1)
                    if i + 2 < 2 * NG:
                        rest_group(i + 2)


def attend_layer1(nc, io, keep):
    with ExitStack() as ctx:
        def sb(n, shape, dt=F32):
            return ctx.enter_context(nc.sbuf_tensor(n, shape, dt))

        def sem(n):
            return nc.alloc_semaphore(n)

        x, ident = keep["x"], keep["ident"]
        wv_hi, wv_lo, wo = keep["wv_hi"], keep["wv_lo"], keep["wo1"]
        batch = keep["batch1"]
        q_now, k_now, mask = batch.q, batch.k, batch.mask
        cq_hi, cq_lo, cq_lo_done = batch.cq_hi, batch.cq_lo, batch.lo_done
        tick, fill = sb("f_tick", [P, 1]), sb("f_fill", [P, 1])
        val = sb("f_val", [P, 2, HD])
        negmax, total = sb("f_negmax", [P, NQ, HQ]), sb("f_total", [P, NQ, HQ])
        rtotal = sb("f_rtotal", [P, NQ, HQ])
        expd, prob = sb("f_expd", [P, NQ, HQ, T]), sb("f_prob", [P, 2, HQ, T])
        probT = sb("f_probT", [P, NQ, HQ, T])
        outT = sb("f_outT", [P, 2, NC // 2, T])
        s_ps = ctx.enter_context(nc.psum_tensor("f_s", [P, 2, HQ, T], F32))
        t_ps = ctx.enter_context(nc.psum_tensor("f_t", [P, 2, HQ, T], F32))
        o_ps = ctx.enter_context(nc.psum_tensor("f_o", [P, 2, NC // 2, T], F32))
        v_ps = ctx.enter_context(nc.psum_tensor("f_v", [P, GT], F32))
        y_ps = ctx.enter_context(nc.psum_tensor("f_y", [P, GT], F32))
        filled = sem("f_filled")
        val_mm, valued = sem("f_val_mm"), sem("f_valued")
        scored, masked, maxed, exped = sem("f_scored"), sem("f_masked"), sem("f_maxed"), sem("f_exped")
        inverted, probed, turned, probTed = sem("f_inverted"), sem("f_probed"), sem("f_turned"), sem("f_probTed")
        mixed, outTed, yed, x_done = sem("f_mixed"), sem("f_outTed"), sem("f_yed"), sem("f_x_done")

        def loops(eng, body):
            for n in range(4):
                body(n, n % 2)
            with eng.Fori(2, NB // 2 - 1) as pair:
                body(pair * 2, 0)
                body(pair * 2 + 1, 1)
            body(NB - 2, 0)
            body(NB - 1, 1)

        def known(n):
            return isinstance(n, int)

        def before(n, b, q, lag):
            back = (lag - q + NQ - 1) // NQ if lag > q else 0
            n, b, q = n - back, (b + back) % 2, q + back * NQ - lag
            return None if known(n) and n < 0 else (n, b, q)

        with nc.Block() as block:
            @block.sync
            def _(sp):
                w_first, w_first_in = keep["w_first"], keep["w_first_in"]
                sp.dma_start(w_first[:, 0, :], io["Wg"][0]).then_inc(w_first_in, 16)
                sp.dma_start(w_first[:, 1, :], io["Wu"][0]).then_inc(w_first_in, 16)
                with sp.Fori(0, NB // 2 - 1) as pair:
                    for b in range(2):
                        n = pair * 2 + b
                        sp.wait_ge(masked, (n + 1) * NQ)
                        batch.load(sp, io, keep, n + 2, b)

            @block.gpsimd
            def _(g):
                g.memset(fill[:], -10000.0).then_inc(filled, 1)

                def columns(n, b):
                    if not (known(n) and n < 2):
                        g.wait_ge(val_mm, (n - 1) * 2)
                    batch.cut_columns(g, n, b)

                def body(n, b):
                    if not (known(n) and n + 1 == NB):
                        columns(n + 1, 1 - b)
                    for q in range(NQ):
                        g.wait_ge(inverted, n * NQ + (q + 1))
                        if not (known(n) and n == 0 and q < 2):
                            g.wait_ge(turned, n * NQ + (q - 1))
                        g.tensor_tensor(prob[:, q % 2, :, :], expd[:, q, :, :],
                                        rtotal[:, q, :].unsqueeze(2).broadcast_to([P, HQ, T]),
                                        ALU.mult).then_inc(probed, 1)

                loops(g, body)
                keep["ln_experts1"].gpsimd(g, 0, NG - 1)

            @block.tensor
            def _(t):
                def values(n, b, half):
                    if half == 0:
                        t.wait_ge(cq_lo_done, n + 1)
                    if not (known(n) and n == 0 and half == 0):
                        t.wait_ge(valued, 2 * n + half)
                    cols = slice(half * GT, half * GT + GT)
                    three_passes(t, v_ps[:], cq_hi[:, b, :], cq_lo[:, b, :], wv_hi[:, cols], wv_lo[:, cols],
                                 True, True).then_inc(val_mm, 1)

                def scores(n, b, q):
                    if q == 0:
                        batch.wait_loaded(t, n, b)
                    if not (known(n) and n == 0 and q < 2):
                        t.wait_ge(exped, n * NQ + (q - 1))
                    for j in range(HQ):
                        m, rows = head(q, j) // 2, slice(q % 2 * DK, q % 2 * DK + DK)
                        ins = t.matmul(s_ps[:, q % 2, j, :], q_now[rows, b, m, :], k_now[rows, b, m, :],
                                       start=True, stop=True)
                    ins.then_inc(scored, 1)

                def turn(n, b, q):
                    t.wait_ge(probed, n * NQ + (q + 1))
                    if not (known(n) and n == 0 and q < 2):
                        t.wait_ge(probTed, n * NQ + (q - 1))
                    for j in range(HQ):
                        ins = t.transpose(t_ps[:, q % 2, j, :], prob[:, q % 2, j, :], ident[:])
                    ins.then_inc(turned, 1)

                def mix(n, b, half):
                    t.wait_ge(probTed, n * NQ + (2 * half + 2))
                    if half == 0:
                        t.wait_ge(valued, 2 * n + 2)
                    if not (known(n) and n == 0):
                        t.wait_ge(outTed, 2 * n + half - 1)
                    for j in range(HQ):
                        for side in range(2):
                            h = head(2 * half + side, j)
                            ins = t.matmul(o_ps[side * DK:side * DK + DK, half, j, :],
                                           val[:, b, h * DK:h * DK + DK], probT[:, 2 * half + side, j, :],
                                           start=True, stop=True)
                    ins.then_inc(mixed, 1)

                def project(n):
                    t.wait_ge(outTed, 2 * n + 2)
                    if not (known(n) and n == 0):
                        t.wait_ge(x_done, n)
                    for m in range(NC):
                        ins = t.matmul(y_ps[:, 0:D], outT[:, m // (NC // 2), m % (NC // 2), :], wo[:, m, :],
                                       start=(m == 0), stop=(m == NC - 1))
                    ins.then_inc(yed, 1)

                values(0, 0, 0)
                values(0, 0, 1)

                def body(n, b):
                    for q in range(NQ):
                        scores(n, b, q)
                        if q >= 2 and not (known(n) and n + 1 == NB):
                            values(n + 1, 1 - b, q - 2)
                        at = before(n, b, q, 2)
                        if at:
                            turn(*at)
                        if q % 2 == 0 and not (known(n) and n == 0):
                            mix(n - 1, 1 - b, q // 2)
                        if q == 3 and not (known(n) and n == 0):
                            project(n - 1)

                loops(t, body)
                turn(NB - 1, 1, 2)
                mix(NB - 1, 1, 0)
                turn(NB - 1, 1, 3)
                mix(NB - 1, 1, 1)
                project(NB - 1)

            @block.scalar
            def _(a):
                def exponentials(n, b, q):
                    a.wait_ge(maxed, n * NQ + (q + 1))
                    if not (known(n) and n == 0):
                        a.wait_ge(probed, (n - 1) * NQ + (q + 1))
                    for j in range(HQ):
                        ins = a.activation(expd[:, q, j, :], s_ps[:, q % 2, j, :], ACT.Exp,
                                           bias=negmax[:, q, j:j + 1], accum_out=total[:, q, j:j + 1])
                    ins.then_inc(exped, 1)

                def copy_turned(n, b, q):
                    a.wait_ge(turned, n * NQ + (q + 1))
                    if not (known(n) and n == 0):
                        a.wait_ge(mixed, 2 * n + (q // 2 - 1))
                    a.activation(probT[:, q, :, :], t_ps[:, q % 2, :, :], ACT.Copy).then_inc(probTed, 1)

                def copy_out(n, half):
                    a.wait_ge(mixed, 2 * n + half + 1)
                    if not (known(n) and n == 0):
                        a.wait_ge(yed, n)
                    a.activation(outT[:, half, :, :], o_ps[:, half, :, :], ACT.Copy).then_inc(outTed, 1)

                def body(n, b):
                    for q in range(NQ):
                        at = before(n, b, q, 1)
                        if at:
                            exponentials(*at)
                        at = before(n, b, q, 2)
                        if at:
                            copy_turned(*at)
                        if q % 2 == 0 and not (known(n) and n == 0):
                            copy_out(n - 1, q // 2)

                loops(a, body)
                exponentials(NB - 1, 1, 3)
                copy_turned(NB - 1, 1, 2)
                copy_out(NB - 1, 0)
                copy_turned(NB - 1, 1, 3)
                copy_out(NB - 1, 1)

            @block.vector
            def _(v):
                v.wait_ge(filled, 1)

                def copy_values(n, b, half):
                    v.wait_ge(val_mm, 2 * n + half + 1)
                    if not (known(n) and n < 2):
                        v.wait_ge(mixed, 2 * n + half - 3)
                    v.tensor_copy(val[:, b, half * GT:half * GT + GT], v_ps[:]).then_inc(valued, 1)

                def maximum(n, b, q):
                    v.wait_ge(scored, n * NQ + (q + 1))
                    v.memset(tick[:], 0.0)
                    v.copy_predicated(s_ps[:, q % 2, :, :], mask[:, b, :].unsqueeze(1).broadcast_to([P, HQ, T]),
                                      fill[:].unsqueeze(2).broadcast_to([P, HQ, T])).then_inc(masked, 1)
                    v.wait_ge(masked, n * NQ + (q + 1))
                    if not (known(n) and n == 0):
                        v.wait_ge(exped, (n - 1) * NQ + (q + 1))
                    v.tensor_reduce(negmax[:, q, :], s_ps[:, q % 2, :, :], AX.X, ALU.max,
                                    negate=True).then_inc(maxed, 1)

                def invert(n, b, q):
                    v.wait_ge(exped, n * NQ + (q + 1))
                    if not (known(n) and n == 0):
                        v.wait_ge(probed, (n - 1) * NQ + (q + 1))
                    v.reciprocal(rtotal[:, q, :], total[:, q, :]).then_inc(inverted, 1)

                def residual(n):
                    v.wait_ge(yed, n + 1)
                    v.tensor_tensor(x[:, bass.ds(n, 1), :], x[:, bass.ds(n, 1), :],
                                    y_ps[:, 0:D].unsqueeze(1), ALU.add).then_inc(x_done, 1)

                copy_values(0, 0, 0)
                copy_values(0, 0, 1)

                def body(n, b):
                    for q in range(NQ):
                        maximum(n, b, q)
                        at = before(n, b, q, 1)
                        if at:
                            invert(*at)
                        if q >= 2 and not (known(n) and n + 1 == NB):
                            copy_values(n + 1, 1 - b, q - 2)
                        if q == 0 and not (known(n) and n < 2):
                            residual(n - 2)

                loops(v, body)
                invert(NB - 1, 1, 3)
                v.wait_ge(x_done, NB - 2)
                keep["ln_experts1"].statistics(v, x, 0, NB - GB)
                residual(NB - 2)
                residual(NB - 1)


def experts_layer1(nc, io, keep, out):
    with ExitStack() as ctx:
        def sb(n, shape, dt=F32):
            return ctx.enter_context(nc.sbuf_tensor(n, shape, dt))

        def sem(n):
            return nc.alloc_semaphore(n)

        x, ident, gate_dram = keep["x"], keep["ident"], keep["gate_dram"]
        xnT = sb("d_xnT", [P, TOK])
        x_hi, x_lo = sb("d_x_hi", [P, TOK], F32R), sb("d_x_lo", [P, TOK], F32R)
        ln, w_first, w_first_in = keep["ln_experts1"], keep["w_first"], keep["w_first_in"]
        ln.place_xn(nc, ctx)
        gate = Gate(nc, ctx, "d_gate")
        zeros = sb("d_zeros", [P, FF])
        expert_no = sb("d_expert_no", [P, E])
        ids = sb("d_ids", [P, NB, 8], U32)
        idf = sb("d_idf", [P, NB, 8])
        share, pick = sb("d_share", [P, NB, 2]), sb("d_pick", [P, NB, E])
        w = sb("d_w", [P, 2, 3, FF])
        w_hi, w_lo = sb("d_w_hi", [P, 2, 3, FF], F32R), sb("d_w_lo", [P, 2, 3, FF], F32R)
        gate_rows = sb("d_gate_rows", [P, 2, TOK])
        gx = sb("d_gx", [P, 2, GT])
        gx_hi, gx_lo = sb("d_gx_hi", [P, 2, GT], F32R), sb("d_gx_lo", [P, 2, GT], F32R)
        relu = sb("d_relu", [P, 2, GT])
        TURN_UNIT = 8
        LAG, RING = 3, 8
        inner = sb("d_inner", [P, KF, GT])
        in_hi, in_lo = sb("d_in_hi", [P, RING, GT], F32R), sb("d_in_lo", [P, RING, GT], F32R)
        acc = sb("d_acc", [P, TOK])
        g_ps = ctx.enter_context(nc.psum_tensor("d_g", [P, 2, GT], F32))
        u_ps = ctx.enter_context(nc.psum_tensor("d_u", [P, 2, GT], F32))
        down_ps = ctx.enter_context(nc.psum_tensor("d_down", [P, NG, GT], F32))
        x_hi_done, x_lo_done = sem("d_x_hi_done"), sem("d_x_lo_done")
        wd_first, wd_first_in = sb("d_wd_first", [P, FF]), sem("d_wd_first_in")
        numbered, zeroed = sem("d_numbered"), sem("d_zeroed")
        first_hi_done, first_lo_done = sem("d_first_hi_done"), sem("d_first_lo_done")
        w_in = [sem("d_w_in0"), sem("d_w_in1")]
        rows_in = [sem("d_rows_in0"), sem("d_rows_in1")]
        w_hi_done, w_lo_done = sem("d_w_hi_done"), sem("d_w_lo_done")
        gx_done, gx_hi_done, gx_lo_done = sem("d_gx_done"), sem("d_gx_hi_done"), sem("d_gx_lo_done")
        g_mm, u_mm, relued = sem("d_g_mm"), sem("d_u_mm"), sem("d_relued")
        innered, in_hi_done, in_lo_done = sem("d_innered"), sem("d_in_hi_done"), sem("d_in_lo_done")
        first_out, stored = sem("d_first_out"), sem("d_stored")
        downed, acc_done, turned, x_done = sem("d_downed"), sem("d_acc_done"), sem("d_turned"), sem("d_x_done")

        def experts(eng, body):
            body(0, 0)
            body(1, 1)
            with eng.Fori(1, E // 2 - 1) as pair:
                body(pair * 2, 0)
                body(pair * 2 + 1, 1)
            body(E - 2, 0)
            body(E - 1, 1)

        def first(e):
            return isinstance(e, int) and e == 0

        def after(e, b, k):
            if k + 1 < NG:
                return e, b, k + 1
            return None if isinstance(e, int) and e == E - 1 else (e + 1, 1 - b, 0)

        def last(e):
            return isinstance(e, int) and e == E - 1

        def next_rows(e, b, k):
            at = after(e, b, k)
            return None if at and first(at[0]) else at

        with nc.Block() as block:
            @block.sync
            def _(sp):
                sp.dma_start(gate.wr[:], io["Wr1"]).then_inc(gate.wr_in, 16)

                def load_weights(e, b):
                    one = bass.ds(e, 1)
                    sp.dma_start(w[:, b, 0, :].unsqueeze(1), io["Wg"][one].rearrange("e c f -> c e f")
                                 ).then_inc(w_in[b], 16)
                    sp.dma_start(w[:, b, 1, :].unsqueeze(1), io["Wu"][one].rearrange("e c f -> c e f")
                                 ).then_inc(w_in[b], 16)
                    sp.dma_start(w[:, b, 2, :].rearrange("p (k d) -> p k d", k=KF),
                                 io["Wd"][one].rearrange("e (k p) d -> p (e k) d", p=P)).then_inc(w_in[b], 16)

                def load_rows(e, b):
                    load_gate_row(sp, gate_dram, e, gate_rows[:, b, :], rows_in[b])

                sp.dma_start(wd_first[:].rearrange("p (k d) -> p k d", k=KF),
                             io["Wd"][0].rearrange("(k p) d -> p k d", p=P)).then_inc(wd_first_in, 16)
                load_weights(1, 1)
                load_weights(2, 0)
                gate.sync_out(sp, gate_dram)
                load_rows(0, 0)
                load_rows(1, 1)

                def refill(e, b):
                    if first(e):
                        sp.wait_ge(first_out, NG)
                    else:
                        sp.wait_ge(w_lo_done, e)
                        load_weights(e + 2, b)
                        sp.wait_ge(gx_done, e * NG)
                    load_rows(e + 2, b)

                refill(0, 0)
                refill(1, 1)
                with sp.Fori(1, E // 2 - 1) as pair:
                    refill(pair * 2, 0)
                    refill(pair * 2 + 1, 1)
                for k in range(NG):
                    sp.wait_ge(x_done, k + 1)
                    rows = slice(GB * k, GB * k + GB)
                    sp.dma_start(out[rows].rearrange("n t d -> t n d"), x[:, rows, :]).then_inc(stored, 16)
                sp.wait_ge(stored, 16 * NG)

            @block.gpsimd
            def _(g):
                g.memset(zeros[:], 0.0).then_inc(zeroed, 1)
                g.wait_ge(zeroed, 1)
                g.wait_ge(w_first_in, 32)
                for i in range(3):
                    if i == 2:
                        g.wait_ge(wd_first_in, 16)
                    split_weights(g, wd_first[:] if i == 2 else w_first[:, i, :], zeros[:],
                                  w_hi[:, 0, i, :], w_lo[:, 0, i, :],
                                  first_hi_done, first_lo_done, i + 1)
                    if i == 0:
                        ln.gpsimd(g, NG - 1)
                gate.gpsimd_clear(g)
                for e in range(E):
                    ins = g.memset(expert_no[:, e:e + 1], float(e))
                ins.then_inc(numbered, 1)

                def body(e, b):
                    if first(e):
                        return
                    g.wait_ge(w_in[b], e * 24 + 24 * b)
                    if not (isinstance(e, int) and e < 2):
                        g.wait_ge(downed, (e - 1) * UNITS)
                    split_weights(g, w[:, b, :, :], zeros[:].unsqueeze(1).broadcast_to([P, 3, FF]),
                                  w_hi[:, b, :, :], w_lo[:, b, :, :],
                                  w_hi_done, w_lo_done, e)

                experts(g, body)

            @block.tensor
            def _(t):
                for k in range(NG - 1):
                    ln.tensor(t, down_ps[:, 0:2, :], ident[:], k)

                def up(e, b, k):
                    cols = slice(k * GT, k * GT + GT)
                    if first(e):
                        t.wait_ge(first_lo_done, 1)
                        t.wait_ge(x_lo_done, k + 1)
                    elif k == 0:
                        t.wait_ge(w_lo_done, e)
                    for c in range(KF):
                        unit, chunk = k * KF + c, slice(c * P, c * P + P)
                        if not (first(e) and unit < 2):
                            t.wait_ge(relued, e * UNITS + (unit - 1))
                        three_passes(t, g_ps[:, c % 2, :], w_hi[:, b, 0, chunk], w_lo[:, b, 0, chunk],
                                     x_hi[:, cols], x_lo[:, cols], True, True).then_inc(g_mm, 1)
                        if first(e):
                            rows_hi, rows_lo = x_hi[:, cols], x_lo[:, cols]
                            t.wait_ge(first_lo_done, 2)
                        else:
                            rows_hi, rows_lo = gx_hi[:, k % 2, :], gx_lo[:, k % 2, :]
                            if c == 0:
                                t.wait_ge(gx_lo_done, (e - 1) * NG + (k + 1))
                        if not (first(e) and unit < 2):
                            t.wait_ge(innered, e * UNITS + (unit - 1))
                        three_passes(t, u_ps[:, c % 2, :], w_hi[:, b, 1, chunk], w_lo[:, b, 1, chunk],
                                     rows_hi, rows_lo, True, True).then_inc(u_mm, 1)
                        if first(e) and unit == 1:
                            ln.tensor(t, down_ps[:, 0:2, :], ident[:], NG - 1)
                        if first(e) and unit == 2:
                            for j in range(NG):
                                gate.tensor_logits(t, down_ps[:, 2, :], xnT, ln.xnT_done, j)
                        if first(e) and unit == TURN_UNIT:
                            t.wait_ge(relued, unit)
                            gate.tensor_turn(t, g_ps[:, (unit + 1) % 2, :], ident[:])
                            t.wait_ge(gate.gateT_done, 1)
                        if last(e) and unit in (8, 12):
                            turn_back(unit // KF - 2)
                        if unit >= LAG:
                            down(e, b, unit - LAG)
                        elif not first(e):
                            down(e - 1, 1 - b, UNITS + unit - LAG)

                def down(e, b, unit):
                    k, c = unit // KF, unit % KF
                    t.wait_ge(in_lo_done, e * UNITS + (unit + 1))
                    if first(e):
                        t.wait_ge(first_lo_done, 3)
                    if isinstance(e, int) and e == 1 and c == 0:
                        t.wait_ge(first_out, k + 1)
                    ins = three_passes(t, down_ps[:, k, :], w_hi[:, b, 2, c * P:c * P + P],
                                       w_lo[:, b, 2, c * P:c * P + P],
                                       in_hi[:, unit % RING, :], in_lo[:, unit % RING, :],
                                       isinstance(e, int) and e < 2 and c == 0, False, skip_group_check=True)
                    ins.then_inc(downed, 1)

                def turn_back(k):
                    t.wait_ge(acc_done, k + 1)
                    for m in range(GB):
                        n = GB * k + m
                        ins = t.transpose(down_ps[:, k, m * T:m * T + T], acc[:, n * T:n * T + T], ident[:])
                    ins.then_inc(turned, 1)

                def body(e, b):
                    for k in range(NG):
                        up(e, b, k)

                experts(t, body)
                for unit in range(UNITS - LAG, UNITS):
                    down(E - 1, 1, unit)
                turn_back(NG - 2)
                turn_back(NG - 1)

            @block.scalar
            def _(a):
                def turned_rows(k):
                    ln.scalar(a, down_ps[:, 0:2, :], xnT, k)
                    cols = slice(k * GT, k * GT + GT)
                    a.wait_ge(ln.xnT_done, k + 1)
                    a.activation(x_hi[:, cols], xnT[:, cols], ACT.Copy).then_inc(x_hi_done, 1)

                for k in range(NG - 1):
                    turned_rows(k)

                def round_inner(e, unit):
                    c = unit % KF
                    a.wait_ge(innered, e * UNITS + (unit + 1))
                    if not (first(e) and unit < RING):
                        a.wait_ge(downed, e * UNITS + (unit - RING + 1))
                    a.activation(in_hi[:, unit % RING, :], inner[:, c, :], ACT.Copy).then_inc(in_hi_done, 1)

                def round_rows(e, b, k):
                    a.wait_ge(gx_done, (e - 1) * NG + (k + 1))
                    a.wait_ge(u_mm, e * UNITS + (k - 1) * KF)
                    a.activation(gx_hi[:, k % 2, :], gx[:, k % 2, :], ACT.Copy).then_inc(gx_hi_done, 1)

                def body(e, b):
                    for unit in range(UNITS):
                        k, c = unit // KF, unit % KF
                        if c == 1 and next_rows(e, b, k):
                            round_rows(*next_rows(e, b, k))
                        a.wait_ge(g_mm, e * UNITS + (unit + 1))
                        if not (first(e) and unit < 2):
                            a.wait_ge(innered, e * UNITS + (unit - 1))
                        a.activation(relu[:, c % 2, :], g_ps[:, c % 2, :], ACT.Relu).then_inc(relued, 1)
                        if first(e) and unit == 1:
                            turned_rows(NG - 1)
                        if first(e) and unit == TURN_UNIT:
                            gate.scalar_turned(a, g_ps[:, (unit + 1) % 2, :])
                        if unit:
                            round_inner(e, unit - 1)
                        elif not first(e):
                            round_inner(e - 1, UNITS - 1)
                        if first(e) and unit == 3:
                            gate.scalar_exp(a)

                experts(a, body)
                round_inner(E - 1, UNITS - 1)

            @block.vector
            def _(v):
                def rest_rows(k):
                    cols = slice(k * GT, k * GT + GT)
                    v.wait_ge(x_hi_done, k + 1)
                    v.tensor_tensor(x_lo[:, cols], xnT[:, cols], x_hi[:, cols].bitcast(F32),
                                    ALU.subtract).then_inc(x_lo_done, 1)

                ln.normalise(v, x, 0)
                ln.normalise(v, x, 1)
                ln.statistics(v, x, NB - GB)
                rest_rows(0)
                ln.normalise(v, x, 2)
                ln.normalise(v, x, 3)
                rest_rows(1)
                all_e = [P, NB, E]

                def below_largest():
                    v.wait_ge(gate.logits, NG)
                    logits = down_ps[:, 2, 0:NB * E].rearrange("p (n e) -> p n e", e=E)
                    gate.then(v, v.tensor_copy(gate.logit[:], logits))
                    gate.then(v, v.tensor_reduce(gate.total[:], gate.logit[:], AX.X, ALU.max))
                    v.tensor_tensor(gate.away[:], gate.logit[:], gate.total[:].unsqueeze(2).broadcast_to(all_e),
                                    ALU.subtract).then_inc(gate.away_done, 1)

                def shares():
                    v.wait_ge(gate.exped, 1)
                    gate.then(v, v.tensor_reduce(gate.total[:], gate.expd[:], AX.X, ALU.add))
                    gate.then(v, v.reciprocal(gate.rtotal[:], gate.total[:]))
                    gate.then(v, v.tensor_tensor(gate.kept[:], gate.expd[:],
                                                 gate.rtotal[:].unsqueeze(2).broadcast_to(all_e), ALU.mult))

                def largest():
                    for n in range(NB):
                        ins = v.max(gate.top[:, n, :], gate.kept[:, n, :])
                    gate.then(v, ins)
                    for n in range(NB):
                        ins = v.max_index(ids[:, n, :], gate.top[:, n, :], gate.kept[:, n, :])
                    gate.then(v, ins)

                def gate_of_largest():
                    gate.then(v, v.tensor_copy(idf[:], ids[:]))
                    gate.then(v, v.tensor_tensor(gate.total[:], gate.top[:, :, 0], gate.top[:, :, 1], ALU.add))
                    gate.then(v, v.tensor_scalar(gate.total[:], gate.total[:], 2.0 ** -23, None, ALU.add))
                    gate.then(v, v.reciprocal(gate.rtotal[:], gate.total[:]))
                    gate.then(v, v.tensor_tensor(share[:], gate.top[:, :, 0:2],
                                                 gate.rtotal[:].unsqueeze(2).broadcast_to([P, NB, 2]), ALU.mult))
                    v.wait_ge(numbered, 1)
                    numbers = expert_no[:].unsqueeze(1).broadcast_to(all_e)
                    for i, hit in enumerate((gate.kept, pick)):
                        gate.then(v, v.tensor_tensor(hit[:], numbers, idf[:, :, i:i + 1].broadcast_to(all_e),
                                                     ALU.is_equal))
                        gate.then(v, v.tensor_tensor(hit[:], hit[:], share[:, :, i:i + 1].broadcast_to(all_e),
                                                     ALU.mult))
                    v.wait_ge(gate.cleared, 1)
                    v.tensor_tensor(gate.gate[:, :, 0:E], gate.kept[:], pick[:], ALU.add).then_inc(gate.gated, 1)

                def gated_rows(e, b, k):
                    cols = slice(k * GT, k * GT + GT)
                    if k == 0:
                        v.wait_ge(rows_in[b], e * 8 + (16 - 8 * b))
                    v.tensor_tensor(gx[:, k % 2, :], xnT[:, cols], gate_rows[:, b, cols],
                                    ALU.mult).then_inc(gx_done, 1)

                def gated_rest(e, b, k):
                    v.wait_ge(gx_hi_done, (e - 1) * NG + (k + 1))
                    v.tensor_tensor(gx_lo[:, k % 2, :], gx[:, k % 2, :], gx_hi[:, k % 2, :].bitcast(F32),
                                    ALU.subtract).then_inc(gx_lo_done, 1)

                def multiply(e, unit):
                    k, c = unit // KF, unit % KF
                    v.wait_ge(relued, e * UNITS + (unit + 1))
                    v.wait_ge(u_mm, e * UNITS + (unit + 1))
                    if not (first(e) and k < 1):
                        v.wait_ge(in_lo_done, e * UNITS + (unit - KF + 1))
                    v.tensor_tensor(inner[:, c, :], relu[:, c % 2, :], u_ps[:, c % 2, :],
                                    ALU.mult).then_inc(innered, 1)

                def rest_inner(e, unit):
                    c = unit % KF
                    v.wait_ge(in_hi_done, e * UNITS + (unit + 1))
                    if not (first(e) and unit < RING):
                        v.wait_ge(downed, e * UNITS + (unit - RING + 1))
                    v.tensor_tensor(in_lo[:, unit % RING, :], inner[:, c, :],
                                    in_hi[:, unit % RING, :].bitcast(F32), ALU.subtract).then_inc(in_lo_done, 1)

                def take_first(k):
                    cols = slice(k * GT, k * GT + GT)
                    v.wait_ge(rows_in[0], 16)
                    v.wait_ge(downed, (k + 1) * KF)
                    v.tensor_tensor(acc[:, cols], down_ps[:, k, :], gate_rows[:, 0, cols],
                                    ALU.mult).then_inc(first_out, 1)

                def body(e, b):
                    for unit in range(UNITS):
                        k, c = unit // KF, unit % KF
                        multiply(e, unit)
                        if c == 0 and next_rows(e, b, k):
                            gated_rows(*next_rows(e, b, k))
                        if c == 2 and next_rows(e, b, k):
                            gated_rest(*next_rows(e, b, k))
                        if unit:
                            rest_inner(e, unit - 1)
                        elif not first(e):
                            rest_inner(e - 1, UNITS - 1)
                        if first(e) and unit in (1, 2):
                            rest_rows(unit + 1)
                        if first(e) and unit == 2:
                            below_largest()
                        if first(e) and unit == 3:
                            shares()
                        if first(e) and unit == 4:
                            largest()
                        if first(e) and unit == 5:
                            gate_of_largest()
                        if isinstance(e, int) and e == 1 and unit < NG:
                            take_first(unit)
                        if last(e) and unit >= 7 and unit % KF == 3:
                            sum_up(unit // KF - 1)
                        if last(e) and unit >= 9 and unit % KF == 1:
                            add_to_x(unit // KF - 2)

                def sum_up(k):
                    v.wait_ge(downed, (E - 1) * UNITS + (k + 1) * KF)
                    cols = slice(k * GT, k * GT + GT)
                    v.tensor_tensor(acc[:, cols], acc[:, cols], down_ps[:, k, :], ALU.add).then_inc(acc_done, 1)

                def add_to_x(k):
                    v.wait_ge(turned, k + 1)
                    v.tensor_tensor(x[:, GB * k:GB * k + GB, :], x[:, GB * k:GB * k + GB, :],
                                    down_ps[:, k, :].rearrange("p (m d) -> p m d", m=GB),
                                    ALU.add).then_inc(x_done, 1)

                experts(v, body)
                rest_inner(E - 1, UNITS - 1)
                sum_up(NG - 1)
                add_to_x(NG - 2)
                add_to_x(NG - 1)


def layer0_attention(nc, io, keep, stack):
    def sb(name, shape, dt=F32):
        keep[name] = stack.enter_context(nc.sbuf_tensor(name, shape, dt))

    keep["k_dram"] = nc.dram_tensor("k_parts", (NB, K_COPIES, D, T), BF16, kind="Internal").ap()
    keep["q_dram"] = nc.dram_tensor("q_parts", (NB, PARTS, D, T), BF16, kind="Internal").ap()
    sb("kn", [KS, 2, PIECES, T], BF16)
    sb("kh", [P, 2, H, RT, PIECES], BF16)
    sb("qn", [P, 2, PIECES, T], BF16)
    sb("val", [P, 2, H, 32])
    sb("kb", [P, PARTS, TOK], BF16)
    sb("qb", [P, PARTS, TOK], BF16)
    sb("vt", [P, NB, D])
    sb("wo0", [P, D])
    sb("bo_rows", [P, D])
    keep["kqv_out"] = [nc.alloc_semaphore(f"kqv_out{seg}") for seg in range(len(SEGMENTS))]
    for name in ("k_in", "q_in", "val_in"):
        keep[name] = [nc.alloc_semaphore(f"{name}{b}") for b in range(2)]
    with nc.sbuf_tensor("xnT0", [P, TOK], F32) as xnT, nc.sbuf_tensor("ctxT0", [P, TOK], F32) as ctxT:
        keep["xnT"], keep["ctxT"] = xnT, ctxT
        project_layer0(nc, io, keep)
    attend_layer0(nc, io, keep)


def program(nc, io, out):
    with ExitStack() as ctx:
        def sb(n, shape, dt=F32):
            return ctx.enter_context(nc.sbuf_tensor(n, shape, dt))

        keep = {
            "x": sb("x", [P, NB, D]),
            "ident": sb("ident", [P, P]),
            "gate_dram": nc.dram_tensor("gate_rows", (P, GT), F32, kind="Internal").ap(),
            "v_dram": nc.dram_tensor("v_rows", (NB, T, D), F32, kind="Internal").ap(),
        }
        for layer in range(2):
            keep[f"ln_experts{layer}"] = LayerNorm(nc, ctx, f"ln_experts{layer}")
        keep["w_first"] = sb("w_first", [P, 2, FF])
        first_in = [nc.alloc_semaphore(f"w_first_in{layer}") for layer in range(2)]
        keep["w_first_in"], keep["wk_in"] = first_in[0], nc.alloc_semaphore("wk_in")
        with nc.cleanup_on_exit(), ExitStack() as early:
            keep["ln_experts0"].place_xn(nc, early)
            keep["rows0"] = Rows(nc, early, "b", keep["ln_experts0"])
            keep["cut"] = CutWeights(nc, early)
            with ExitStack() as first:
                layer0_attention(nc, io, keep, first)
            experts_layer0(nc, io, keep)
        keep["w_first_in"] = first_in[1]
        with nc.cleanup_on_exit(), ExitStack() as second:
            for name, shape, dt in (
                    ("kT", [P, NC, TOK], F32), ("qT", [P, NC, TOK], F32),
                    ("wv_hi", [P, HD], F32R), ("wv_lo", [P, HD], F32R), ("wo1", [P, NC, D], F32)):
                keep[name] = second.enter_context(nc.sbuf_tensor(name, shape, dt))
            keep["batch1"] = Batch1(nc, second)
            project_layer1(nc, io, keep)
            attend_layer1(nc, io, keep)
        experts_layer1(nc, io, keep, out)


def layouts(a):
    col = lambda v: v.reshape(-1, 1)
    row = lambda v: v.reshape(1, -1)
    by_d = np.arange(D).reshape(PIECES, DH).T.ravel()
    return {
        "x": a["x"],
        "ctxT": a["ctx_1024"].reshape(TOK, D).T,
        "Wq0": a["L0_xattn_Wq"][:, by_d], "Wk0": a["L0_xattn_Wk"][:, by_d], "Wv0": a["L0_xattn_Wv"],
        "Wo0": a["L0_xattn_Wo"][by_d], "bq0": col(a["L0_xattn_bq"][by_d]), "bk0": col(a["L0_xattn_bk"][by_d]),
        "wQ": a["L1_xattn_wQ_w"].T, "wK": a["L1_xattn_wK_w"].T, "wV": a["L1_xattn_wV_w"].T,
        "wO": a["L1_xattn_wOut_w"].T, "bQ": a["L1_xattn_wQ_b"].reshape(NC, P).T,
        "bK": a["L1_xattn_wK_b"].reshape(NC, P).T, "bV": a["L1_xattn_wV_b"].reshape(NC, P).T,
        "bO": row(a["L1_xattn_wOut_b"]), "mask": a["mask_BxSxS2_bf0"],
        "Wr1": a["L1_ffn_Wr"].T, "Wg": a["L1_ffn_Wg"].transpose(0, 2, 1), "Wu": a["L1_ffn_Wu"].transpose(0, 2, 1),
        "Wd": a["L1_ffn_Wd"].transpose(0, 2, 1),
        "Wr0": a["L0_ffn_Wr"], "br0": row(a["L0_ffn_br"]), "W1": a["L0_ffn_W1"], "W2": a["L0_ffn_W2"],
        "b1": a["L0_ffn_b1"].reshape(E, KF, P).transpose(2, 0, 1), "b2": a["L0_ffn_b2"].T,
        "bv0": row(a["L0_xattn_bv"]), "bo0": row(a["L0_xattn_bo"]),
    }


def kernel(**inputs):
    from concourse import bacc
    from concourse.bass_utils import run_bass_kernel_spmd

    nc = bacc.Bacc("TRN2", target_bir_lowering=False, num_devices=1)
    arrays, io = {}, {}
    for name, a in layouts({name: np.asarray(a) for name, a in inputs.items()}).items():
        a = np.ascontiguousarray(a)
        arrays[f"in_{name}_dram"] = a
        io[name] = nc.dram_tensor(f"in_{name}_dram", a.shape, mybir.dt.from_np(a.dtype), kind="ExternalInput").ap()
    out = nc.dram_tensor("out_0_dram", (NB, T, D), F32, kind="ExternalOutput").ap()
    program(nc, io, out)
    r = run_bass_kernel_spmd(nc, [arrays], core_ids=[0])
    return r.results[0]["out_0_dram"]
```
